# Optimizing a Trainium2 kernel written in Bass

```python
import numpy as np
import jax
import jax.numpy as jnp

def _softmax(x, axis=-1):
    return jax.nn.softmax(x, axis=axis)

def _gelu(x):
    return jax.nn.gelu(x, approximate=True)

def _silu(x):
    return jax.nn.silu(x)

def _sigmoid(x):
    return jax.nn.sigmoid(x)

def _layernorm(x, axis=-1, eps=1e-05):
    m = jnp.mean(x, axis=axis, keepdims=True)
    v = jnp.var(x, axis=axis, keepdims=True)
    return (x - m) / jnp.sqrt(v + eps)

def _scatter_add(tgt, idx, src, axis=0):
    return tgt.at[idx].add(src)

def _segment_sum(src, seg, n):
    return jax.ops.segment_sum(src, seg, n)
kernel_name = 'mk_flamingo_gated_d1_seqx_r4_269d28'

def setup_inputs(seed: int=0):
    np.random.seed(seed)
    _w = jnp.asarray

    def _rec_inputs():
        import jax
        import jax.numpy as jnp
        _rk = jax.random.key(seed)
        x = 7.22e-05 + 1 * jax.random.normal(jax.random.fold_in(_rk, 1), (4, 512, 512), jnp.float32)
        _lenS = 512 - jax.random.randint(jax.random.fold_in(_rk, 7), (4,), 0, max(1, 512 // 4) + 1, jnp.int32)
        _lenS2 = 512 - jax.random.randint(jax.random.fold_in(_rk, 8), (4,), 0, max(1, 512 // 4) + 1, jnp.int32)
        _ctx_1024P = jax.random.normal(jax.random.fold_in(_rk, 11), (4, 16, 256), jnp.float32)
        _ctx_1024c = jax.random.dirichlet(jax.random.fold_in(_rk, 511), 0.3 * jnp.ones((16,), jnp.float32), (4, 512))
        _ctx_1024t = jnp.einsum('bsk,bkd->bsd', _ctx_1024c, _ctx_1024P)
        _ctx_1024t = _ctx_1024t * jax.lax.rsqrt(jnp.mean(jnp.square(_ctx_1024t)) + 1e-12) * 0.953939
        ctx_1024 = -0.000673644 + 1.00013 * (_ctx_1024t + 0.3 * jax.random.normal(jax.random.fold_in(_rk, 611), (4, 512, 256), jnp.float32))
        _g = jax.random.normal(jax.random.fold_in(_rk, 9001), (2, 1), jnp.float32)
        _g = jnp.sign(_g) * jnp.maximum(jnp.abs(_g), 1.0) + (_g == 0) * 1.0
        g_xattn = _g[0]
        g_ffn = _g[1]
        return (x, ctx_1024, g_xattn, g_ffn)
    x, ctx_1024, g_xattn, g_ffn = _rec_inputs()

    def _L0_xattn_setup():
        import jax, jax.numpy as jnp
        import numpy as np
        B, S1, S2, DCA = (2, 512, 256, 16)
        QDIM, KDIM, H = (512, 256, 16)
        HD = QDIM // H
        SCALE = HD ** (-0.5)
        EPS = 1e-06
        DCA_WEIGHT = 1.0

        def _ln(t, w, b):
            m = jnp.mean(t, axis=-1, keepdims=True)
            v = jnp.var(t, axis=-1, keepdims=True)
            return (t - m) * jax.lax.rsqrt(v + EPS) * w + b

        def _attn(q, k, v):
            s = jnp.einsum('bhqd,bhkd->bhqk', q, k) * SCALE
            p = jax.nn.softmax(s, axis=-1)
            return jnp.einsum('bhqk,bhkd->bhqd', p, v)
        key = jax.random.key(seed)
        ks = jax.random.split(key, 8)
        w = lambda k, shape: jax.random.normal(k, shape, jnp.float32) * 0.02
        return {'x': jax.random.normal(ks[0], (B, S1, QDIM), jnp.float32), 'y': jax.random.normal(ks[1], (B, S2 + DCA, KDIM), jnp.float32), 'Wq': w(ks[2], (QDIM, QDIM)), 'bq': jnp.zeros((QDIM,), jnp.float32), 'Wk': w(ks[3], (KDIM, QDIM)), 'bk': jnp.zeros((QDIM,), jnp.float32), 'Wv': w(ks[4], (KDIM, QDIM)), 'bv': jnp.zeros((QDIM,), jnp.float32), 'Wkv_dca': w(ks[5], (KDIM, 2 * QDIM)), 'bkv_dca': jnp.zeros((2 * QDIM,), jnp.float32), 'qn_w': jnp.ones((HD,), jnp.float32), 'qn_b': jnp.zeros((HD,), jnp.float32), 'kn_w': jnp.ones((HD,), jnp.float32), 'kn_b': jnp.zeros((HD,), jnp.float32), 'kn_dca_w': jnp.ones((HD,), jnp.float32), 'kn_dca_b': jnp.zeros((HD,), jnp.float32), 'Wo': w(ks[6], (QDIM, QDIM)), 'bo': jnp.zeros((QDIM,), jnp.float32)}
    _L0_xattn_all = _L0_xattn_setup()
    _L0_xattn_in = {k: v for k, v in _L0_xattn_all.items() if k in ('Wq', 'bq', 'Wk', 'bk', 'Wv', 'bv', 'Wkv_dca', 'bkv_dca', 'qn_w', 'qn_b', 'kn_w', 'kn_b', 'kn_dca_w', 'kn_dca_b', 'Wo', 'bo')}
    del _L0_xattn_all

    def _L0_ffn_setup():
        import jax, jax.numpy as jnp
        import numpy as np
        BLOCK_SIZE = 32
        HIDDEN_SIZE = 512
        MLP_DIM = 4096
        NVFP4_LUT = jnp.array([0.0, 0.5, 1.0, 1.5, 2.0, 3.0, 4.0, 6.0, 0.0, -0.5, -1.0, -1.5, -2.0, -3.0, -4.0, -6.0], dtype=jnp.float32)

        def dequant_nvfp4(W_packed, scales, block=BLOCK_SIZE):
            N = W_packed.shape[0]
            low = W_packed & 15
            high = W_packed >> 4 & 15
            idx = jnp.stack([low, high], axis=-1).reshape(N, -1)
            vals = NVFP4_LUT[idx]
            K = vals.shape[1]
            vals = vals.reshape(N, K // block, block) * scales[:, :, None]
            return vals.reshape(N, K)
        key = jax.random.key(seed)
        ks = jax.random.split(key, 7)
        x = jax.random.normal(ks[0], (4, 32, HIDDEN_SIZE), dtype=jnp.float32)
        gate_W_packed = jax.random.randint(ks[1], (MLP_DIM, HIDDEN_SIZE // 2), 0, 64, dtype=jnp.int32)
        gate_scales = jax.random.uniform(ks[2], (MLP_DIM, HIDDEN_SIZE // BLOCK_SIZE), dtype=jnp.float32) * 0.1 + 0.001
        up_W_packed = jax.random.randint(ks[3], (MLP_DIM, HIDDEN_SIZE // 2), 0, 64, dtype=jnp.int32)
        up_scales = jax.random.uniform(ks[4], (MLP_DIM, HIDDEN_SIZE // BLOCK_SIZE), dtype=jnp.float32) * 0.1 + 0.001
        down_W_packed = jax.random.randint(ks[5], (HIDDEN_SIZE, MLP_DIM // 2), 0, 64, dtype=jnp.int32)
        down_scales = jax.random.uniform(ks[6], (HIDDEN_SIZE, MLP_DIM // BLOCK_SIZE), dtype=jnp.float32) * 0.1 + 0.001
        return {'x': x, 'gate_W_packed': gate_W_packed, 'gate_scales': gate_scales, 'up_W_packed': up_W_packed, 'up_scales': up_scales, 'down_W_packed': down_W_packed, 'down_scales': down_scales}
    _L0_ffn_all = _L0_ffn_setup()
    _L0_ffn_in = {k: v for k, v in _L0_ffn_all.items() if k in ('gate_W_packed', 'gate_scales', 'up_W_packed', 'up_scales', 'down_W_packed', 'down_scales')}
    del _L0_ffn_all
    return {'x': x, 'ctx_1024': ctx_1024, 'g_xattn': g_xattn, 'g_ffn': g_ffn, 'L0_xattn_Wq': _L0_xattn_in['Wq'], 'L0_xattn_bq': _L0_xattn_in['bq'], 'L0_xattn_Wk': _L0_xattn_in['Wk'], 'L0_xattn_bk': _L0_xattn_in['bk'], 'L0_xattn_Wv': _L0_xattn_in['Wv'], 'L0_xattn_bv': _L0_xattn_in['bv'], 'L0_xattn_Wkv_dca': _L0_xattn_in['Wkv_dca'], 'L0_xattn_bkv_dca': _L0_xattn_in['bkv_dca'], 'L0_xattn_qn_w': _L0_xattn_in['qn_w'], 'L0_xattn_qn_b': _L0_xattn_in['qn_b'], 'L0_xattn_kn_w': _L0_xattn_in['kn_w'], 'L0_xattn_kn_b': _L0_xattn_in['kn_b'], 'L0_xattn_kn_dca_w': _L0_xattn_in['kn_dca_w'], 'L0_xattn_kn_dca_b': _L0_xattn_in['kn_dca_b'], 'L0_xattn_Wo': _L0_xattn_in['Wo'], 'L0_xattn_bo': _L0_xattn_in['bo'], 'L0_ffn_gate_W_packed': _L0_ffn_in['gate_W_packed'], 'L0_ffn_gate_scales': _L0_ffn_in['gate_scales'], 'L0_ffn_up_W_packed': _L0_ffn_in['up_W_packed'], 'L0_ffn_up_scales': _L0_ffn_in['up_scales'], 'L0_ffn_down_W_packed': _L0_ffn_in['down_W_packed'], 'L0_ffn_down_scales': _L0_ffn_in['down_scales']}

def reference(x, ctx_1024, g_xattn, g_ffn, L0_xattn_Wq, L0_xattn_bq, L0_xattn_Wk, L0_xattn_bk, L0_xattn_Wv, L0_xattn_bv, L0_xattn_Wkv_dca, L0_xattn_bkv_dca, L0_xattn_qn_w, L0_xattn_qn_b, L0_xattn_kn_w, L0_xattn_kn_b, L0_xattn_kn_dca_w, L0_xattn_kn_dca_b, L0_xattn_Wo, L0_xattn_bo, L0_ffn_gate_W_packed, L0_ffn_gate_scales, L0_ffn_up_W_packed, L0_ffn_up_scales, L0_ffn_down_W_packed, L0_ffn_down_scales):
    import jax
    import jax.numpy as jnp

    def _L0_xattn_ref(x, y, Wq, bq, Wk, bk, Wv, bv, Wkv_dca, bkv_dca, qn_w, qn_b, kn_w, kn_b, kn_dca_w, kn_dca_b, Wo, bo):
        import jax, jax.numpy as jnp
        import numpy as np
        B, S1, S2, DCA = (2, 512, 256, 16)
        QDIM, KDIM, H = (512, 256, 16)
        HD = QDIM // H
        SCALE = HD ** (-0.5)
        EPS = 1e-06
        DCA_WEIGHT = 1.0

        def _ln(t, w, b):
            m = jnp.mean(t, axis=-1, keepdims=True)
            v = jnp.var(t, axis=-1, keepdims=True)
            return (t - m) * jax.lax.rsqrt(v + EPS) * w + b

        def _attn(q, k, v):
            s = jnp.einsum('bhqd,bhkd->bhqk', q, k) * SCALE
            p = jax.nn.softmax(s, axis=-1)
            return jnp.einsum('bhqk,bhkd->bhqd', p, v)
        b, s1, _ = x.shape
        y_dca = y[:, -DCA:, :]
        y_main = y[:, :-DCA, :]
        kv_dca = (y_dca @ Wkv_dca + bkv_dca).reshape(b, DCA, 2, H, HD)
        k_dca = _ln(kv_dca[:, :, 0], kn_dca_w, kn_dca_b)
        v_dca = kv_dca[:, :, 1]
        s2 = y_main.shape[1]
        q = _ln((x @ Wq + bq).reshape(b, s1, H, HD), qn_w, qn_b)
        kv = jnp.concatenate([y_main @ Wk + bk, y_main @ Wv + bv], axis=-1)
        kv = kv.reshape(b, s2, H, 2 * HD)
        k = _ln(kv[..., :HD], kn_w, kn_b)
        v = kv[..., HD:]
        qT = q.transpose(0, 2, 1, 3)
        ctx = _attn(qT, k.transpose(0, 2, 1, 3), v.transpose(0, 2, 1, 3))
        ctx = ctx.transpose(0, 2, 1, 3).reshape(b, s1, QDIM)
        ctx_dca = _attn(qT, k_dca.transpose(0, 2, 1, 3), v_dca.transpose(0, 2, 1, 3))
        ctx_dca = ctx_dca.transpose(0, 2, 1, 3).reshape(b, s1, QDIM)
        ctx = ctx + DCA_WEIGHT * ctx_dca
        return ctx @ Wo + bo

    def _L0_ffn_ref(x, gate_W_packed, gate_scales, up_W_packed, up_scales, down_W_packed, down_scales):
        import jax, jax.numpy as jnp
        import numpy as np
        BLOCK_SIZE = 32
        HIDDEN_SIZE = 512
        MLP_DIM = 4096
        NVFP4_LUT = jnp.array([0.0, 0.5, 1.0, 1.5, 2.0, 3.0, 4.0, 6.0, 0.0, -0.5, -1.0, -1.5, -2.0, -3.0, -4.0, -6.0], dtype=jnp.float32)

        def dequant_nvfp4(W_packed, scales, block=BLOCK_SIZE):
            N = W_packed.shape[0]
            low = W_packed & 15
            high = W_packed >> 4 & 15
            idx = jnp.stack([low, high], axis=-1).reshape(N, -1)
            vals = NVFP4_LUT[idx]
            K = vals.shape[1]
            vals = vals.reshape(N, K // block, block) * scales[:, :, None]
            return vals.reshape(N, K)
        B, S, H = x.shape
        xt = x.reshape(B * S, H)
        Wg = dequant_nvfp4(gate_W_packed, gate_scales)
        Wu = dequant_nvfp4(up_W_packed, up_scales)
        Wd = dequant_nvfp4(down_W_packed, down_scales)
        gate = jnp.einsum('th,nh->tn', xt, Wg)
        up = jnp.einsum('th,nh->tn', xt, Wu)
        gelu = jnp.tanh(0.7978845608028654 * (gate + 0.044715 * gate ** 3)) * gate * 0.5 + gate * 0.5
        inter = gelu * up
        out = jnp.einsum('tn,hn->th', inter, Wd)
        return out.reshape(B, S, H)
    x = x + jnp.tanh(g_xattn[0]) * _L0_xattn_ref(_layernorm(x, axis=-1), ctx_1024, L0_xattn_Wq, L0_xattn_bq, L0_xattn_Wk, L0_xattn_bk, L0_xattn_Wv, L0_xattn_bv, L0_xattn_Wkv_dca, L0_xattn_bkv_dca, L0_xattn_qn_w, L0_xattn_qn_b, L0_xattn_kn_w, L0_xattn_kn_b, L0_xattn_kn_dca_w, L0_xattn_kn_dca_b, L0_xattn_Wo, L0_xattn_bo)
    x = x + jnp.tanh(g_ffn[0]) * _L0_ffn_ref(_layernorm(x, axis=-1), L0_ffn_gate_W_packed, L0_ffn_gate_scales, L0_ffn_up_W_packed, L0_ffn_up_scales, L0_ffn_down_W_packed, L0_ffn_down_scales)
    return x

_drawn_inputs = setup_inputs


def setup_inputs(seed=0):
    import zlib

    import numpy as np

    out = dict(_drawn_inputs(seed))
    spreads = {'L0_xattn_bq': (0.0, 0.753),
     'L0_xattn_bk': (0.0, 0.1),
     'L0_xattn_bv': (0.0, 0.1),
     'L0_xattn_bkv_dca': (0.0, 0.1),
     'L0_xattn_qn_w': (1.0, 0.6),
     'L0_xattn_qn_b': (0.0, 0.8),
     'L0_xattn_kn_w': (1.0, 0.6),
     'L0_xattn_kn_b': (0.0, 0.8),
     'L0_xattn_kn_dca_w': (1.0, 0.6),
     'L0_xattn_kn_dca_b': (0.0, 0.8),
     'L0_xattn_bo': (0.0, 0.1)}
    factors = {}
    for name, (base, spread) in spreads.items():
        noise = np.random.default_rng([zlib.crc32(name.encode()), seed]).standard_normal(out[name].shape)
        drawn = base * np.exp(spread * noise) if base else spread * noise
        out[name] = jnp.asarray(drawn.astype(out[name].dtype))
    for name, factor in factors.items():
        out[name] = (out[name] * factor).astype(out[name].dtype)
    return out
```

```python
from contextlib import ExitStack

import concourse.bass as bass
from concourse import mybir

F32 = mybir.dt.float32
F16 = mybir.dt.float16
BF16 = mybir.dt.bfloat16
I32 = mybir.dt.int32
U32 = mybir.dt.uint32
U16 = mybir.dt.uint16
U8 = mybir.dt.uint8
ALU = mybir.AluOpType
ACT = mybir.ActivationFunctionType
AX = mybir.AxisListType

P = 128
B, S, D = 4, 512, 512
H, HD = 16, 32
KD, DCA = 256, 16
SM = S - DCA
F = 4096
TT = S // P
KT = D // P
YT = KD // P
NC = F // P
LASTM = SM - (TT - 1) * P
VW = 3 * HD + 1
QW = 3 * HD
KW = QW + 2
EPS_X, EPS_H = 1e-5, 1e-6
SCALE = HD ** -0.5
WS = 4
R = 2
GU = 2 * 2 * KT * P
WCH = GU + 2 * D
UG, UD = NC, NC // 2
POW2 = 0x7F800000
TINY = 2.0 ** -40
W_UP = 2.0 ** 10
X_UP = 2.0 ** 8
I_UP = 2.0 ** -10
CODE = 2.0 ** 14

TP_X, TP_Y = 0, TT
TP_Q = TP_Y + TT
TP_K = TP_Q + H
TP_M = TP_K + H
TP_C = TP_M + H
TP_L = TP_C + TT
TP_N = TP_L + 2 * TT
SA_Q = 0
SA_KV = SA_Q + TT
SA_A = SA_KV + 2 * TT
SA_O = SA_A + TT * H
SA_U = SA_O + TT
SA_N = SA_U + NC
SB_B = 0
SB_G = TT * H
SB_N = SB_G + NC


def block_kernel(nc, x, ctx, g_xattn, g_ffn, Wq, bq, Wk, bk, Wv, bv, Wkv_dca, bkv_dca, qn_w, qn_b,
                 kn_w, kn_b, knd_w, knd_b, Wo, bo, gW, gS, uW, uS, dW, dS, out):
    wscratch = nc.dram_tensor("wscratch", [NC, P, WCH], F16, kind="Internal").ap()
    with ExitStack() as stack:
        def sb(name, shape, dt):
            return stack.enter_context(nc.sbuf_tensor(name, shape, dt))

        def psum(name, shape, dt):
            return stack.enter_context(nc.psum_tensor(name, shape, dt))

        def sem(name):
            return stack.enter_context(nc.semaphore(name))

        ident = sb("ident", [P, P], F32)
        ident16 = sb("ident16", [P, P], F16)
        identb = sb("identb", [P, P], BF16)
        wq = sb("wq", [P, KT, D], F32)
        wkv = sb("wkv", [P, YT, 2 * D], F32)
        wdca = sb("wdca", [P, YT, 2 * D], F32)
        wo = sb("wo", [P, KT, D], F32)
        bq_b = sb("bq_b", [P, D], F32)
        bkv_b = sb("bkv_b", [P, 2, 2 * D], F32)
        bo_b = sb("bo_b", [P, D], F32)
        qwb = sb("qwb", [P, 2, HD], F32)
        kwb = sb("kwb", [P, 2, 2, HD], F32)
        kall = sb("kall", [P, 4, HD], F32)
        gates = sb("gates", [P, 2], F32)
        tgates = sb("tgates", [P, 2], F32)
        kmask = sb("kmask", [P, 2, 2], F32)
        mhalf = sb("mhalf", [P, TT * H], F32)
        qk_p2 = sb("qk_p2", [P, 4], F32)
        exp_scale = sb("exp_scale", [P, 1], F32)
        dg = sb("dg", [P, NC], F32)
        mu = sb("mu", [P, NC], F32)
        out_scale = sb("out_scale", [P, 1], F32)
        sgu = sb("sgu", [P, 2, NC, 16], F32)
        sd = sb("sd", [P, TT, P], F32)
        pgu = sb("pgu", [P, 2, NC], F32)
        igu = sb("igu", [P, 2, NC], F32)
        mprod = sb("mprod", [P, NC], F32)
        stat = sb("stat", [P, 8], F32)
        sst = sb("sst", [P, R, 4, P], F32)
        x_sb = sb("x_sb", [P, TT, D], F32)
        xn = sb("xn", [P, TT, D], F32)
        bst = sb("bst", [P, TT, 6], F32)
        mv = sb("mv", [P, TT, 2], F32)
        rstd = sb("rstd", [P, TT], F32)
        y_sb = sb("y_sb", [P, TT, KD], F32)
        yT = sb("yT", [P, YT, S], F32)
        yTd = sb("yTd", [P, YT, P], F32)
        xnT = sb("xnT", [P, KT, S], F32)
        t0 = sb("t0", [P, 2 * D], F32)
        t1 = sb("t1", [P, D], F32)
        t2 = sb("t2", [P, D], F32)
        hsum = sb("hsum", [P, H], F32)
        hrs = sb("hrs", [P, 2, TT, H], F32)
        cat = sb("cat", [P, TT, H, KW], F16)
        qkT = sb("qkT", [P, 2, H, S], F16)
        vv = sb("vv", [P, TT, H, VW], BF16)
        vd = sb("vd", [P, H, VW], BF16)
        pmx = sb("pmx", [P, TT, S // DCA], F32)
        mneg = sb("mneg", [P, R, TT, 2], F16)
        pf = sb("pf", [P, R, S], F32)
        phl = sb("phl", [P, R, 2, TT, S], F16)
        osum = sb("osum", [P, 2, TT, HD], F32)
        orec = sb("orec", [P, 2, TT], F32)
        gl = sb("gl", [P, R, S], F32)
        it = sb("it", [P, R, S], F32)
        ihl = sb("ihl", [P, R, 2, S], F16)
        xhl = sb("xhl", [P, R, 2, D], F16)
        ost = sb("ost", [P, R, D], F32)

        qT, kT = qkT[:, 0, :, :], qkT[:, 1, :, :]
        wst = qkT[:, :, :, :].rearrange("p a h t -> p (a h t)")[:, 0:WS * WCH].rearrange("p (s n) -> p s n", s=WS)
        xT = xnT[:, :, :].rearrange("p k t -> p (k t)").bitcast(F16).rearrange("p (l k t) -> p l k t", l=2, k=KT)
        cen = phl[:, :, :, :, :].rearrange("p r l k t -> p (r l k t)").bitcast(F32).rearrange(
            "p (a t d) -> p a t d", a=2, t=TT)
        codes = phl[:, 0, :, :, :].rearrange("p l k t -> p (l k t)").bitcast(I32).rearrange(
            "p (s k c) -> p s k c", s=4, k=4)
        codesb = phl[:, 1, 0, 0:2, :].bitcast(BF16)
        codes16 = phl[:, 1, 0, 2, :].bitcast(U16)
        nib = phl[:, 1, 1, 0:2, :].bitcast(U16)
        nibs = phl[:, 1, 1, 2:4, :].bitcast(U16)
        ssb = pf
        wf = xn[:, :, :].rearrange("p a b -> p (a b)").rearrange("p (s n) -> p s n", s=R)
        whl = xnT[:, :, :].rearrange("p k t -> p (k t)").bitcast(F16).rearrange("p (s n) -> p s n", s=R)

        ringA = psum("ringA", [P, R, 512], F32)
        ringB = psum("ringB", [P, R, 512], F32)
        ringO = psum("ringO", [P, R, 512], F32)
        ringT = psum("ringT", [P, R, 512], F32)
        ringT16 = ringT[:, :, :].bitcast(F16)
        ringOb = ringO[:, :, :].bitcast(BF16)

        s_init = sem("s_init")
        s_par = sem("s_par")
        s_scales = sem("s_scales")
        s_stat = sem("s_stat")
        s_allmax = sem("s_allmax")
        s_norm = sem("s_norm")
        s_tanh = sem("s_tanh")
        s_code = [sem(f"s_code{i}") for i in range(4)]
        s_cb = sem("s_cb")
        s_sst = sem("s_sst")
        s_ct = sem("s_ct")
        s_c16 = sem("s_c16")
        s_ss = sem("s_ss")
        s_wf = sem("s_wf")
        s_whi = sem("s_whi")
        s_wlo = sem("s_wlo")
        s_wst = [sem(f"s_wst{i}") for i in range(R)]
        s_x = sem("s_x")
        s_y = sem("s_y")
        s_var = sem("s_var")
        s_rstd = sem("s_rstd")
        s_xn = sem("s_xn")
        tp_full, tp_free = sem("tp_full"), sem("tp_free")
        sa_full, sa_free = sem("sa_full"), sem("sa_free")
        sb_full, sb_free = sem("sb_full"), sem("sb_free")
        s_hn = sem("s_hn")
        s_cat = sem("s_cat")
        s_v = sem("s_v")
        s_mneg = sem("s_mneg")
        s_ph = sem("s_ph")
        s_pl = sem("s_pl")
        s_pv = sem("s_pv")
        s_of = sem("s_of")
        s_ctx = sem("s_ctx")
        s_l2 = sem("s_l2")
        s_load = [sem(f"s_load{i}") for i in range(WS)]
        s_wused = sem("s_wused")
        s_ih = sem("s_ih")
        s_il = sem("s_il")
        s_dn = sem("s_dn")
        s_ost = sem("s_ost")
        s_out = [sem(f"s_out{i}") for i in range(R)]

        def acc(tt):
            return ringO[:, tt, :] if tt < R else ringT[:, tt - R, :]

        params = [
            (wq[:, :, :], Wq.rearrange("(k p) n -> p k n", p=P)),
            (wkv[:, :, 0:D], Wk.rearrange("(k p) n -> p k n", p=P)),
            (wkv[:, :, D:2 * D], Wv.rearrange("(k p) n -> p k n", p=P)),
            (wdca[:, :, :], Wkv_dca.rearrange("(k p) n -> p k n", p=P)),
            (wo[:, :, :], Wo.rearrange("(k p) n -> p k n", p=P)),
            (bq_b[:, :], bq.partition_broadcast(P)),
            (bo_b[:, :], bo.partition_broadcast(P)),
            (bkv_b[:, 0, 0:D], bk.partition_broadcast(P)),
            (bkv_b[:, 0, D:2 * D], bv.partition_broadcast(P)),
            (bkv_b[0:LASTM, 1, 0:D], bk.partition_broadcast(LASTM)),
            (bkv_b[0:LASTM, 1, D:2 * D], bv.partition_broadcast(LASTM)),
            (bkv_b[LASTM:P, 1, :].rearrange("p (h a d) -> p a h d", h=H, a=2)[:, 0],
             bkv_dca[0:D].rearrange("(h d) -> h d", h=H).partition_broadcast(DCA)),
            (bkv_b[LASTM:P, 1, :].rearrange("p (h a d) -> p a h d", h=H, a=2)[:, 1],
             bkv_dca[D:2 * D].rearrange("(h d) -> h d", h=H).partition_broadcast(DCA)),
            (qwb[:, 0, :], qn_w.partition_broadcast(P)),
            (qwb[:, 1, :], qn_b.partition_broadcast(P)),
            (kwb[:, 0, 0, :], kn_w.partition_broadcast(P)),
            (kwb[:, 0, 1, :], kn_b.partition_broadcast(P)),
            (kwb[0:LASTM, 1, 0, :], kn_w.partition_broadcast(LASTM)),
            (kwb[0:LASTM, 1, 1, :], kn_b.partition_broadcast(LASTM)),
            (kwb[LASTM:P, 1, 0, :], knd_w.partition_broadcast(DCA)),
            (kwb[LASTM:P, 1, 1, :], knd_b.partition_broadcast(DCA)),
            (kall[:, 0, :], kn_w.partition_broadcast(P)),
            (kall[:, 1, :], kn_b.partition_broadcast(P)),
            (kall[:, 2, :], knd_w.partition_broadcast(P)),
            (kall[:, 3, :], knd_b.partition_broadcast(P)),
            (gates[:, 0:1], g_xattn.partition_broadcast(P)),
            (gates[:, 1:2], g_ffn.partition_broadcast(P)),
        ]
        NPAR = 16 * len(params)

        block = stack.enter_context(nc.Block())

        @block.sync
        def _(sp):
            for n in range(R):
                sp.sem_inc(s_wst[n], 16)
                sp.sem_inc(s_out[n], 16)
            for m, sc in enumerate((gS, uS)):
                sp.dma_start(sgu[:, m, :, :].rearrange("p (j r) k -> p j (r k)", r=2),
                             sc.rearrange("(j p r) k -> p j (r k)", p=P, r=2)).then_inc(s_scales, 16)
            sp.dma_start(sd[:, :, :], dS.rearrange("(t p) k -> p t k", p=P)).then_inc(s_scales, 16)

            gWv = gW.rearrange("(j p r) k -> j r p k", p=P, r=2)
            uWv = uW.rearrange("(j p r) k -> j r p k", p=P, r=2)
            dWv = dW.rearrange("(t p) (j c) -> j p t c", p=P, j=UD)

            def codes_gu(j, r, slot):
                sp.dma_start(codes[:, slot, 0:2, :].rearrange("p k c -> p (k c)"), gWv[j, r]).then_inc(s_code[slot], 16)
                sp.dma_start(codes[:, slot, 2:4, :].rearrange("p k c -> p (k c)"), uWv[j, r]).then_inc(s_code[slot], 16)

            def codes_d(j, slot):
                sp.dma_start(codes[:, slot, 0:2, :], dWv[j][:, 0:2]).then_inc(s_code[slot], 16)
                sp.dma_start(codes[:, slot, 2:4, :], dWv[j][:, 2:4]).then_inc(s_code[slot], 16)

            for n in range(4):
                codes_gu(n // 2, n % 2, n)
            for dst, src in params:
                sp.dma_start(dst, src).then_inc(s_par, 16)
            sp.dma_start(x_sb[:, :, :], x[0].rearrange("(t p) d -> p t d", p=P)).then_inc(s_x, 16)
            sp.dma_start(y_sb[:, :, :], ctx[0].rearrange("(t p) d -> p t d", p=P)).then_inc(s_y, 16)

            def store_gu(c, u, n):
                sp.wait_ge(s_wlo, u + (1 + R))
                sp.dma_start(wscratch[c][:, 0:GU], whl[:, n % R, :]).then_inc(s_wst[n % R], 16)

            with sp.Fori(0, UG // 4 - 1) as q:
                for n in range(4):
                    sp.wait_ge(s_cb, 4 * q + (n + 1))
                    codes_gu(2 * q + (2 + n // 2), n % 2, n)
                    store_gu(4 * q + n, 4 * q + n, n)
            for n in range(4):
                sp.wait_ge(s_cb, UG - 4 + n + 1)
                codes_d(n, n)
                store_gu(UG - 4 + n, UG - 4 + n, n)

            def store_d(j, u, n):
                sp.wait_ge(s_wlo, u + (1 + R))
                for r in range(2):
                    sp.dma_start(wscratch[2 * j + r][:, GU:WCH], whl[:, n % R, r * 2 * D:(r + 1) * 2 * D]).then_inc(
                        s_wst[n % R], 16)

            with sp.Fori(0, UD // 4 - 1) as q:
                for n in range(4):
                    sp.wait_ge(s_cb, 4 * q + (UG + n + 1))
                    codes_d(4 * q + (4 + n), n)
                    store_d(4 * q + n, 4 * q + (UG + n), n)
            for n in range(4):
                store_d(UD - 4 + n, UG + UD - 4 + n, n)
            for n in range(R):
                sp.wait_ge(s_wst[n], 16 + 16 * UG // R + 32 * UD // R)

            def batch(b, last):
                heads = sp.snap(b * H + (H + R)) if not last else B * H + R
                with sp.Fori(0, NC // WS) as q:
                    for n in range(WS):
                        sp.wait_ge(s_wused, b * NC + q * WS + (n + 1))
                        sp.wait_ge(s_pv, heads)
                        sp.dma_start(wst[:, n, :], wscratch[q * WS + n]).then_inc(s_load[n], 16)
                for tt in range(TT):
                    sp.wait_ge(s_ost, b * TT + (tt + 2))
                    sp.dma_start(out[b, tt * P:(tt + 1) * P, :], ost[:, tt % R, :]).then_inc(s_out[tt % R], 16)
                if not last:
                    sp.dma_start(x_sb[:, :, :], x[b + 1].rearrange("(t p) d -> p t d", p=P)).then_inc(s_x, 16)
                    sp.dma_start(y_sb[:, :, :], ctx[b + 1].rearrange("(t p) d -> p t d", p=P)).then_inc(s_y, 16)

            with sp.Fori(0, B - 1) as b:
                batch(b, False)
            batch(B - 1, True)
            for n in range(R):
                sp.wait_ge(s_out[n], 16 + 16 * B * TT // R)

        @block.gpsimd
        def _(pool):
            for m in (ident, ident16, identb):
                pool.memset(m[:, :], 0.0)
            pool.memset(mhalf[:, :], -0.5)
            pool.memset(kmask[:, :, :], 0.0)
            pool.memset(yTd[:, :, :], 0.0)
            pool.memset(yT[:, :, SM:S], 0.0)
            pool.drain()
            for m in (ident, ident16, identb):
                pool.affine_select(out=m[:, :], in_=m[:, :], compare_op=ALU.not_equal, fill=1.0,
                                   base=0, pattern=[[-1, P]], channel_multiplier=1)
            pool.memset(kmask[:, 0, 0:1], 1.0)
            pool.affine_select(out=kmask[:, 1, 0:1], in_=kmask[:, 1, 0:1], compare_op=ALU.is_ge, fill=1.0,
                               base=-LASTM, pattern=[[0, 1]], channel_multiplier=1)
            pool.affine_select(out=kmask[:, 1, 1:2], in_=kmask[:, 1, 1:2], compare_op=ALU.is_gt, fill=1.0,
                               base=LASTM, pattern=[[0, 1]], channel_multiplier=-1)
            pool.drain()
            pool.memset(stat[:, 6:8], 0.0).then_inc(s_init, 1)
            pool.sem_inc(s_wlo, R)
            pool.sem_inc(s_pl, R)
            pool.sem_inc(s_il, R)
            pool.wait_ge(s_stat, 1)
            pool.partition_all_reduce(stat[:, 2:4], stat[:, 0:2], P, bass.bass_isa.ReduceOp.max).then_inc(s_allmax, 1)
            pool.wait_ge(s_norm, 1)

            def stage_gu(c, u, n):
                pool.wait_ge(s_ct, u + 1)
                pool.tensor_copy(sst[:, n % R, :, :].rearrange("p (m a) (e s) -> p m (a e) s", m=2, s=16),
                                 sgu[:, :, bass.ds(c, 1), :].rearrange("p m c e -> p m (c e)").unsqueeze(3).broadcast_to(
                                     [P, 2, 16, 16])).then_inc(s_sst, 1)

            def stage_d(j, u, n):
                pool.wait_ge(s_ct, u + 1)
                pool.tensor_copy(sst[:, n % R, :, :].rearrange("p k (e s) -> p k e s", s=16),
                                 sd[:, :, bass.ds(j * 8, 8)].unsqueeze(3).broadcast_to([P, 4, 8, 16])).then_inc(s_sst, 1)

            def low_gu(u, n):
                pool.wait_ge(s_whi, u + 1)
                pool.tensor_tensor(whl[:, n % R, 1024:2048], wf[:, n % R, :], whl[:, n % R, 0:1024],
                                   ALU.subtract).then_inc(s_wlo, 1)

            def low_d(u, n):
                pool.wait_ge(s_whi, u + 1)
                w = whl[:, n % R, :].rearrange("p (r l k c) -> p r l k c", r=2, l=2, k=4)
                f = wf[:, n % R, :].rearrange("p (k r c) -> p r k c", k=4, r=2)
                for r in range(2):
                    i = pool.tensor_tensor(w[:, r, 1], f[:, r], w[:, r, 0], ALU.subtract)
                i.then_inc(s_wlo, 1)

            stage_gu(0, 0, 0)
            with pool.Fori(0, (UG - 2) // 2) as q:
                for n in range(2):
                    stage_gu(2 * q + (n + 1), 2 * q + (n + 1), n + 1)
                    low_gu(2 * q + n, n)
            stage_gu(UG - 1, UG - 1, 1)
            low_gu(UG - 2, 0)
            stage_d(0, UG, 0)
            low_gu(UG - 1, 1)
            with pool.Fori(0, (UD - 2) // 2) as q:
                for n in range(2):
                    stage_d(2 * q + (n + 1), 2 * q + (UG + n + 1), n + 1)
                    low_d(2 * q + (UG + n), n)
            stage_d(UD - 1, UG + UD - 1, 1)
            low_d(UG + UD - 2, 0)
            low_d(UG + UD - 1, 1)

            def inverse_root(v, n, count):
                pool.wait_ge(s_var, count)
                pool.tensor_tensor(v, v, mhalf[:, 0:n], ALU.pow).then_inc(s_rstd, 1)

            with pool.Fori(0, B) as b:
                inverse_root(rstd[:, :], TT, b * 4 + 1)
                for a in range(2):
                    inverse_root(hrs[:, a, :, :].rearrange("p t h -> p (t h)"), TT * H, b * 4 + (2 + a))
                with pool.Fori(0, H // 2) as q:
                    for n in range(2):
                        for k in range(TT):
                            pool.wait_ge(s_ph, b * (H * TT) + q * (2 * TT) + (n * TT + k + 1))
                            pool.tensor_tensor(phl[:, n, 1, k, :], pf[:, k % R, :], phl[:, n, 0, k, :],
                                               ALU.subtract).then_inc(s_pl, 1)
                inverse_root(rstd[:, :], TT, b * 4 + 4)
                with pool.Fori(0, NC // 2) as q:
                    for n in range(2):
                        pool.wait_ge(s_ih, b * NC + 2 * q + (n + 1))
                        pool.tensor_tensor(ihl[:, n, 1, :], it[:, n, :], ihl[:, n, 0, :], ALU.subtract).then_inc(s_il, 1)

        @block.scalar
        def _(act):
            act.sem_inc(tp_free, R)
            act.sem_inc(sb_free, R)
            act.sem_inc(s_ss, R)

            def cast_codes(q, n):
                act.wait_ge(s_code[n], q * 32 + 32)
                act.wait_ge(s_ct, q * 4 + (n + 1))
                act.activation(codesb[:, n % R, :],
                               codes[:, n, :, :].rearrange("p k c -> p (k c)").bitcast(U8)[:, 0:4 * 512:4],
                               ACT.Copy).then_inc(s_cb, 1)

            def scales_out(u, n):
                act.wait_ge(s_ct, u + (1 + R))
                act.wait_ge(s_wf, u + 1)
                act.activation(ssb[:, n % R, :], ringT[:, n % R, :], ACT.Copy).then_inc(s_ss, 1)

            def high_gu(u, stores, n):
                act.wait_ge(s_wf, u + (1 + R))
                act.wait_ge(s_wst[n % R], stores)
                act.activation(whl[:, n % R, 0:1024], wf[:, n % R, :], ACT.Copy).then_inc(s_whi, 1)

            def high_d(u, stores, n):
                act.wait_ge(s_wf, u + (1 + R))
                act.wait_ge(s_wst[n % R], stores)
                w = whl[:, n % R, :].rearrange("p (r l k c) -> p r l k c", r=2, l=2, k=4)
                f = wf[:, n % R, :].rearrange("p (k r c) -> p r k c", k=4, r=2)
                for r in range(2):
                    i = act.activation(w[:, r, 0], f[:, r], ACT.Copy)
                i.then_inc(s_whi, 1)

            cast_codes(0, 0)
            cast_codes(0, 1)
            scales_out(0, 0)
            with act.Fori(0, UG // 4) as q:
                for n in range(4):
                    cast_codes(q + (n + 2) // 4, (n + 2) % 4)
                    scales_out(q * 4 + (n + 1), n + 1)
                    high_gu(q * 4 + n, q * 32 + (16 + 16 * (n // R)), n)
            done = 16 + 16 * UG // R
            with act.Fori(0, UD // 4 - 1) as q:
                for n in range(4):
                    cast_codes(q + (UG // 4 + (n + 2) // 4), (n + 2) % 4)
                    scales_out(q * 4 + (UG + n + 1), n + 1)
                    high_d(q * 4 + (UG + n), q * 64 + (done + 32 * (n // R)), n)
            for n in range(4):
                if n < 2:
                    cast_codes((UG + UD) // 4 - 1, n + 2)
                if n < 3:
                    scales_out(UG + UD - 4 + n + 1, n + 1)
                high_d(UG + UD - 4 + n, (UD // 4 - 1) * 64 + done + 32 * (n // R), n)

            for n in range(R):
                act.wait_ge(s_wst[n], 16 + 16 * UG // R + 32 * UD // R)
            act.wait_ge(s_par, NPAR)
            act.activation(tgates[:, :], gates[:, :], ACT.Tanh).then_inc(s_tanh, 1)

            with act.Fori(0, B) as b:
                def tp_wait(i):
                    act.wait_ge(tp_full, b * TP_N + (i + 1))

                for tt in range(TT):
                    tp_wait(TP_X + tt)
                    act.activation(xnT[:, :, tt * P:(tt + 1) * P],
                                   ringT[:, tt % R, :].rearrange("p (k t) -> p k t", k=KT), ACT.Copy).then_inc(tp_free, 1)
                for tt in range(TT):
                    tp_wait(TP_Y + tt)
                    src = ringT[:, tt % R, 0:YT * P].rearrange("p (k t) -> p k t", k=YT)
                    if tt < TT - 1:
                        i = act.activation(yT[:, :, tt * P:(tt + 1) * P], src, ACT.Copy)
                    else:
                        act.activation(yT[:, :, tt * P:SM], src[:, :, 0:LASTM], ACT.Copy)
                        i = act.activation(yTd[:, :, LASTM:P], src[:, :, LASTM:P], ACT.Copy)
                    i.then_inc(tp_free, 1)
                for a, (tp, dup, rows) in enumerate(((TP_Q, 1, QW), (TP_K, 2, KW))):
                    for tt in range(TT):
                        act.wait_ge(s_hn, b * (2 * TT) + (a * TT + tt + 1))
                        act.activation(cat[:, tt, :, dup * HD:(dup + 1) * HD], cat[:, tt, :, 0:HD],
                                       ACT.Copy).then_inc(s_cat, 1)
                    with act.Fori(0, H // R) as q:
                        for n in range(R):
                            act.wait_ge(tp_full, b * TP_N + R * q + (tp + n + 1))
                            act.activation(qkT[0:rows, a, bass.ds(R * q + n, 1), :].rearrange("p a t -> p (a t)"),
                                           ringT16[0:rows, n, 0:S], ACT.Copy).then_inc(tp_free, 1)

                def maxima(h, n):
                    act.wait_ge(tp_full, b * TP_N + h + (TP_M + 1))
                    act.activation(qT[QW:KW, bass.ds(h, 1), :].rearrange("p a t -> p (a t)"),
                                   ringT16[QW:KW, n, 0:S], ACT.Copy).then_inc(tp_free, 1)

                def exps(h):
                    for k in range(TT):
                        act.wait_ge(sb_full, b * SB_N + h * TT + (k + 1))
                        act.wait_ge(s_pl, b * (H * TT) + h * TT + (k + 1))
                        act.activation(pf[:, k % R, :], ringB[:, k % R, :], ACT.Exp,
                                       scale=exp_scale[:, 0:1]).then_inc(sb_free, 1)

                maxima(0, 0)
                exps(0)
                maxima(1, 1)
                with act.Fori(0, (H - 2) // 2) as q:
                    for n in range(2):
                        exps(2 * q + (n + 1))
                        maxima(2 * q + (n + 2), n)
                exps(H - 1)
                for tt in range(TT):
                    tp_wait(TP_C + tt)
                    act.activation(xnT[:, :, tt * P:(tt + 1) * P],
                                   ringT[:, tt % R, :].rearrange("p (k t) -> p k t", k=KT), ACT.Copy).then_inc(tp_free, 1)
                for tt in range(TT):
                    for l in range(2):
                        tp_wait(TP_L + 2 * tt + l)
                        act.activation(xT[:, l, :, tt * P:(tt + 1) * P],
                                       ringT16[:, l, 0:512].rearrange("p (k t) -> p k t", k=KT), ACT.Copy).then_inc(tp_free, 1)
                with act.Fori(0, NC // 2) as q:
                    for n in range(2):
                        act.wait_ge(sb_full, b * SB_N + q * 2 + (SB_G + n + 1))
                        act.wait_ge(sa_free, b * SA_N + q * 2 + (SA_U + n + 1))
                        act.activation(gl[:, n, :], ringB[:, n, :], ACT.Gelu_apprx_tanh,
                                       scale=dg[:, bass.ds(q * 2 + n, 1)]).then_inc(sb_free, 1)
                        act.wait_ge(sa_free, b * SA_N + q * 2 + (SA_U + n + 1 + R))
                        act.wait_ge(s_wused, b * NC + q * 2 + (n + 1 + WS - R))
                        act.activation(ihl[:, n, 0, :], it[:, n, :], ACT.Copy).then_inc(s_ih, 1)

        @block.tensor
        def _(pe):
            pe.sem_inc(s_ct, R)
            pe.sem_inc(s_pv, R)
            pe.sem_inc(s_wused, WS)
            pe.wait_ge(s_init, 1)

            def turn(u, n):
                pe.wait_ge(s_cb, u + 1)
                pe.wait_ge(s_c16, u + 1)
                for k in range(4):
                    pe.transpose(ringOb[:, n, k * P:(k + 1) * P], codesb[:, n, k * P:(k + 1) * P], identb[:, :])
                pe.wait_ge(s_sst, u + 1)
                pe.wait_ge(s_ss, u + 1)
                for k in range(4):
                    i = pe.transpose(ringT[:, n, k * P:(k + 1) * P],
                                     sst[:, n, k, :], ident[:, :])
                i.then_inc(s_ct, 1)

            with pe.Fori(0, (UG + UD) // 2) as q:
                for n in range(2):
                    turn(2 * q + n, n)
            pe.wait_ge(s_c16, UG + UD + R)
            pe.wait_ge(s_ss, UG + UD + R)
            pe.wait_ge(s_par, NPAR)

            def batch(b):
                def tp_wait(i):
                    pe.wait_ge(tp_free, b * TP_N + (i + 1))

                def sa_wait(i):
                    pe.wait_ge(sa_free, b * SA_N + (i + 1))

                pe.wait_ge(s_ost, b * TT + 1)
                for tt in range(TT):
                    tp_wait(TP_X + tt)
                    pe.wait_ge(s_xn, b * TT + (tt + 1))
                    for k in range(KT):
                        i = pe.transpose(ringT[:, tt % R, k * P:(k + 1) * P], xn[:, tt, k * P:(k + 1) * P], ident[:, :])
                    i.then_inc(tp_full, 1)
                pe.wait_ge(s_y, b * 16 + 16)
                for tt in range(TT):
                    tp_wait(TP_Y + tt)
                    for k in range(YT):
                        i = pe.transpose(ringT[:, tt % R, k * P:(k + 1) * P], y_sb[:, tt, k * P:(k + 1) * P], ident[:, :])
                    i.then_inc(tp_full, 1)
                for tt in range(TT):
                    sa_wait(SA_Q + tt)
                    tp_wait(TP_X + tt + R)
                    for k in range(KT):
                        i = pe.matmul(ringA[:, tt % R, :], xnT[:, k, tt * P:(tt + 1) * P], wq[:, k, :],
                                      start=(k == 0), stop=(k == KT - 1))
                    i.then_inc(sa_full, 1)
                for tt in range(TT):
                    tp_wait(TP_Y + tt + R)
                    for e in range(2):
                        sa_wait(SA_KV + 2 * tt + e)
                        last = tt == TT - 1
                        for k in range(YT):
                            i = pe.matmul(ringA[:, e, :], yT[:, k, tt * P:(tt + 1) * P], wkv[:, k, e * D:(e + 1) * D],
                                          start=(k == 0), stop=(k == YT - 1 and not last))
                        if last:
                            for k in range(YT):
                                w = wdca[:, k, :].rearrange("p (a h d) -> p h a d", a=2, h=H)
                                i = pe.matmul(ringA[:, e, :], yTd[:, k, :], w[:, e * (H // 2):(e + 1) * (H // 2)],
                                              start=False, stop=(k == YT - 1))
                        i.then_inc(sa_full, 1)
                for a, (tp, rows) in enumerate(((TP_Q, QW), (TP_K, KW))):
                    with pe.Fori(0, H // R) as q:
                        for n in range(R):
                            pe.wait_ge(s_cat, b * (2 * TT) + (a + 1) * TT)
                            pe.wait_ge(tp_free, b * TP_N + R * q + (tp + n + 1))
                            for tt in range(TT):
                                i = pe.transpose(ringT16[0:rows, n, tt * P:(tt + 1) * P],
                                                 cat[:, tt, bass.ds(R * q + n, 1), 0:rows].rearrange("p a w -> p (a w)"),
                                                 ident16[:, :])
                            i.then_inc(tp_full, 1)

                def scores_max(h):
                    for tt in range(TT):
                        pe.wait_ge(sa_free, b * SA_N + h * TT + (SA_A + tt + 1))
                        pe.matmul(ringA[:, tt % R, :], qT[0:QW, bass.ds(h, 1), tt * P:(tt + 1) * P].rearrange("p a t -> p (a t)"),
                                  kT[0:QW, bass.ds(h, 1), :].rearrange("p a t -> p (a t)"),
                                  start=True, stop=True).then_inc(sa_full, 1)

                def turn_max(h, n):
                    pe.wait_ge(s_mneg, b * H + h + 1)
                    pe.wait_ge(tp_free, b * TP_N + h + (TP_M + 1))
                    for tt in range(TT):
                        i = pe.transpose(ringT16[QW:KW, n, tt * P:(tt + 1) * P], mneg[:, n, tt, :], ident16[:, :])
                    i.then_inc(tp_full, 1)

                def scores(h):
                    pe.wait_ge(tp_free, b * TP_N + h + (TP_M + 1 + R))
                    for k in range(TT):
                        pe.wait_ge(sb_free, b * SB_N + h * TT + (k + 1))
                        pe.matmul(ringB[:, k % R, :], kT[0:KW, bass.ds(h, 1), k * P:(k + 1) * P].rearrange("p a t -> p (a t)"),
                                  qT[0:KW, bass.ds(h, 1), :].rearrange("p a t -> p (a t)"),
                                  start=True, stop=True).then_inc(sb_full, 1)

                def weigh(h, n):
                    pe.wait_ge(s_pl, b * (H * TT) + h * TT + (TT + R))
                    pe.wait_ge(s_of, b * H + h + 1)
                    for tt in range(TT):
                        for k in range(TT):
                            for l in range(2):
                                pe.matmul(ringO[:, 0, tt * VW:(tt + 1) * VW], phl[:, n, l, k, tt * P:(tt + 1) * P],
                                          vv[:, k, bass.ds(h, 1), :].rearrange("p a w -> p (a w)"),
                                          start=(k == 0 and l == 0), stop=(k == TT - 1 and l == 1))
                        for l in range(2):
                            i = pe.matmul(ringO[:, 1, tt * VW:(tt + 1) * VW], phl[:, n, l, TT - 1, tt * P:(tt + 1) * P],
                                          vd[:, bass.ds(h, 1), :].rearrange("p a w -> p (a w)"),
                                          start=(l == 0), stop=(l == 1))
                    i.then_inc(s_pv, 1)

                pe.wait_ge(tp_free, b * TP_N + (TP_M + R))
                pe.wait_ge(s_v, b + 1)
                scores_max(0)
                turn_max(0, 0)
                scores_max(1)
                scores(0)
                turn_max(1, 1)
                with pe.Fori(0, (H - 2) // 2) as q:
                    for n in range(2):
                        h = 2 * q + (n + 1)
                        scores_max(h + 1)
                        scores(h)
                        turn_max(h + 1, n)
                        weigh(h - 1, n)
                scores(H - 1)
                weigh(H - 2, 0)
                weigh(H - 1, 1)
                pe.wait_ge(s_ctx, b * H + H)
                for tt in range(TT):
                    tp_wait(TP_C + tt)
                    for k in range(KT):
                        i = pe.transpose(ringT[:, tt % R, k * P:(k + 1) * P], xn[:, tt, k * P:(k + 1) * P], ident[:, :])
                    i.then_inc(tp_full, 1)
                for tt in range(TT):
                    sa_wait(SA_O + tt)
                    tp_wait(TP_C + tt + R)
                    for k in range(KT):
                        i = pe.matmul(ringA[:, tt % R, :], xnT[:, k, tt * P:(tt + 1) * P], wo[:, k, :],
                                      start=(k == 0), stop=(k == KT - 1))
                    i.then_inc(sa_full, 1)
                for tt in range(TT):
                    pe.wait_ge(s_l2, b * TT + (tt + 1))
                    for l in range(2):
                        tp_wait(TP_L + 2 * tt + l)
                        v = xhl[:, tt % R, l, :].rearrange("p (j c r) -> p j r c", j=2, r=2)
                        for k in range(KT):
                            i = pe.transpose(ringT16[:, l, k * P:(k + 1) * P], v[:, k // 2, k % 2, :], ident16[:, :])
                        i.then_inc(tp_full, 1)

                def gate_up(q, c, n):
                    w = wst[:, n % WS, 0:GU].rearrange("p (l m k c) -> p l m k c", l=2, m=2, k=KT)
                    pe.wait_ge(s_load[n % WS], b * (16 * NC // WS) + q * 16 + 16)
                    for m in range(2):
                        if m == 0:
                            pe.wait_ge(sb_free, b * SB_N + c + (SB_G + 1))
                            dst = ringB[:, n % R, :]
                        else:
                            pe.wait_ge(sa_free, b * SA_N + c + (SA_U + 1))
                            dst = ringA[:, n % R, :]
                        for k in range(KT):
                            for e, (wl, xl) in enumerate(((0, 0), (0, 1), (1, 0))):
                                i = pe.matmul(dst, w[:, wl, m, k, :], xT[:, xl, k, :], start=(k == 0 and e == 0),
                                              stop=(k == KT - 1 and e == 2))
                        i.then_inc(sb_full if m == 0 else sa_full, 1)

                def down(c, n, first, last):
                    w = wst[:, n % WS, GU:WCH].rearrange("p (l d) -> p l d", l=2)
                    pe.wait_ge(s_il, b * NC + c + (1 + R))
                    for tt in range(TT):
                        for e, (il, wl) in enumerate(((0, 0), (0, 1), (1, 0))):
                            i = pe.matmul(acc(tt), ihl[:, n % R, il, tt * P:(tt + 1) * P], w[:, wl, :],
                                          start=(first and e == 0), stop=(last and e == 2))
                    i.then_inc(s_wused, 1)

                pe.wait_ge(tp_free, b * TP_N + (TP_N + R))
                pe.wait_ge(s_of, b * H + (H + 1))
                gate_up(0, 0, 0)
                for n in range(3):
                    gate_up(0, n + 1, n + 1)
                    down(n, n, n == 0, False)
                with pe.Fori(1, NC // WS) as q:
                    for n in range(WS):
                        gate_up(q, q * WS + n, n)
                        down(q * WS + (n - 1), n - 1 + WS, False, False)
                down(NC - 1, NC - 1, False, True)
                pe.wait_ge(s_wused, b * NC + (NC + WS))
                pe.sem_inc(s_dn, 1)

            with pe.Fori(0, B) as b:
                batch(b)

        @block.vector
        def _(dve):
            dve.sem_inc(sa_free, R)
            dve.sem_inc(s_c16, R)
            dve.sem_inc(s_wf, R)
            dve.sem_inc(s_of, 1)
            dve.sem_inc(s_ost, 1)

            dve.wait_ge(s_scales, 48)
            dve.wait_ge(s_init, 1)
            dve.tensor_reduce(pgu[:, :, :], sgu[:, :, :, :], AX.X, ALU.max, apply_absolute_value=True)
            dve.tensor_reduce(stat[:, 1:2], sd[:, :, :].rearrange("p t k -> p (t k)"), AX.X, ALU.max,
                              apply_absolute_value=True)
            dve.drain()
            dve.tensor_scalar(pgu[:, :, :], pgu[:, :, :], TINY, None, ALU.max)
            dve.drain()
            dve.tensor_scalar(pgu[:, :, :].bitcast(U32), pgu[:, :, :].bitcast(U32), POW2, None, ALU.bitwise_and)
            dve.drain()
            dve.reciprocal(igu[:, :, :], pgu[:, :, :])
            dve.tensor_tensor(mprod[:, :], pgu[:, 0, :], pgu[:, 1, :], ALU.mult)
            dve.tensor_scalar(dg[:, :], pgu[:, 0, :], 1.0 / (W_UP * X_UP), None, ALU.mult)
            dve.drain()
            dve.tensor_scalar(mu[:, :], igu[:, 0, :], I_UP / (W_UP * X_UP), None, ALU.mult)
            dve.tensor_reduce(stat[:, 0:1], mprod[:, :], AX.X, ALU.max)
            dve.drain()
            dve.tensor_scalar(igu[:, :, :], igu[:, :, :], W_UP * CODE, None, ALU.mult)
            dve.drain()
            dve.tensor_tensor(sgu[:, :, :, :].rearrange("p m c k -> p (m c) k"), sgu[:, :, :, :].rearrange("p m c k -> p (m c) k"),
                              igu[:, :, :].rearrange("p m c -> p (m c)").unsqueeze(2).broadcast_to([P, 2 * NC, 16]),
                              ALU.mult).then_inc(s_stat, 1)
            dve.wait_ge(s_allmax, 1)
            dve.tensor_scalar(stat[:, 2:4], stat[:, 2:4], TINY, None, ALU.max)
            dve.drain()
            dve.tensor_scalar(stat[:, 2:4].bitcast(U32), stat[:, 2:4].bitcast(U32), POW2, None, ALU.bitwise_and)
            dve.drain()
            dve.reciprocal(stat[:, 4:6], stat[:, 2:4])
            dve.tensor_tensor(out_scale[:, :], stat[:, 2:3], stat[:, 3:4], ALU.mult)
            dve.drain()
            dve.tensor_scalar(mprod[:, :], mprod[:, :], stat[:, 4:5], None, ALU.mult)
            dve.tensor_scalar(sd[:, :, :], sd[:, :, :], stat[:, 5:6], W_UP * CODE, ALU.mult, ALU.mult).then_inc(s_norm, 1)
            dve.drain()

            def weights(u, n, down):
                dve.wait_ge(s_ct, u + (1 + R))
                dve.tensor_copy(codes16, ringOb[:, n, 0:512]).then_inc(s_c16, 1)
                dve.drain()
                for r in range(2):
                    dve.tensor_scalar(nib[:, r, :], codes16, 9 - 4 * r, 0x0E00, ALU.logical_shift_left, ALU.bitwise_and)
                    dve.tensor_scalar(nibs[:, r, :], codes16, 12 - 4 * r, 0x8000, ALU.logical_shift_left, ALU.bitwise_and)
                dve.drain()
                dve.tensor_tensor(nib, nib, nibs, ALU.bitwise_or)
                dve.drain()
                dve.wait_ge(s_ss, u + (1 + R))
                dve.wait_ge(s_wlo, u + 1)
                w = wf[:, n, :].rearrange("p (k r c) -> p r k c", k=4, r=2)
                s4 = ssb[:, n, :].rearrange("p (k c) -> p k c", k=4)
                for r in range(2):
                    v = nib[:, r, :].bitcast(F16).rearrange("p (k c) -> p k c", k=4)
                    if down is None:
                        i = dve.tensor_tensor(w[:, r], v, s4, ALU.mult)
                    else:
                        i = dve.scalar_tensor_tensor(w[:, r], v, mprod[:, bass.ds(down + r, 1)], s4, ALU.mult, ALU.mult)
                i.then_inc(s_wf, 1)

            with dve.Fori(0, UG // 2) as q:
                for n in range(2):
                    weights(2 * q + n, n, None)
            with dve.Fori(0, UD // 2) as q:
                for n in range(2):
                    weights(2 * q + (UG + n), n, 4 * q + 2 * n)

            dve.wait_ge(s_par, NPAR)
            dve.tensor_reduce(qk_p2[:, 0:1], qwb[:, :, :].rearrange("p a d -> p (a d)"), AX.X, ALU.max,
                              apply_absolute_value=True)
            dve.tensor_reduce(qk_p2[:, 1:2], kall[:, :, :].rearrange("p a d -> p (a d)"), AX.X, ALU.max,
                              apply_absolute_value=True)
            dve.drain()
            dve.tensor_scalar(qk_p2[:, 0:2], qk_p2[:, 0:2], TINY, None, ALU.max)
            dve.drain()
            dve.tensor_scalar(qk_p2[:, 0:2].bitcast(U32), qk_p2[:, 0:2].bitcast(U32), POW2, None, ALU.bitwise_and)
            dve.drain()
            dve.reciprocal(qk_p2[:, 2:4], qk_p2[:, 0:2])
            dve.scalar_tensor_tensor(exp_scale[:, :], qk_p2[:, 0:1], SCALE, qk_p2[:, 1:2], ALU.mult, ALU.mult)
            dve.drain()
            dve.tensor_scalar(qwb[:, :, :], qwb[:, :, :], qk_p2[:, 2:3], None, ALU.mult)
            dve.tensor_scalar(kwb[:, :, :, :].rearrange("p a b d -> p (a b d)"),
                              kwb[:, :, :, :].rearrange("p a b d -> p (a b d)"), qk_p2[:, 3:4], None, ALU.mult)
            for tt in range(TT):
                kind = tt // (TT - 1)
                dve.tensor_copy(cat[:, tt, :, QW:KW], kmask[:, kind, :].unsqueeze(1).broadcast_to([P, H, 2]))
                dve.tensor_copy(vv[:, tt, :, VW - 1:VW], kmask[:, kind, 0:1].unsqueeze(1).broadcast_to([P, H, 1]))
            dve.tensor_copy(vd[:, :, VW - 1:VW], kmask[:, 1, 1:2].unsqueeze(1).broadcast_to([P, H, 1]))
            dve.wait_ge(s_tanh, 1)
            dve.tensor_scalar(bo_b[:, :], bo_b[:, :], tgates[:, 0:1], None, ALU.mult)
            dve.tensor_scalar(out_scale[:, :], out_scale[:, :], tgates[:, 1:2], None, ALU.mult)
            dve.drain()

            dve.wait_ge(s_wlo, UG + UD + R)

            with dve.Fori(0, B) as b:
                def layer_norm(roots, up, tile):
                    for tt in range(TT):
                        dve.bn_stats(bst[:, tt, :], x_sb[:, tt, :])
                    dve.drain()
                    for tt in range(TT):
                        dve.bn_aggr(mv[:, tt, :], bst[:, tt, :])
                    dve.drain()
                    dve.tensor_scalar(rstd[:, :], mv[:, :, 1], up ** -2, EPS_X * up ** -2, ALU.mult,
                                      ALU.add).then_inc(s_var, 1)
                    dve.wait_ge(s_rstd, b * 4 + roots)
                    for tt in range(TT):
                        i = dve.tensor_scalar(xn[:, tt, :], x_sb[:, tt, :], mv[:, tt, 0:1], rstd[:, tt:tt + 1],
                                              ALU.subtract, ALU.mult)
                        tile(tt, i)

                dve.wait_ge(s_x, b * 16 + 16)
                layer_norm(1, 1.0, lambda tt, i: i.then_inc(s_xn, 1))

                def head_stats(a, tt, src):
                    dve.drain()
                    dve.tensor_reduce(hsum[:, :], src, AX.X, ALU.add)
                    dve.drain()
                    c = cen[:, a, tt, :].rearrange("p (h d) -> p h d", h=H)
                    dve.scalar_tensor_tensor(c, hsum[:, :].unsqueeze(2).broadcast_to([P, H, HD]), -1.0 / HD, src,
                                             ALU.mult, ALU.add)
                    dve.drain()
                    dve.tensor_tensor(t2[:, :], cen[:, a, tt, :], cen[:, a, tt, :], ALU.mult)
                    dve.drain()
                    dve.tensor_reduce(hrs[:, a, tt, :], t2[:, :].rearrange("p (h d) -> p h d", h=H), AX.X, ALU.add)
                    if tt == TT - 1:
                        dve.drain()
                        dve.tensor_scalar(hrs[:, a, :, :], hrs[:, a, :, :], 1.0 / HD, EPS_H, ALU.mult,
                                          ALU.add).then_inc(s_var, 1)

                for tt in range(TT):
                    dve.wait_ge(sa_full, b * SA_N + (SA_Q + tt + 1))
                    dve.tensor_tensor(t1[:, :], ringA[:, tt % R, :], bq_b[:, :], ALU.add).then_inc(sa_free, 1)
                    head_stats(0, tt, t1[:, :].rearrange("p (h d) -> p h d", h=H))

                def split_values(dst, src):
                    dve.tensor_copy(dst[:, :, 0:HD], src)
                    dve.drain()
                    dve.tensor_tensor(src, src, dst[:, :, 0:HD], ALU.subtract)
                    dve.drain()
                    dve.tensor_copy(dst[:, :, HD:2 * HD], src)
                    dve.drain()
                    return dve.tensor_tensor(dst[:, :, 2 * HD:3 * HD], src, dst[:, :, HD:2 * HD], ALU.subtract)

                for tt in range(TT):
                    kind = tt // (TT - 1)
                    for e in range(2):
                        dve.wait_ge(sa_full, b * SA_N + (SA_KV + 2 * tt + e + 1))
                        dve.tensor_tensor(t0[:, e * D:(e + 1) * D], ringA[:, e, :], bkv_b[:, kind, e * D:(e + 1) * D],
                                          ALU.add).then_inc(sa_free, 1)
                    kv = t0[:, :].rearrange("p (h w) -> p h w", h=H)
                    head_stats(1, tt, kv[:, :, 0:HD])
                    val = kv[:, :, HD:2 * HD]
                    if kind:
                        v2 = t1[:, :].rearrange("p (h d) -> p h d", h=H)
                        dve.tensor_scalar(v2, val, kmask[:, 1, 1:2], None, ALU.mult)
                        dve.drain()
                        dve.tensor_scalar(val, val, kmask[:, 1, 0:1], None, ALU.mult)
                        split_values(vd, v2)
                    i = split_values(vv[:, tt, :, :], val)
                    if kind:
                        i.then_inc(s_v, 1)
                    dve.drain()

                for a, wb in ((0, None), (1, None)):
                    dve.wait_ge(s_rstd, b * 4 + (2 + a))
                    if a:
                        dve.wait_ge(tp_full, b * TP_N + TP_K)
                    for tt in range(TT):
                        w = qwb if a == 0 else kwb[:, tt // (TT - 1), :, :]
                        c = cen[:, a, tt, :].rearrange("p (h d) -> p h d", h=H)
                        lo = 2 if a == 0 else 1
                        dve.tensor_tensor(c, c, hrs[:, a, tt, :].unsqueeze(2).broadcast_to([P, H, HD]), ALU.mult)
                        dve.drain()
                        dve.tensor_tensor(c, c, w[:, 0, :].unsqueeze(1).broadcast_to([P, H, HD]), ALU.mult)
                        dve.drain()
                        dve.tensor_tensor(c, c, w[:, 1, :].unsqueeze(1).broadcast_to([P, H, HD]), ALU.add)
                        dve.drain()
                        dve.tensor_copy(cat[:, tt, :, 0:HD], c)
                        dve.drain()
                        dve.tensor_tensor(cat[:, tt, :, lo * HD:(lo + 1) * HD], c, cat[:, tt, :, 0:HD],
                                          ALU.subtract).then_inc(s_hn, 1)
                dve.drain()

                def maxima(h, n):
                    dve.drain()
                    for tt in range(TT):
                        dve.wait_ge(sa_full, b * SA_N + h * TT + (SA_A + tt + 1))
                        dve.tensor_reduce(pmx[:, tt, :], ringA[:, tt % R, :].rearrange("p (g k) -> p g k", k=DCA),
                                          AX.X, ALU.max).then_inc(sa_free, 1)
                    dve.drain()
                    dve.wait_ge(tp_full, b * TP_N + h + (TP_M - 1))
                    dve.tensor_reduce(mneg[:, n, :, 0], pmx[:, :, 0:SM // DCA], AX.X, ALU.max, negate=True)
                    dve.tensor_scalar(mneg[:, n, :, 1], pmx[:, :, SM // DCA], -1.0, None, ALU.mult).then_inc(s_mneg, 1)

                def high(h, n):
                    dve.wait_ge(s_pv, b * H + h + 1)
                    for k in range(TT):
                        dve.wait_ge(sb_free, b * SB_N + h * TT + (k + 1 + R))
                        dve.tensor_copy(phl[:, n, 0, k, :], pf[:, k % R, :]).then_inc(s_ph, 1)

                def head_out(h, n):
                    dve.drain()
                    dve.wait_ge(s_pv, b * H + h + (1 + R))
                    o = ringO[:, :, 0:TT * VW].rearrange("p a (t w) -> p a t w", t=TT)
                    for a in range(2):
                        dve.tensor_reduce(osum[:, a, :, :], o[:, a, :, 0:3 * HD].rearrange("p t (w d) -> p t d w", w=3),
                                          AX.X, ALU.add)
                    dve.reciprocal(orec[:, :, :], o[:, :, :, VW - 1]).then_inc(s_of, 1)
                    dve.drain()
                    dve.tensor_tensor(osum[:, :, :, :].rearrange("p a t d -> p (a t) d"),
                                      osum[:, :, :, :].rearrange("p a t d -> p (a t) d"),
                                      orec[:, :, :].rearrange("p a t -> p (a t)").unsqueeze(2).broadcast_to([P, 2 * TT, HD]),
                                      ALU.mult)
                    dve.drain()
                    dve.tensor_tensor(xn[:, :, bass.ds(h * HD, HD)], osum[:, 0, :, :], osum[:, 1, :, :],
                                      ALU.add).then_inc(s_ctx, 1)

                maxima(0, 0)
                maxima(1, 1)
                high(0, 0)
                with dve.Fori(0, (H - 2) // 2) as q:
                    for n in range(2):
                        h = 2 * q + (n + 1)
                        maxima(h + 1, n)
                        high(h, 1 - n)
                        head_out(h - 1, n)
                high(H - 1, 1)
                head_out(H - 2, 0)
                head_out(H - 1, 1)

                for tt in range(TT):
                    dve.wait_ge(sa_full, b * SA_N + (SA_O + tt + 1))
                    dve.scalar_tensor_tensor(x_sb[:, tt, :], ringA[:, tt % R, :], tgates[:, 0:1], x_sb[:, tt, :],
                                             ALU.mult, ALU.add).then_inc(sa_free, 1)
                dve.drain()
                for tt in range(TT):
                    dve.tensor_tensor(x_sb[:, tt, :], x_sb[:, tt, :], bo_b[:, :], ALU.add)
                dve.drain()

                def split(tt, i):
                    dve.drain()
                    if tt >= R:
                        dve.wait_ge(tp_full, b * TP_N + (TP_L + 2 * (tt - R) + 2))
                    dve.tensor_copy(xhl[:, tt % R, 0, :], xn[:, tt, :])
                    dve.drain()
                    dve.tensor_tensor(xhl[:, tt % R, 1, :], xn[:, tt, :], xhl[:, tt % R, 0, :],
                                      ALU.subtract).then_inc(s_l2, 1)

                layer_norm(4, X_UP, split)
                with dve.Fori(0, NC // 2) as q:
                    for n in range(2):
                        dve.wait_ge(sa_full, b * SA_N + q * 2 + (SA_U + n + 1))
                        dve.wait_ge(sb_free, b * SB_N + q * 2 + (SB_G + n + 1 + R))
                        dve.wait_ge(s_il, b * NC + q * 2 + (n + 1))
                        dve.scalar_tensor_tensor(it[:, n, :], ringA[:, n, :], mu[:, bass.ds(q * 2 + n, 1)], gl[:, n, :],
                                                 ALU.mult, ALU.mult).then_inc(sa_free, 1)
                dve.wait_ge(s_dn, b + 1)
                for tt in range(TT):
                    dve.wait_ge(s_out[tt % R], b * (16 * TT // R) + (16 + 16 * (tt // R)))
                    dve.scalar_tensor_tensor(ost[:, tt % R, :], acc(tt), out_scale[:, 0:1], x_sb[:, tt, :],
                                             ALU.mult, ALU.add).then_inc(s_ost, 1)


_INS = ['x', 'ctx_1024', 'g_xattn', 'g_ffn'] + ['L0_xattn_' + n for n in (
    'Wq', 'bq', 'Wk', 'bk', 'Wv', 'bv', 'Wkv_dca', 'bkv_dca', 'qn_w', 'qn_b', 'kn_w', 'kn_b', 'kn_dca_w', 'kn_dca_b',
    'Wo', 'bo')] + ['L0_ffn_' + n for n in (
        'gate_W_packed', 'gate_scales', 'up_W_packed', 'up_scales', 'down_W_packed', 'down_scales')]
_OUTS = [((B, S, D), 'float32')]


def kernel(**inputs):
    import numpy as _np
    import concourse.bacc as _bacc
    from concourse import mybir as _mybir
    from concourse.bass_utils import run_bass_kernel_spmd as _run

    nc = _bacc.Bacc("TRN2", target_bir_lowering=False, num_devices=1)
    arrays, args = {}, []
    for name in _INS:
        a = _np.ascontiguousarray(inputs[name])
        arrays[f"in_{name}_dram"] = a
        args.append(nc.dram_tensor(f"in_{name}_dram", a.shape, _mybir.dt.from_np(a.dtype), kind="ExternalInput").ap())
    for i, (shape, dtype) in enumerate(_OUTS):
        dt = _mybir.dt.from_np(_np.dtype(dtype))
        args.append(nc.dram_tensor(f"out_{i}_dram", shape, dt, kind="ExternalOutput").ap())
    block_kernel(nc, *args)
    r = _run(nc, [arrays], core_ids=[0])
    return r.results[0]["out_0_dram"]
```

```python
from contextlib import ExitStack

import concourse.bass as bass
from concourse import mybir

F32 = mybir.dt.float32
F16 = mybir.dt.float16
BF16 = mybir.dt.bfloat16
I32 = mybir.dt.int32
U32 = mybir.dt.uint32
U16 = mybir.dt.uint16
U8 = mybir.dt.uint8
ALU = mybir.AluOpType
ACT = mybir.ActivationFunctionType
AX = mybir.AxisListType

P = 128
B, S, D = 4, 512, 512
H, HD = 16, 32
KD, DCA = 256, 16
SM = S - DCA
F = 4096
TT = S // P
KT = D // P
YT = KD // P
NC = F // P
LASTM = SM - (TT - 1) * P
VW = 3 * HD + 1
QW = 3 * HD
KW = QW + 2
EPS_X, EPS_H = 1e-5, 1e-6
SCALE = HD ** -0.5
WS = 4
R = 2
GU = 2 * 2 * KT * P
WCH = GU + 2 * D
GR = NC * 16 // P
SG = 2 * GR + TT
UG, UD = NC, NC // 2
POW2 = 0x7F800000
TINY = 2.0 ** -40
W_UP = 2.0 ** 10
X_UP = 2.0 ** 8
I_UP = 2.0 ** -10
CODE = 2.0 ** 14

PR = TT
NV = 1 + TT
ROOT = 1597463007.0
OST = (0, 2, 3, 1)

TP_X, TP_Y = 0, TT
TP_Q = TP_Y + TT
TP_K = TP_Q + H
TP_M = TP_K + H
TP_C = TP_M + H
TP_L = TP_C + TT
TP_N = TP_L + 2 * TT
SA_Q = 0
SA_KV = SA_Q + TT
SA_A = SA_KV + 2 * TT
SA_O = SA_A + TT * H
SA_U = SA_O + TT
SA_N = SA_U + NC
SB_B = 0
SB_G = TT * H
SB_N = SB_G + NC


def block_kernel(nc, x, ctx, g_xattn, g_ffn, Wq, bq, Wk, bk, Wv, bv, Wkv_dca, bkv_dca, qn_w, qn_b,
                 kn_w, kn_b, knd_w, knd_b, Wo, bo, gW, gS, uW, uS, dW, dS, out):
    wscratch = nc.dram_tensor("wscratch", [NC, P, WCH], F16, kind="Internal").ap()
    with ExitStack() as stack:
        def sb(name, shape, dt):
            return stack.enter_context(nc.sbuf_tensor(name, shape, dt))

        def psum(name, shape, dt):
            return stack.enter_context(nc.psum_tensor(name, shape, dt))

        def sem(name):
            return stack.enter_context(nc.semaphore(name))

        ident = sb("ident", [P, P], F32)
        ident16 = sb("ident16", [P, P], F16)
        identb = sb("identb", [P, P], BF16)
        wq = sb("wq", [P, KT, D], F32)
        wkv = sb("wkv", [P, YT, 2 * D], F32)
        wdca = sb("wdca", [P, YT, 2 * D], F32)
        wo = sb("wo", [P, KT, D], F32)
        bq_b = sb("bq_b", [P, D], F32)
        bkv_b = sb("bkv_b", [P, 2, 2 * D], F32)
        bo_b = sb("bo_b", [P, D], F32)
        qwb = sb("qwb", [P, 2, HD], F32)
        kwb = sb("kwb", [P, 2, 2, HD], F32)
        kall = sb("kall", [P, 4, HD], F32)
        gates = sb("gates", [P, 2], F32)
        tgates = sb("tgates", [P, 2], F32)
        kmask = sb("kmask", [P, 2, 2], F32)
        mhalf = sb("mhalf", [P, TT], F32)
        qk_p2 = sb("qk_p2", [P, 4], F32)
        exp_scale = sb("exp_scale", [P, 1], F32)
        dg = sb("dg", [P, NC], F32)
        mu = sb("mu", [P, NC], F32)
        out_scale = sb("out_scale", [P, 1], F32)
        scales = sb("scales", [P, SG * P], F32)
        sgu = scales[:, 0:2 * NC * 16].rearrange("p (m c k) -> p m c k", m=2, k=16)
        sd = scales[:, 2 * NC * 16:SG * P].rearrange("p (t k) -> p t k", t=TT)
        pgu = sb("pgu", [P, 2, NC], F32)
        igu = sb("igu", [P, 2, NC], F32)
        mprod = sb("mprod", [P, NC], F32)
        stat = sb("stat", [P, 8], F32)
        x_sb = sb("x_sb", [P, TT, D], F32)
        xn = sb("xn", [P, TT, D], F32)
        bst = sb("bst", [P, TT, 6], F32)
        mv = sb("mv", [P, TT, 2], F32)
        rstd = sb("rstd", [P, TT], F32)
        y_sb = sb("y_sb", [P, TT, KD], F32)
        yT = sb("yT", [P, YT, S], F32)
        yTd = sb("yTd", [P, YT, P], F32)
        xnT = sb("xnT", [P, KT, S], F32)
        val = sb("val", [P, D], F32)
        vald = sb("vald", [P, D], F32)
        sq = sb("sq", [P, R, D], F32)
        hsum = sb("hsum", [P, KT * H], F32)
        nv = sb("nv", [P, 2, TT * H], F32)
        hrs = sb("hrs", [P, 2, TT, H], F32)
        cat = sb("cat", [P, TT, H, KW], F16)
        qkT = sb("qkT", [P, 2, H, S], F16)
        vv = sb("vv", [P, TT, H, VW], BF16)
        vd = sb("vd", [P, H, VW], BF16)
        pmx = sb("pmx", [P, TT, S // DCA], F32)
        mneg = sb("mneg", [P, R, TT, 2], F16)
        pf = sb("pf", [P, PR, S], F32)
        phl = sb("phl", [P, R, 2, TT, S], F16)
        osum = sb("osum", [P, 2, TT, HD], F32)
        orec = sb("orec", [P, 2, TT], F32)
        gl = sb("gl", [P, R, S], F32)
        it = sb("it", [P, R, S], F32)
        ihl = sb("ihl", [P, R, 2, S], F16)
        xhl = sb("xhl", [P, R, 2, D], F16)
        ost = sb("ost", [P, R, D], F32)

        qT, kT = qkT[:, 0, :, :], qkT[:, 1, :, :]
        wst = qkT[:, :, :, :].rearrange("p a h t -> p (a h t)")[:, 0:WS * WCH].rearrange("p (s n) -> p s n", s=WS)
        xT = xnT[:, :, :].rearrange("p k t -> p (k t)").bitcast(F16).rearrange("p (l k t) -> p l k t", l=2, k=KT)
        cen = phl[:, :, :, :, :].rearrange("p r l k t -> p (r l k t)").bitcast(F32).rearrange(
            "p (a t d) -> p a t d", a=2, t=TT)
        codes = phl[:, 0, :, :, :].rearrange("p l k t -> p (l k t)").bitcast(I32).rearrange(
            "p (s k c) -> p s k c", s=4, k=4)
        codesb = phl[:, 1, 0, 0:2, :].bitcast(BF16)
        codes16 = phl[:, 1, 0, 2:4, :].bitcast(U16)
        nib = phl[:, 1, 1, 0:2, :].bitcast(U16)
        nibs = phl[:, 1, 1, 2:4, :].bitcast(U16)
        val16 = phl[:, 1, 1, 2:4, :]
        ssb = pf[:, 0:R, :].rearrange("p s n -> p (s n)").bitcast(F16).rearrange("p (s k l c) -> p s k l c", s=R, k=4, l=2)
        free16 = qkT[:, :, :, :].rearrange("p a h t -> p (a h t)")
        spread = free16[:, 0:16 * P].rearrange("p (j c) -> p j c", j=16)
        shl = free16[:, 16 * P:16 * P + 2 * SG * P].rearrange("p (l n) -> p l n", l=2)
        sT = free16[:, 16 * P + 2 * SG * P:16 * P + 4 * SG * P].rearrange("p (g l c) -> p g l c", g=SG, l=2)
        whl = xnT[:, :, :].rearrange("p k t -> p (k t)").bitcast(F16).rearrange("p (s n) -> p s n", s=R)

        ringA = psum("ringA", [P, R, 512], F32)
        ringB = psum("ringB", [P, R, 512], F32)
        ringO = psum("ringO", [P, R, 512], F32)
        ringT = psum("ringT", [P, R, 512], F32)
        ringT16 = ringT[:, :, :].bitcast(F16)
        ringOb = ringO[:, :, :].bitcast(BF16)

        s_init = sem("s_init")
        s_par = sem("s_par")
        s_scales = sem("s_scales")
        s_stat = sem("s_stat")
        s_allmax = sem("s_allmax")
        s_tanh = sem("s_tanh")
        s_code = [sem(f"s_code{i}") for i in range(4)]
        s_cb = sem("s_cb")
        s_shl = sem("s_shl")
        s_st = sem("s_st")
        s_stc = sem("s_stc")
        s_ct = sem("s_ct")
        s_c16 = sem("s_c16")
        s_ss = sem("s_ss")
        s_wf = sem("s_wf")
        s_wst = [sem(f"s_wst{i}") for i in range(R)]
        s_x = sem("s_x")
        s_xl = sem("s_xl")
        s_y = sem("s_y")
        s_var = sem("s_var")
        s_rstd = sem("s_rstd")
        s_xn = sem("s_xn")
        tp_full, tp_free = sem("tp_full"), sem("tp_free")
        sa_full, sa_free = sem("sa_full"), sem("sa_free")
        sb_full, sb_free = sem("sb_full"), sem("sb_free")
        s_cen = sem("s_cen")
        s_sq = sem("s_sq")
        s_hn = sem("s_hn")
        s_cat = sem("s_cat")
        s_hl = sem("s_hl")
        s_v = sem("s_v")
        s_mneg = sem("s_mneg")
        s_pl = sem("s_pl")
        s_pv = sem("s_pv")
        s_of = sem("s_of")
        s_ctx = sem("s_ctx")
        s_l2 = sem("s_l2")
        s_load = [sem(f"s_load{i}") for i in range(WS)]
        s_wused = sem("s_wused")
        s_ih = sem("s_ih")
        s_il = sem("s_il")
        s_dn = sem("s_dn")
        s_ost = sem("s_ost")
        s_out = [sem(f"s_out{i}") for i in range(R)]

        def turn_bank(i):
            return (ringO[:, 0, :], ringO[:, 1, :], ringA[:, 0, :])[i].bitcast(F16)

        def spread_ring(n):
            return (ringB, ringT)[n % R][:, :, :]

        def acc(tt):
            return ringO[:, tt, :] if tt < R else ringT[:, tt - R, :]

        params = [
            (wq[:, :, :], Wq.rearrange("(k p) n -> p k n", p=P)),
            (wkv[:, :, 0:D], Wk.rearrange("(k p) n -> p k n", p=P)),
            (wkv[:, :, D:2 * D], Wv.rearrange("(k p) n -> p k n", p=P)),
            (wdca[:, :, :], Wkv_dca.rearrange("(k p) n -> p k n", p=P)),
            (wo[:, :, :], Wo.rearrange("(k p) n -> p k n", p=P)),
            (bq_b[:, :], bq.partition_broadcast(P)),
            (bo_b[:, :], bo.partition_broadcast(P)),
            (bkv_b[:, 0, 0:D], bk.partition_broadcast(P)),
            (bkv_b[:, 0, D:2 * D], bv.partition_broadcast(P)),
            (bkv_b[0:LASTM, 1, 0:D], bk.partition_broadcast(LASTM)),
            (bkv_b[0:LASTM, 1, D:2 * D], bv.partition_broadcast(LASTM)),
            (bkv_b[LASTM:P, 1, :].rearrange("p (h a d) -> p a h d", h=H, a=2)[:, 0],
             bkv_dca[0:D].rearrange("(h d) -> h d", h=H).partition_broadcast(DCA)),
            (bkv_b[LASTM:P, 1, :].rearrange("p (h a d) -> p a h d", h=H, a=2)[:, 1],
             bkv_dca[D:2 * D].rearrange("(h d) -> h d", h=H).partition_broadcast(DCA)),
            (qwb[:, 0, :], qn_w.partition_broadcast(P)),
            (qwb[:, 1, :], qn_b.partition_broadcast(P)),
            (kwb[:, 0, 0, :], kn_w.partition_broadcast(P)),
            (kwb[:, 0, 1, :], kn_b.partition_broadcast(P)),
            (kwb[0:LASTM, 1, 0, :], kn_w.partition_broadcast(LASTM)),
            (kwb[0:LASTM, 1, 1, :], kn_b.partition_broadcast(LASTM)),
            (kwb[LASTM:P, 1, 0, :], knd_w.partition_broadcast(DCA)),
            (kwb[LASTM:P, 1, 1, :], knd_b.partition_broadcast(DCA)),
            (kall[:, 0, :], kn_w.partition_broadcast(P)),
            (kall[:, 1, :], kn_b.partition_broadcast(P)),
            (kall[:, 2, :], knd_w.partition_broadcast(P)),
            (kall[:, 3, :], knd_b.partition_broadcast(P)),
            (gates[:, 0:1], g_xattn.partition_broadcast(P)),
            (gates[:, 1:2], g_ffn.partition_broadcast(P)),
        ]
        NPAR = 16 * len(params)

        block = stack.enter_context(nc.Block())

        @block.sync
        def _(sp):
            for n in range(R):
                sp.sem_inc(s_wst[n], 16)
                sp.sem_inc(s_out[n], 16)
            for m, sc in enumerate((gS, uS)):
                sp.dma_start(sgu[:, m, :, :].rearrange("p (j r) k -> p j (r k)", r=2),
                             sc.rearrange("(j p r) k -> p j (r k)", p=P, r=2)).then_inc(s_scales, 16)
            sp.dma_start(sd[:, :, :], dS.rearrange("(t p) k -> p t k", p=P)).then_inc(s_scales, 16)

            gWv = gW.rearrange("(j p r) k -> j r p k", p=P, r=2)
            uWv = uW.rearrange("(j p r) k -> j r p k", p=P, r=2)
            dWv = dW.rearrange("(t p) (j c) -> j p t c", p=P, j=UD)

            def codes_gu(j, r, slot):
                sp.dma_start(codes[:, slot, 0:2, :].rearrange("p k c -> p (k c)"), gWv[j, r]).then_inc(s_code[slot], 16)
                sp.dma_start(codes[:, slot, 2:4, :].rearrange("p k c -> p (k c)"), uWv[j, r]).then_inc(s_code[slot], 16)

            def codes_d(j, slot):
                sp.dma_start(codes[:, slot, 0:2, :], dWv[j][:, 0:2]).then_inc(s_code[slot], 16)
                sp.dma_start(codes[:, slot, 2:4, :], dWv[j][:, 2:4]).then_inc(s_code[slot], 16)

            for n in range(4):
                codes_gu(n // 2, n % 2, n)
            for dst, src in params:
                sp.dma_start(dst, src).then_inc(s_par, 16)
            sp.dma_start(xn[:, :, :], x[0].rearrange("(t p) d -> p t d", p=P)).then_inc(s_xl, 16)
            sp.dma_start(x_sb[:, :, :], x[0].rearrange("(t p) d -> p t d", p=P)).then_inc(s_x, 16)
            sp.dma_start(y_sb[:, :, :], ctx[0].rearrange("(t p) d -> p t d", p=P)).then_inc(s_y, 16)

            def store_gu(c, u, n):
                sp.wait_ge(s_wf, u + (1 + R))
                sp.dma_start(wscratch[c][:, 0:GU], whl[:, n % R, :]).then_inc(s_wst[n % R], 16)

            with sp.Fori(0, UG // 4 - 1) as q:
                for n in range(4):
                    sp.wait_ge(s_cb, 4 * q + (n + 1))
                    codes_gu(2 * q + (2 + n // 2), n % 2, n)
                    store_gu(4 * q + n, 4 * q + n, n)
            for n in range(4):
                sp.wait_ge(s_cb, UG - 4 + n + 1)
                codes_d(n, n)
                store_gu(UG - 4 + n, UG - 4 + n, n)

            def store_d(j, u, n):
                sp.wait_ge(s_wf, u + (1 + R))
                for r in range(2):
                    sp.dma_start(wscratch[2 * j + r][:, GU:WCH], whl[:, n % R, r * 2 * D:(r + 1) * 2 * D]).then_inc(
                        s_wst[n % R], 16)

            with sp.Fori(0, UD // 4 - 1) as q:
                for n in range(4):
                    sp.wait_ge(s_cb, 4 * q + (UG + n + 1))
                    codes_d(4 * q + (4 + n), n)
                    store_d(4 * q + n, 4 * q + (UG + n), n)
            for n in range(4):
                store_d(UD - 4 + n, UG + UD - 4 + n, n)
            for n in range(R):
                sp.wait_ge(s_wst[n], 16 + 16 * UG // R + 32 * UD // R)

            def batch(b, last):
                heads = sp.snap(b * H + (H + R)) if not last else B * H + R
                with sp.Fori(0, NC // WS) as q:
                    for n in range(WS):
                        sp.wait_ge(s_wused, b * NC + q * WS + (n + 1))
                        sp.wait_ge(s_pv, heads)
                        sp.dma_start(wst[:, n, :], wscratch[q * WS + n]).then_inc(s_load[n], 16)
                if not last:
                    sp.dma_start(xn[:, :, :], x[b + 1].rearrange("(t p) d -> p t d", p=P)).then_inc(s_xl, 16)
                    sp.dma_start(y_sb[:, :, :], ctx[b + 1].rearrange("(t p) d -> p t d", p=P)).then_inc(s_y, 16)
                for i, tt in enumerate(OST):
                    sp.wait_ge(s_ost, b * TT + (i + R + 1))
                    sp.dma_start(out[b, tt * P:(tt + 1) * P, :], ost[:, i % R, :]).then_inc(s_out[i % R], 16)
                if not last:
                    sp.dma_start(x_sb[:, :, :], x[b + 1].rearrange("(t p) d -> p t d", p=P)).then_inc(s_x, 16)

            with sp.Fori(0, B - 1) as b:
                batch(b, False)
            batch(B - 1, True)
            for n in range(R):
                sp.wait_ge(s_out[n], 16 + 16 * B * TT // R)

        @block.gpsimd
        def _(pool):
            for m in (ident, ident16, identb):
                pool.memset(m[:, :], 0.0)
            pool.memset(mhalf[:, :], -0.5)
            pool.memset(kmask[:, :, :], 0.0)
            pool.memset(yTd[:, :, :], 0.0)
            pool.memset(yT[:, :, SM:S], 0.0)
            pool.drain()
            for m in (ident, ident16, identb):
                pool.affine_select(out=m[:, :], in_=m[:, :], compare_op=ALU.not_equal, fill=1.0,
                                   base=0, pattern=[[-1, P]], channel_multiplier=1)
            pool.memset(kmask[:, 0, 0:1], 1.0)
            pool.affine_select(out=kmask[:, 1, 0:1], in_=kmask[:, 1, 0:1], compare_op=ALU.is_ge, fill=1.0,
                               base=-LASTM, pattern=[[0, 1]], channel_multiplier=1)
            pool.affine_select(out=kmask[:, 1, 1:2], in_=kmask[:, 1, 1:2], compare_op=ALU.is_gt, fill=1.0,
                               base=LASTM, pattern=[[0, 1]], channel_multiplier=-1)
            pool.memset(spread, 1.0)
            pool.drain()
            pool.affine_select(out=spread, in_=spread, compare_op=ALU.is_ge, fill=0.0,
                               base=0, pattern=[[P, 16], [1, P]], channel_multiplier=-16)
            pool.drain()
            pool.affine_select(out=spread, in_=spread, compare_op=ALU.is_ge, fill=0.0,
                               base=15, pattern=[[-P, 16], [-1, P]], channel_multiplier=16)
            pool.drain()
            pool.memset(stat[:, 6:8], 0.0).then_inc(s_init, 1)
            pool.sem_inc(s_il, R)
            pool.wait_ge(s_stat, 1)
            pool.partition_all_reduce(stat[:, 2:4], stat[:, 0:2], P, bass.bass_isa.ReduceOp.max).then_inc(s_allmax, 1)
            def inverse_root(v, n, count):
                pool.wait_ge(s_var, count)
                pool.tensor_tensor(v, v, mhalf[:, 0:n], ALU.pow).then_inc(s_rstd, 1)

            with pool.Fori(0, B) as b:
                inverse_root(rstd[:, :], TT, b * NV + 1)
                for tt in range(TT):
                    inverse_root(rstd[:, tt:tt + 1], 1, b * NV + (2 + tt))
                with pool.Fori(0, NC // 2) as q:
                    for n in range(2):
                        pool.wait_ge(s_ih, b * NC + 2 * q + (n + 1))
                        pool.tensor_tensor(ihl[:, n, 1, :], it[:, n, :], ihl[:, n, 0, :], ALU.subtract).then_inc(s_il, 1)

        @block.scalar
        def _(act):
            act.sem_inc(tp_free, R)
            act.sem_inc(sb_free, R)
            act.sem_inc(s_c16, R)
            act.sem_inc(s_ss, R)

            def cast_codes(q, n):
                act.wait_ge(s_code[n], q * 32 + 32)
                act.wait_ge(s_ct, q * 4 + (n + 1))
                act.activation(codesb[:, n % R, :],
                               codes[:, n, :, :].rearrange("p k c -> p (k c)").bitcast(U8)[:, 0:4 * 512:4],
                               ACT.Copy).then_inc(s_cb, 1)

            def codes_out(u, n):
                act.wait_ge(s_ct, u + (1 + R))
                act.wait_ge(s_wf, u + 1)
                act.activation(codes16[:, n % R, :], ringOb[:, n % R, 0:512], ACT.Copy).then_inc(s_c16, 1)
                act.activation(ssb[:, n % R, :, :, :].rearrange("p k l c -> p (k l c)"),
                               spread_ring(n).rearrange("p a b -> p (a b)"), ACT.Copy).then_inc(s_ss, 1)

            for i in range(3):
                act.wait_ge(s_st, i + 1)
                act.activation(sT[:, 4 * i:4 * i + 4, :, :].rearrange("p g l c -> p (g l c)"), turn_bank(i),
                               ACT.Copy).then_inc(s_stc, 1)
            cast_codes(0, 0)
            cast_codes(0, 1)
            codes_out(0, 0)
            with act.Fori(0, (UG + UD) // 4 - 1) as q:
                for n in range(4):
                    cast_codes(q + (n + 2) // 4, (n + 2) % 4)
                    codes_out(q * 4 + (n + 1), n + 1)
            for n in range(3):
                if n < 2:
                    cast_codes((UG + UD) // 4 - 1, n + 2)
                codes_out(UG + UD - 4 + n + 1, n + 1)

            for n in range(R):
                act.wait_ge(s_wst[n], 16 + 16 * UG // R + 32 * UD // R)
            act.wait_ge(s_par, NPAR)
            act.activation(tgates[:, :], gates[:, :], ACT.Tanh).then_inc(s_tanh, 1)

            with act.Fori(0, B) as b:
                def tp_wait(i):
                    act.wait_ge(tp_full, b * TP_N + (i + 1))

                for tt in range(TT):
                    tp_wait(TP_X + tt)
                    act.activation(xnT[:, :, tt * P:(tt + 1) * P],
                                   ringT[:, tt % R, :].rearrange("p (k t) -> p k t", k=KT), ACT.Copy).then_inc(tp_free, 1)
                for tt in range(TT):
                    tp_wait(TP_Y + tt)
                    src = ringT[:, tt % R, 0:YT * P].rearrange("p (k t) -> p k t", k=YT)
                    if tt < TT - 1:
                        i = act.activation(yT[:, :, tt * P:(tt + 1) * P], src, ACT.Copy)
                    else:
                        act.activation(yT[:, :, tt * P:SM], src[:, :, 0:LASTM], ACT.Copy)
                        i = act.activation(yTd[:, :, LASTM:P], src[:, :, LASTM:P], ACT.Copy)
                    i.then_inc(tp_free, 1)
                def squares(i):
                    act.wait_ge(s_cen, b * (2 * TT) + (i + 1))
                    act.activation(sq[:, i % R, :], cen[:, i // TT, i % TT, :], ACT.Square).then_inc(s_sq, 1)

                def high(a):
                    for tt in range(TT):
                        act.wait_ge(s_hn, b * (2 * TT) + (a * TT + tt + 1))
                        c = cen[:, a, tt, :].rearrange("p (h d) -> p h d", h=H)
                        hi = cat[:, tt, :, 0:QW].rearrange("p h (w d) -> p h w d", w=3)[:, :, 0:2 + a:1 + a, :]
                        act.activation(hi, c.unsqueeze(2).broadcast_to([P, H, 2, HD]), ACT.Copy).then_inc(s_cat, 1)

                def turned(a, start, heads):
                    tp, rows = ((TP_Q, QW), (TP_K, KW))[a]
                    with act.Fori(start // R, (start + heads) // R) as q:
                        for n in range(R):
                            act.wait_ge(tp_full, b * TP_N + R * q + (tp + n + 1))
                            act.activation(qkT[0:rows, a, bass.ds(R * q + n, 1), :].rearrange("p a t -> p (a t)"),
                                           ringT16[0:rows, n, 0:S], ACT.Copy).then_inc(tp_free, 1)

                for i in range(TT + 1):
                    squares(i)
                high(0)
                squares(TT + 1)
                turned(0, 0, H // 2)
                squares(TT + 2)
                turned(0, H // 2, H // 2)
                squares(TT + 3)
                high(1)
                turned(1, 0, H)

                def maxima(h, n):
                    act.wait_ge(tp_full, b * TP_N + h + (TP_M + 1))
                    act.activation(qT[QW:KW, bass.ds(h, 1), :].rearrange("p a t -> p (a t)"),
                                   ringT16[QW:KW, n, 0:S], ACT.Copy).then_inc(tp_free, 1)

                def exps(h, n):
                    act.wait_ge(s_pv, b * H + h + 1)
                    for k in range(TT):
                        act.wait_ge(sb_full, b * SB_N + h * TT + (k + 1))
                        if k % 2 == 0:
                            act.wait_ge(s_pl, b * (H * 2) + h * 2 + (k // 2 + 1))
                        act.activation(pf[:, k, :], ringB[:, k % R, :], ACT.Exp, scale=exp_scale[:, 0:1])
                        act.activation(phl[:, n, 0, k, :], ringB[:, k % R, :], ACT.Exp, scale=exp_scale[:, 0:1]).then_inc(sb_free, 1)

                maxima(0, 0)
                exps(0, 0)
                maxima(1, 1)
                with act.Fori(0, (H - 2) // 2) as q:
                    for n in range(2):
                        exps(2 * q + (n + 1), 1 - n)
                        maxima(2 * q + (n + 2), n)
                exps(H - 1, 1)
                for tt in range(TT):
                    tp_wait(TP_C + tt)
                    act.activation(xnT[:, :, tt * P:(tt + 1) * P],
                                   ringT[:, tt % R, :].rearrange("p (k t) -> p k t", k=KT), ACT.Copy).then_inc(tp_free, 1)
                for tt in range(TT):
                    for l in range(2):
                        tp_wait(TP_L + 2 * tt + l)
                        act.activation(xT[:, l, :, tt * P:(tt + 1) * P],
                                       ringT16[:, l, 0:512].rearrange("p (k t) -> p k t", k=KT), ACT.Copy).then_inc(tp_free, 1)
                with act.Fori(0, NC // 2) as q:
                    for n in range(2):
                        act.wait_ge(sb_full, b * SB_N + q * 2 + (SB_G + n + 1))
                        act.wait_ge(sa_free, b * SA_N + q * 2 + (SA_U + n + 1))
                        act.activation(gl[:, n, :], ringB[:, n, :], ACT.Gelu_apprx_tanh,
                                       scale=dg[:, bass.ds(q * 2 + n, 1)]).then_inc(sb_free, 1)
                        act.wait_ge(sa_free, b * SA_N + q * 2 + (SA_U + n + 1 + R))
                        act.wait_ge(s_wused, b * NC + q * 2 + (n + 1 + WS - R))
                        act.activation(ihl[:, n, 0, :], it[:, n, :], ACT.Copy).then_inc(s_ih, 1)

        @block.tensor
        def _(pe):
            pe.sem_inc(s_ct, R)
            pe.sem_inc(s_pv, R)
            pe.sem_inc(s_wused, WS)
            pe.wait_ge(s_init, 1)

            pe.wait_ge(s_shl, 1)
            for i in range(3):
                for g in range(4):
                    for l in range(2):
                        e = pe.transpose(turn_bank(i)[:, (2 * g + l) * P:(2 * g + l + 1) * P],
                                         shl[:, l, (4 * i + g) * P:(4 * i + g + 1) * P], ident16[:, :])
                e.then_inc(s_st, 1)
            pe.wait_ge(s_stc, 3)

            def turn(u, n, block_of):
                pe.wait_ge(s_cb, u + 1)
                pe.wait_ge(s_c16, u + 1)
                for k in range(4):
                    pe.transpose(ringOb[:, n, k * P:(k + 1) * P], codesb[:, n, k * P:(k + 1) * P], identb[:, :])
                pe.wait_ge(s_ss, u + 1)
                for k in range(4):
                    e, g = block_of(k)
                    i = pe.matmul(spread_ring(n)[:, k // 2, (k % 2) * 2 * P:(k % 2 + 1) * 2 * P],
                                  spread[:, bass.ds(e, 1), :].rearrange("p a c -> p (a c)"),
                                  sT[:, g, :, :].rearrange("p a l c -> p (a l c)"), start=True, stop=True)
                i.then_inc(s_ct, 1)

            with pe.Fori(0, GR) as g:
                with pe.Fori(0, NC // GR // 2) as q:
                    for n in range(2):
                        turn((NC // GR) * g + 2 * q + n, n,
                             lambda k: (4 * q + (2 * n + k % 2), bass.ds(g + GR * (k // 2), 1)))
            with pe.Fori(0, UD // 2) as q:
                for n in range(2):
                    turn(2 * q + (UG + n), n, lambda k: (2 * q + n, slice(2 * GR + k, 2 * GR + k + 1)))
            pe.wait_ge(s_c16, UG + UD + R)
            pe.wait_ge(s_ss, UG + UD + R)
            pe.wait_ge(s_par, NPAR)

            def batch(b):
                def tp_wait(i):
                    pe.wait_ge(tp_free, b * TP_N + (i + 1))

                def sa_wait(i):
                    pe.wait_ge(sa_free, b * SA_N + (i + 1))

                pe.wait_ge(s_ost, b * TT + 1)
                for tt in range(TT):
                    tp_wait(TP_X + tt)
                    pe.wait_ge(s_xn, b * TT + (tt + 1))
                    for k in range(KT):
                        i = pe.transpose(ringT[:, tt % R, k * P:(k + 1) * P], xn[:, tt, k * P:(k + 1) * P], ident[:, :])
                    i.then_inc(tp_full, 1)
                pe.wait_ge(s_y, b * 16 + 16)
                for tt in range(TT):
                    tp_wait(TP_Y + tt)
                    for k in range(YT):
                        i = pe.transpose(ringT[:, tt % R, k * P:(k + 1) * P], y_sb[:, tt, k * P:(k + 1) * P], ident[:, :])
                    i.then_inc(tp_full, 1)
                for tt in range(TT):
                    sa_wait(SA_Q + tt)
                    tp_wait(TP_X + tt + R)
                    for k in range(KT):
                        i = pe.matmul(ringA[:, tt % R, :], xnT[:, k, tt * P:(tt + 1) * P], wq[:, k, :],
                                      start=(k == 0), stop=(k == KT - 1))
                    i.then_inc(sa_full, 1)
                def keys_values(tt):
                    tp_wait(TP_Y + tt + R)
                    for e in range(2):
                        sa_wait(SA_KV + 2 * tt + e)
                        last = tt == TT - 1
                        for k in range(YT):
                            i = pe.matmul(ringA[:, e, :], yT[:, k, tt * P:(tt + 1) * P], wkv[:, k, e * D:(e + 1) * D],
                                          start=(k == 0), stop=(k == YT - 1 and not last))
                        if last:
                            for k in range(YT):
                                w = wdca[:, k, :].rearrange("p (a h d) -> p h a d", a=2, h=H)
                                i = pe.matmul(ringA[:, e, :], yTd[:, k, :], w[:, e * (H // 2):(e + 1) * (H // 2)],
                                              start=False, stop=(k == YT - 1))
                        i.then_inc(sa_full, 1)
                def turn_qk(a, start, heads):
                    tp, rows = ((TP_Q, QW), (TP_K, KW))[a]
                    with pe.Fori(start // R, (start + heads) // R) as q:
                        for n in range(R):
                            pe.wait_ge(s_hl, b * (2 * TT) + (a + 1) * TT)
                            pe.wait_ge(tp_free, b * TP_N + R * q + (tp + n + 1))
                            for tt in range(TT):
                                i = pe.transpose(ringT16[0:rows, n, tt * P:(tt + 1) * P],
                                                 cat[:, tt, bass.ds(R * q + n, 1), 0:rows].rearrange("p a w -> p (a w)"),
                                                 ident16[:, :])
                            i.then_inc(tp_full, 1)

                keys_values(0)
                keys_values(1)
                turn_qk(0, 0, H // 2)
                keys_values(2)
                turn_qk(0, H // 2, H // 2)
                keys_values(3)
                turn_qk(1, 0, H)

                def scores_max(h, tiles=range(TT)):
                    for tt in tiles:
                        pe.wait_ge(sa_free, b * SA_N + h * TT + (SA_A + tt + 1))
                        pe.matmul(ringA[:, tt % R, :], qT[0:QW, bass.ds(h, 1), tt * P:(tt + 1) * P].rearrange("p a t -> p (a t)"),
                                  kT[0:QW, bass.ds(h, 1), :].rearrange("p a t -> p (a t)"),
                                  start=True, stop=True).then_inc(sa_full, 1)

                def turn_max(h, n):
                    pe.wait_ge(s_mneg, b * H + h + 1)
                    pe.wait_ge(tp_free, b * TP_N + h + (TP_M + 1))
                    for tt in range(TT):
                        i = pe.transpose(ringT16[QW:KW, n, tt * P:(tt + 1) * P], mneg[:, n, tt, :], ident16[:, :])
                    i.then_inc(tp_full, 1)

                def scores(h, tiles=range(TT)):
                    pe.wait_ge(tp_free, b * TP_N + h + (TP_M + 1 + R))
                    for k in tiles:
                        pe.wait_ge(sb_free, b * SB_N + h * TT + (k + 1))
                        pe.matmul(ringB[:, k % R, :], kT[0:KW, bass.ds(h, 1), k * P:(k + 1) * P].rearrange("p a t -> p (a t)"),
                                  qT[0:KW, bass.ds(h, 1), :].rearrange("p a t -> p (a t)"),
                                  start=True, stop=True).then_inc(sb_full, 1)

                def weigh(h, n):
                    pe.wait_ge(s_pl, b * (H * 2) + h * 2 + (2 + PR // 2))
                    pe.wait_ge(s_of, b * H + h + 1)
                    for tt in range(TT):
                        for k in range(TT):
                            for l in range(2):
                                pe.matmul(ringO[:, 0, tt * VW:(tt + 1) * VW], phl[:, n, l, k, tt * P:(tt + 1) * P],
                                          vv[:, k, bass.ds(h, 1), :].rearrange("p a w -> p (a w)"),
                                          start=(k == 0 and l == 0), stop=(k == TT - 1 and l == 1))
                        for l in range(2):
                            i = pe.matmul(ringO[:, 1, tt * VW:(tt + 1) * VW], phl[:, n, l, TT - 1, tt * P:(tt + 1) * P],
                                          vd[:, bass.ds(h, 1), :].rearrange("p a w -> p (a w)"),
                                          start=(l == 0), stop=(l == 1))
                    i.then_inc(s_pv, 1)

                pe.wait_ge(tp_free, b * TP_N + (TP_M + R))
                pe.wait_ge(s_v, b + 1)
                scores_max(0)
                turn_max(0, 0)
                scores_max(1)
                scores(0)
                turn_max(1, 1)
                with pe.Fori(0, (H - 2) // 2) as q:
                    for n in range(2):
                        h = 2 * q + (n + 1)
                        scores_max(h + 1, (0, 1))
                        scores(h, (0, 1))
                        scores_max(h + 1, (2, 3))
                        scores(h, (2, 3))
                        turn_max(h + 1, n)
                        weigh(h - 1, n)
                scores(H - 1)
                weigh(H - 2, 0)
                weigh(H - 1, 1)
                pe.wait_ge(s_ctx, b * H + H)
                for tt in range(TT):
                    tp_wait(TP_C + tt)
                    for k in range(KT):
                        i = pe.transpose(ringT[:, tt % R, k * P:(k + 1) * P], xn[:, tt, k * P:(k + 1) * P], ident[:, :])
                    i.then_inc(tp_full, 1)
                for tt in range(TT):
                    sa_wait(SA_O + tt)
                    tp_wait(TP_C + tt + R)
                    for k in range(KT):
                        i = pe.matmul(ringA[:, tt % R, :], xnT[:, k, tt * P:(tt + 1) * P], wo[:, k, :],
                                      start=(k == 0), stop=(k == KT - 1))
                    i.then_inc(sa_full, 1)
                for tt in range(TT):
                    pe.wait_ge(s_l2, b * TT + (tt + 1))
                    for l in range(2):
                        tp_wait(TP_L + 2 * tt + l)
                        v = xhl[:, tt % R, l, :].rearrange("p (j c r) -> p j r c", j=2, r=2)
                        for k in range(KT):
                            i = pe.transpose(ringT16[:, l, k * P:(k + 1) * P], v[:, k // 2, k % 2, :], ident16[:, :])
                        i.then_inc(tp_full, 1)

                def gate_up(q, c, n):
                    w = wst[:, n % WS, 0:GU].rearrange("p (l m k c) -> p l m k c", l=2, m=2, k=KT)
                    pe.wait_ge(s_load[n % WS], b * (16 * NC // WS) + q * 16 + 16)
                    for m in range(2):
                        if m == 0:
                            pe.wait_ge(sb_free, b * SB_N + c + (SB_G + 1))
                            dst = ringB[:, n % R, :]
                        else:
                            pe.wait_ge(sa_free, b * SA_N + c + (SA_U + 1))
                            dst = ringA[:, n % R, :]
                        for k in range(KT):
                            for e, (wl, xl) in enumerate(((0, 0), (0, 1), (1, 0))):
                                i = pe.matmul(dst, w[:, wl, m, k, :], xT[:, xl, k, :], start=(k == 0 and e == 0),
                                              stop=(k == KT - 1 and e == 2))
                        i.then_inc(sb_full if m == 0 else sa_full, 1)

                def down(c, n, first, last):
                    w = wst[:, n % WS, GU:WCH].rearrange("p (l d) -> p l d", l=2)
                    pe.wait_ge(s_il, b * NC + c + (1 + R))
                    for tt in range(TT):
                        for e, (il, wl) in enumerate(((0, 0), (0, 1), (1, 0))):
                            i = pe.matmul(acc(tt), ihl[:, n % R, il, tt * P:(tt + 1) * P], w[:, wl, :],
                                          start=(first and e == 0), stop=(last and e == 2))
                    i.then_inc(s_wused, 1)

                pe.wait_ge(tp_free, b * TP_N + (TP_N + R))
                pe.wait_ge(s_of, b * H + (H + 1))
                gate_up(0, 0, 0)
                for n in range(3):
                    gate_up(0, n + 1, n + 1)
                    down(n, n, n == 0, False)
                with pe.Fori(1, NC // WS) as q:
                    for n in range(WS):
                        gate_up(q, q * WS + n, n)
                        down(q * WS + (n - 1), n - 1 + WS, False, False)
                down(NC - 1, NC - 1, False, True)
                pe.wait_ge(s_wused, b * NC + (NC + WS))
                pe.sem_inc(s_dn, 1)

            with pe.Fori(0, B) as b:
                batch(b)

        @block.vector
        def _(dve):
            dve.sem_inc(sa_free, R)
            dve.sem_inc(s_wf, R)
            dve.sem_inc(s_of, 1)
            dve.sem_inc(s_ost, R)
            dve.sem_inc(s_pl, PR // 2)

            dve.wait_ge(s_scales, 48)
            dve.wait_ge(s_init, 1)
            dve.tensor_reduce(pgu[:, :, :], sgu[:, :, :, :], AX.X, ALU.max, apply_absolute_value=True)
            dve.tensor_reduce(stat[:, 1:2], sd[:, :, :].rearrange("p t k -> p (t k)"), AX.X, ALU.max,
                              apply_absolute_value=True)
            dve.drain()
            dve.tensor_scalar(pgu[:, :, :], pgu[:, :, :], TINY, None, ALU.max)
            dve.drain()
            dve.tensor_scalar(pgu[:, :, :].bitcast(U32), pgu[:, :, :].bitcast(U32), POW2, None, ALU.bitwise_and)
            dve.drain()
            dve.reciprocal(igu[:, :, :], pgu[:, :, :])
            dve.tensor_tensor(mprod[:, :], pgu[:, 0, :], pgu[:, 1, :], ALU.mult)
            dve.tensor_scalar(dg[:, :], pgu[:, 0, :], 1.0 / (W_UP * X_UP), None, ALU.mult)
            dve.drain()
            dve.tensor_scalar(mu[:, :], igu[:, 0, :], I_UP / (W_UP * X_UP), None, ALU.mult)
            dve.tensor_reduce(stat[:, 0:1], mprod[:, :], AX.X, ALU.max)
            dve.drain()
            dve.tensor_scalar(igu[:, :, :], igu[:, :, :], W_UP, None, ALU.mult)
            dve.drain()
            dve.tensor_tensor(sgu[:, :, :, :].rearrange("p m c k -> p (m c) k"), sgu[:, :, :, :].rearrange("p m c k -> p (m c) k"),
                              igu[:, :, :].rearrange("p m c -> p (m c)").unsqueeze(2).broadcast_to([P, 2 * NC, 16]),
                              ALU.mult).then_inc(s_stat, 1)
            dve.wait_ge(s_allmax, 1)
            dve.tensor_scalar(stat[:, 2:4], stat[:, 2:4], TINY, None, ALU.max)
            dve.drain()
            dve.tensor_scalar(stat[:, 2:4].bitcast(U32), stat[:, 2:4].bitcast(U32), POW2, None, ALU.bitwise_and)
            dve.drain()
            dve.reciprocal(stat[:, 4:6], stat[:, 2:4])
            dve.tensor_tensor(out_scale[:, :], stat[:, 2:3], stat[:, 3:4], ALU.mult)
            dve.drain()
            dve.tensor_scalar(mprod[:, :], mprod[:, :], stat[:, 4:5], None, ALU.mult)
            dve.tensor_scalar(sd[:, :, :], sd[:, :, :], stat[:, 5:6], W_UP, ALU.mult, ALU.mult)
            dve.drain()
            big = gl[:, :, :].rearrange("p a b -> p (a b)")[:, 0:SG * P // 2]
            dif = sq[:, :, :].rearrange("p a b -> p (a b)")[:, 0:SG * P // 2]
            for h in range(2):
                half = slice(h * SG * P // 2, (h + 1) * SG * P // 2)
                dve.tensor_scalar(big, scales[:, half], 2.0 ** 15 + 1.0, None, ALU.mult)
                dve.drain()
                dve.tensor_tensor(dif, big, scales[:, half], ALU.subtract)
                dve.drain()
                dve.tensor_tensor(shl[:, 0, half], big, dif, ALU.subtract)
                dve.drain()
                dve.tensor_tensor(shl[:, 1, half], scales[:, half], shl[:, 0, half], ALU.subtract)
            dve.drain()
            dve.sem_inc(s_shl, 1)

            def weights(u, n, stores, down):
                dve.drain()
                dve.wait_ge(s_c16, u + (1 + R))
                for r in range(2):
                    c = codes16[:, n % R, :]
                    dve.tensor_scalar(nib[:, r, :], c, 9 - 4 * r, 0x0E00, ALU.logical_shift_left, ALU.bitwise_and)
                    dve.tensor_scalar(nibs[:, r, :], c, 12 - 4 * r, 0x8000, ALU.logical_shift_left, ALU.bitwise_and)
                dve.drain()
                dve.tensor_tensor(nib, nib, nibs, ALU.bitwise_or)
                dve.drain()
                if down is None:
                    dve.tensor_scalar(val16, nib.bitcast(F16), CODE, None, ALU.mult)
                else:
                    for r in range(2):
                        dve.tensor_scalar(val16[:, r, :], nib[:, r, :].bitcast(F16), mprod[:, bass.ds(down + r, 1)], CODE,
                                          ALU.mult, ALU.mult)
                dve.drain()
                dve.wait_ge(s_ss, u + (1 + R))
                dve.wait_ge(s_wst[n % R], stores)
                v = val16.rearrange("p r (k c) -> p k r c", k=4)
                for l in range(2):
                    if down is None:
                        w = whl[:, n % R, l * 1024:(l + 1) * 1024].rearrange("p (k r c) -> p k r c", k=4, r=2)
                    else:
                        w = whl[:, n % R, :].rearrange("p (r l k c) -> p l k r c", r=2, l=2, k=4)[:, l]
                    i = dve.tensor_tensor(w, v, ssb[:, n % R, :, l, :].unsqueeze(2).broadcast_to([P, 4, 2, P]), ALU.mult)
                i.then_inc(s_wf, 1)

            done = 16 + 16 * UG // R
            with dve.Fori(0, UG // 4) as q:
                for n in range(4):
                    weights(4 * q + n, n, q * 32 + (16 + 16 * (n // R)), None)
            with dve.Fori(0, UD // 4) as q:
                for n in range(4):
                    weights(4 * q + (UG + n), n, q * 64 + (done + 32 * (n // R)), 8 * q + 2 * n)

            dve.wait_ge(s_par, NPAR)

            def center(v, n):
                dve.tensor_reduce(hsum[:, 0:n], v, AX.X, ALU.add)
                dve.drain()
                dve.scalar_tensor_tensor(v, hsum[:, 0:n].unsqueeze(2).broadcast_to([P, n, HD]), -1.0 / HD, v,
                                         ALU.mult, ALU.add)
                dve.drain()

            center(wq[:, :, :].rearrange("p k (h d) -> p (k h) d", h=H), KT * H)
            center(bq_b[:, :].rearrange("p (h d) -> p h d", h=H), H)
            for k in range(YT):
                center(wkv[:, k, :].rearrange("p (h w) -> p h w", h=H)[:, :, 0:HD], H)
                center(wdca[:, k, 0:D].rearrange("p (h d) -> p h d", h=H), H)
            for kind in range(2):
                center(bkv_b[:, kind, :].rearrange("p (h w) -> p h w", h=H)[:, :, 0:HD], H)

            dve.tensor_reduce(qk_p2[:, 0:1], qwb[:, :, :].rearrange("p a d -> p (a d)"), AX.X, ALU.max,
                              apply_absolute_value=True)
            dve.tensor_reduce(qk_p2[:, 1:2], kall[:, :, :].rearrange("p a d -> p (a d)"), AX.X, ALU.max,
                              apply_absolute_value=True)
            dve.drain()
            dve.tensor_scalar(qk_p2[:, 0:2], qk_p2[:, 0:2], TINY, None, ALU.max)
            dve.drain()
            dve.tensor_scalar(qk_p2[:, 0:2].bitcast(U32), qk_p2[:, 0:2].bitcast(U32), POW2, None, ALU.bitwise_and)
            dve.drain()
            dve.reciprocal(qk_p2[:, 2:4], qk_p2[:, 0:2])
            dve.scalar_tensor_tensor(exp_scale[:, :], qk_p2[:, 0:1], SCALE, qk_p2[:, 1:2], ALU.mult, ALU.mult)
            dve.drain()
            dve.tensor_scalar(qwb[:, :, :], qwb[:, :, :], qk_p2[:, 2:3], None, ALU.mult)
            dve.tensor_scalar(kwb[:, :, :, :].rearrange("p a b d -> p (a b d)"),
                              kwb[:, :, :, :].rearrange("p a b d -> p (a b d)"), qk_p2[:, 3:4], None, ALU.mult)
            dve.drain()
            dve.tensor_scalar(qwb[:, 0, :], qwb[:, 0, :], HD ** 0.5, None, ALU.mult)
            for kind in range(2):
                dve.tensor_scalar(kwb[:, kind, 0, :], kwb[:, kind, 0, :], HD ** 0.5, None, ALU.mult)
            for tt in range(TT):
                kind = tt // (TT - 1)
                dve.tensor_copy(cat[:, tt, :, QW:KW], kmask[:, kind, :].unsqueeze(1).broadcast_to([P, H, 2]))
                dve.tensor_copy(vv[:, tt, :, VW - 1:VW], kmask[:, kind, 0:1].unsqueeze(1).broadcast_to([P, H, 1]))
            dve.tensor_copy(vd[:, :, VW - 1:VW], kmask[:, 1, 1:2].unsqueeze(1).broadcast_to([P, H, 1]))
            dve.wait_ge(s_tanh, 1)
            dve.tensor_scalar(bo_b[:, :], bo_b[:, :], tgates[:, 0:1], None, ALU.mult)
            dve.tensor_scalar(out_scale[:, :], out_scale[:, :], tgates[:, 1:2], None, ALU.mult)
            dve.drain()


            def first_norm(b):
                dve.wait_ge(s_xl, b * 16 + 16)
                for tt in range(TT):
                    dve.bn_stats(bst[:, tt, :], xn[:, tt, :])
                dve.drain()
                for tt in range(TT):
                    dve.bn_aggr(mv[:, tt, :], bst[:, tt, :])
                dve.drain()
                dve.tensor_scalar(rstd[:, :], mv[:, :, 1], EPS_X, None, ALU.add).then_inc(s_var, 1)
                dve.wait_ge(s_rstd, b * NV + 1)
                for tt in range(TT):
                    dve.tensor_scalar(xn[:, tt, :], xn[:, tt, :], mv[:, tt, 0:1], rstd[:, tt:tt + 1],
                                      ALU.subtract, ALU.mult).then_inc(s_xn, 1)

            first_norm(0)

            def batch(b, last):
                def head_roots(v):
                    dve.tensor_scalar(nv[:, 0, :], v, HD * EPS_H, None, ALU.add)
                    dve.drain()
                    dve.tensor_scalar(nv[:, 1, :].bitcast(I32), nv[:, 0, :].bitcast(I32), 1, None, ALU.logical_shift_right)
                    dve.tensor_scalar(nv[:, 0, :], nv[:, 0, :], -0.5, None, ALU.mult)
                    dve.drain()
                    dve.tensor_scalar(v.bitcast(I32), nv[:, 1, :].bitcast(I32), -1.0, ROOT, ALU.mult, ALU.add)
                    dve.drain()
                    for _ in range(3):
                        dve.tensor_tensor(nv[:, 1, :], v, v, ALU.mult)
                        dve.drain()
                        dve.tensor_tensor(nv[:, 1, :], nv[:, 1, :], nv[:, 0, :], ALU.mult)
                        dve.drain()
                        dve.scalar_tensor_tensor(v, nv[:, 1, :], 1.5, v, ALU.add, ALU.mult)
                        dve.drain()

                def head_sums(i):
                    a, tt = i // TT, i % TT
                    dve.wait_ge(s_sq, b * (2 * TT) + (i + 1))
                    dve.tensor_reduce(hrs[:, a, tt, :], sq[:, i % R, :].rearrange("p (h d) -> p h d", h=H), AX.X, ALU.add)
                    if tt == TT - 1:
                        dve.drain()
                        head_roots(hrs[:, a, :, :].rearrange("p t h -> p (t h)"))

                def split_values(dst, src):
                    dve.tensor_copy(dst[:, :, 0:HD], src)
                    dve.drain()
                    dve.tensor_tensor(src, src, dst[:, :, 0:HD], ALU.subtract)
                    dve.drain()
                    dve.tensor_copy(dst[:, :, HD:2 * HD], src)
                    dve.drain()
                    return dve.tensor_tensor(dst[:, :, 2 * HD:3 * HD], src, dst[:, :, HD:2 * HD], ALU.subtract)

                def keys_values(tt):
                    kind = tt // (TT - 1)
                    dve.drain()
                    for e in range(2):
                        dve.wait_ge(sa_full, b * SA_N + (SA_KV + 2 * tt + e + 1))
                        src = ringA[:, e, :].rearrange("p (h w) -> p h w", h=H // 2)
                        bias = bkv_b[:, kind, e * D:(e + 1) * D].rearrange("p (h w) -> p h w", h=H // 2)
                        half = slice(e * D // 2, (e + 1) * D // 2)
                        i = dve.tensor_tensor(cen[:, 1, tt, half].rearrange("p (h d) -> p h d", d=HD), src[:, :, 0:HD],
                                              bias[:, :, 0:HD], ALU.add)
                        if e == 1:
                            i.then_inc(s_cen, 1)
                        dve.tensor_tensor(val[:, half].rearrange("p (h d) -> p h d", d=HD), src[:, :, HD:2 * HD],
                                          bias[:, :, HD:2 * HD], ALU.add).then_inc(sa_free, 1)
                    dve.drain()
                    v = val[:, :].rearrange("p (h d) -> p h d", h=H)
                    if kind:
                        v2 = vald[:, :].rearrange("p (h d) -> p h d", h=H)
                        dve.tensor_scalar(v2, v, kmask[:, 1, 1:2], None, ALU.mult)
                        dve.drain()
                        dve.tensor_scalar(v, v, kmask[:, 1, 0:1], None, ALU.mult)
                        dve.drain()
                        split_values(vd, v2)
                    i = split_values(vv[:, tt, :, :], v)
                    if kind:
                        i.then_inc(s_v, 1)
                    head_sums(TT + tt)

                def low(a, tt):
                    c = cen[:, a, tt, :].rearrange("p (h d) -> p h d", h=H)
                    lo = 2 - a
                    dve.wait_ge(s_cat, b * (2 * TT) + (a * TT + tt + 1))
                    dve.tensor_tensor(cat[:, tt, :, lo * HD:(lo + 1) * HD], c, cat[:, tt, :, 0:HD],
                                      ALU.subtract).then_inc(s_hl, 1)

                def norm(a):
                    for tt in range(TT):
                        w = qwb if a == 0 else kwb[:, tt // (TT - 1), :, :]
                        c = cen[:, a, tt, :].rearrange("p (h d) -> p h d", h=H)
                        dve.tensor_tensor(c, c, hrs[:, a, tt, :].unsqueeze(2).broadcast_to([P, H, HD]), ALU.mult)
                        dve.drain()
                        dve.tensor_tensor(c, c, w[:, 0, :].unsqueeze(1).broadcast_to([P, H, HD]), ALU.mult)
                        dve.drain()
                        dve.tensor_tensor(c, c, w[:, 1, :].unsqueeze(1).broadcast_to([P, H, HD]), ALU.add).then_inc(s_hn, 1)
                        if tt:
                            low(a, tt - 1)
                    low(a, TT - 1)

                for tt in range(TT):
                    dve.wait_ge(sa_full, b * SA_N + (SA_Q + tt + 1))
                    dve.tensor_tensor(cen[:, 0, tt, :], ringA[:, tt % R, :], bq_b[:, :], ALU.add).then_inc(sa_free, 1)
                    dve.drain()
                    dve.sem_inc(s_cen, 1)
                    if tt:
                        head_sums(tt - 1)
                head_sums(TT - 1)
                keys_values(0)
                norm(0)
                for tt in range(1, TT):
                    keys_values(tt)
                norm(1)

                def maxima(h, n):
                    dve.drain()
                    for tt in range(TT):
                        dve.wait_ge(sa_full, b * SA_N + h * TT + (SA_A + tt + 1))
                        dve.tensor_reduce(pmx[:, tt, :], ringA[:, tt % R, :].rearrange("p (g k) -> p g k", k=DCA),
                                          AX.X, ALU.max).then_inc(sa_free, 1)
                    dve.drain()
                    dve.wait_ge(tp_full, b * TP_N + h + (TP_M - 1))
                    dve.tensor_reduce(mneg[:, n, :, 0], pmx[:, :, 0:SM // DCA], AX.X, ALU.max, negate=True)
                    dve.tensor_scalar(mneg[:, n, :, 1], pmx[:, :, SM // DCA], -1.0, None, ALU.mult).then_inc(s_mneg, 1)

                def lows(h, n):
                    for j in range(TT // 2):
                        dve.wait_ge(sb_free, b * SB_N + h * TT + (2 * j + 2 + R))
                        dve.tensor_tensor(phl[:, n, 1, 2 * j:2 * j + 2, :], pf[:, 2 * j:2 * j + 2, :],
                                          phl[:, n, 0, 2 * j:2 * j + 2, :], ALU.subtract).then_inc(s_pl, 1)

                def head_out(h, n):
                    dve.drain()
                    dve.wait_ge(s_pv, b * H + h + (1 + R))
                    o = ringO[:, :, 0:TT * VW].rearrange("p a (t w) -> p a t w", t=TT)
                    for a in range(2):
                        dve.tensor_reduce(osum[:, a, :, :], o[:, a, :, 0:3 * HD].rearrange("p t (w d) -> p t d w", w=3),
                                          AX.X, ALU.add)
                    dve.reciprocal(orec[:, :, :], o[:, :, :, VW - 1]).then_inc(s_of, 1)
                    dve.drain()
                    dve.tensor_tensor(osum[:, :, :, :].rearrange("p a t d -> p (a t) d"),
                                      osum[:, :, :, :].rearrange("p a t d -> p (a t) d"),
                                      orec[:, :, :].rearrange("p a t -> p (a t)").unsqueeze(2).broadcast_to([P, 2 * TT, HD]),
                                      ALU.mult)
                    dve.drain()
                    dve.tensor_tensor(xn[:, :, bass.ds(h * HD, HD)], osum[:, 0, :, :], osum[:, 1, :, :],
                                      ALU.add).then_inc(s_ctx, 1)

                maxima(0, 0)
                maxima(1, 1)
                lows(0, 0)
                maxima(2, 0)
                lows(1, 1)
                maxima(3, 1)
                head_out(0, 0)
                lows(2, 0)
                with dve.Fori(0, (H - 4) // 2) as q:
                    for n in range(2):
                        h = 2 * q + (n + 3)
                        maxima(h + 1, n)
                        head_out(h - 2, 1 - n)
                        lows(h, 1 - n)
                head_out(H - 3, 1)
                lows(H - 1, 1)
                head_out(H - 2, 0)
                head_out(H - 1, 1)

                dve.wait_ge(s_x, b * 16 + 16)
                for tt in range(TT):
                    dve.tensor_tensor(x_sb[:, tt, :], x_sb[:, tt, :], bo_b[:, :], ALU.add)

                def split(tt):
                    dve.wait_ge(s_rstd, b * NV + (2 + tt))
                    dve.tensor_scalar(xn[:, tt, :], x_sb[:, tt, :], mv[:, tt, 0:1], rstd[:, tt:tt + 1],
                                      ALU.subtract, ALU.mult)
                    dve.drain()
                    if tt >= R:
                        dve.wait_ge(tp_full, b * TP_N + (TP_L + 2 * (tt - R) + 2))
                    dve.tensor_copy(xhl[:, tt % R, 0, :], xn[:, tt, :])
                    dve.drain()
                    dve.tensor_tensor(xhl[:, tt % R, 1, :], xn[:, tt, :], xhl[:, tt % R, 0, :],
                                      ALU.subtract).then_inc(s_l2, 1)

                for tt in range(TT):
                    dve.drain()
                    dve.wait_ge(sa_full, b * SA_N + (SA_O + tt + 1))
                    dve.scalar_tensor_tensor(x_sb[:, tt, :], ringA[:, tt % R, :], tgates[:, 0:1], x_sb[:, tt, :],
                                             ALU.mult, ALU.add).then_inc(sa_free, 1)
                    dve.drain()
                    dve.bn_stats(bst[:, tt, :], x_sb[:, tt, :])
                    dve.drain()
                    dve.bn_aggr(mv[:, tt, :], bst[:, tt, :])
                    dve.drain()
                    dve.tensor_scalar(rstd[:, tt:tt + 1], mv[:, tt, 1:2], X_UP ** -2, EPS_X * X_UP ** -2, ALU.mult,
                                      ALU.add).then_inc(s_var, 1)
                    if tt:
                        split(tt - 1)
                split(TT - 1)
                with dve.Fori(0, NC // 2) as q:
                    for n in range(2):
                        dve.wait_ge(sa_full, b * SA_N + q * 2 + (SA_U + n + 1))
                        dve.wait_ge(sb_free, b * SB_N + q * 2 + (SB_G + n + 1 + R))
                        dve.wait_ge(s_il, b * NC + q * 2 + (n + 1))
                        dve.scalar_tensor_tensor(it[:, n, :], ringA[:, n, :], mu[:, bass.ds(q * 2 + n, 1)], gl[:, n, :],
                                                 ALU.mult, ALU.mult).then_inc(sa_free, 1)
                if not last:
                    first_norm(b + 1)
                dve.wait_ge(s_dn, b + 1)
                for i, tt in enumerate(OST):
                    dve.wait_ge(s_out[i % R], b * (16 * TT // R) + (16 + 16 * (i // R)))
                    dve.scalar_tensor_tensor(ost[:, i % R, :], acc(tt), out_scale[:, 0:1], x_sb[:, tt, :],
                                             ALU.mult, ALU.add).then_inc(s_ost, 1)

            with dve.Fori(0, B - 1) as b:
                batch(b, False)
            batch(B - 1, True)


_INS = ['x', 'ctx_1024', 'g_xattn', 'g_ffn'] + ['L0_xattn_' + n for n in (
    'Wq', 'bq', 'Wk', 'bk', 'Wv', 'bv', 'Wkv_dca', 'bkv_dca', 'qn_w', 'qn_b', 'kn_w', 'kn_b', 'kn_dca_w', 'kn_dca_b',
    'Wo', 'bo')] + ['L0_ffn_' + n for n in (
        'gate_W_packed', 'gate_scales', 'up_W_packed', 'up_scales', 'down_W_packed', 'down_scales')]
_OUTS = [((B, S, D), 'float32')]


def kernel(**inputs):
    import numpy as _np
    import concourse.bacc as _bacc
    from concourse import mybir as _mybir
    from concourse.bass_utils import run_bass_kernel_spmd as _run

    nc = _bacc.Bacc("TRN2", target_bir_lowering=False, num_devices=1)
    arrays, args = {}, []
    for name in _INS:
        a = _np.ascontiguousarray(inputs[name])
        arrays[f"in_{name}_dram"] = a
        args.append(nc.dram_tensor(f"in_{name}_dram", a.shape, _mybir.dt.from_np(a.dtype), kind="ExternalInput").ap())
    for i, (shape, dtype) in enumerate(_OUTS):
        dt = _mybir.dt.from_np(_np.dtype(dtype))
        args.append(nc.dram_tensor(f"out_{i}_dram", shape, dt, kind="ExternalOutput").ap())
    block_kernel(nc, *args)
    r = _run(nc, [arrays], core_ids=[0])
    return r.results[0]["out_0_dram"]
```

```python
from contextlib import ExitStack

import concourse.bass as bass
from concourse import mybir

F32 = mybir.dt.float32
F16 = mybir.dt.float16
BF16 = mybir.dt.bfloat16
I32 = mybir.dt.int32
U32 = mybir.dt.uint32
U16 = mybir.dt.uint16
U8 = mybir.dt.uint8
ALU = mybir.AluOpType
ACT = mybir.ActivationFunctionType
AX = mybir.AxisListType

P = 128
B, S, D = 4, 512, 512
H, HD = 16, 32
KD, DCA = 256, 16
SM = S - DCA
F = 4096
TT = S // P
KT = D // P
YT = KD // P
NC = F // P
LASTM = SM - (TT - 1) * P
VW = 3 * HD + 1
QW = 3 * HD
KW = QW + 2
EPS_X, EPS_H = 1e-5, 1e-6
SCALE = HD ** -0.5
R = 2
GU = 2 * 2 * KT * P
WCH = GU + 2 * D
GR = NC * 16 // P
SG = 2 * GR + TT
UG, UD = NC, NC // 2
POW2 = 0x7F800000
TINY = 2.0 ** -40
W_UP = 2.0 ** 10
X_UP = 2.0 ** 8
I_UP = 2.0 ** -10
CODE = 2.0 ** 14

PR = TT
NV = 1 + TT // 2
ROOT = 1597463007.0
OST = (0, 2, 3, 1)

CH_Y, CH_X = 0, TT
CH_KV = 2
CH_Q = CH_KV + 2 * TT
CH_TK = CH_Q + TT + 1
CH_TQ = NC - H // 2
PT_Y, PT_X, PT_K, PT_Q = 0, TT, 2 * TT, 2 * TT + H // 2
PT_N = PT_Q + H // 2
PP_KV, PP_Q = 0, 2 * TT
PP_N = PP_Q + TT
TP_M = 0
TP_C = TP_M + H
TP_L = TP_C + TT
TP_N = TP_L + 2 * TT
SA_A = 0
SA_O = SA_A + TT * H
SA_N = SA_O + R
SB_O = TT * H
SB_N = SB_O + TT - R


def block_kernel(nc, x, ctx, g_xattn, g_ffn, Wq, bq, Wk, bk, Wv, bv, Wkv_dca, bkv_dca, qn_w, qn_b,
                 kn_w, kn_b, knd_w, knd_b, Wo, bo, gW, gS, uW, uS, dW, dS, out):
    wscratch = nc.dram_tensor("wscratch", [NC, P, WCH], F16, kind="Internal").ap()
    with ExitStack() as stack:
        def sb(name, shape, dt):
            return stack.enter_context(nc.sbuf_tensor(name, shape, dt))

        def psum(name, shape, dt):
            return stack.enter_context(nc.psum_tensor(name, shape, dt))

        def sem(name):
            return stack.enter_context(nc.semaphore(name))

        ident = sb("ident", [P, P], F32)
        ident16 = sb("ident16", [P, P], F16)
        identb = sb("identb", [P, P], BF16)
        wq = sb("wq", [P, KT, D], F32)
        wkv = sb("wkv", [P, YT, 2 * D], F32)
        wdca = sb("wdca", [P, YT, 2 * D], F32)
        wo = sb("wo", [P, KT, D], F32)
        bq_b = sb("bq_b", [P, D], F32)
        bkv_b = sb("bkv_b", [P, 2, 2 * D], F32)
        bo_b = sb("bo_b", [P, D], F32)
        qwb = sb("qwb", [P, 2, HD], F32)
        kwb = sb("kwb", [P, 2, 2, HD], F32)
        kall = sb("kall", [P, 4, HD], F32)
        gates = sb("gates", [P, 2], F32)
        tgates = sb("tgates", [P, 2], F32)
        kmask = sb("kmask", [P, 2, 2], F32)
        mhalf = sb("mhalf", [P, TT], F32)
        qk_p2 = sb("qk_p2", [P, 4], F32)
        exp_scale = sb("exp_scale", [P, 1], F32)
        dg = sb("dg", [P, NC], F32)
        mu = sb("mu", [P, NC], F32)
        out_scale = sb("out_scale", [P, 1], F32)
        xT = sb("xT", [P, 2, KT, S], F16)
        scales = xT[:, :, :, :].rearrange("p l k t -> p (l k t)").bitcast(F32)[:, 0:SG * P]
        sgu = scales[:, 0:2 * NC * 16].rearrange("p (m c k) -> p m c k", m=2, k=16)
        sd = scales[:, 2 * NC * 16:SG * P].rearrange("p (t k) -> p t k", t=TT)
        pgu = sb("pgu", [P, 2, NC], F32)
        igu = sb("igu", [P, 2, NC], F32)
        mprod = sb("mprod", [P, NC], F32)
        stat = sb("stat", [P, 8], F32)
        x_sb = sb("x_sb", [P, TT, D], F32)
        xn = sb("xn", [P, TT, D], F32)
        bst = sb("bst", [P, TT, 6], F32)
        mv = sb("mv", [P, TT, 2], F32)
        rstd = sb("rstd", [P, TT], F32)
        y_sb = sb("y_sb", [P, TT, KD], F32)
        yT = sb("yT", [P, YT, S], F32)
        yTd = sb("yTd", [P, YT, P], F32)
        xnT = sb("xnT", [P, KT, S], F32)
        val = sb("val", [P, D], F32)
        vald = sb("vald", [P, D], F32)
        sq = sb("sq", [P, R, D], F32)
        hsum = sb("hsum", [P, KT * H], F32)
        nv = sb("nv", [P, 2, TT * H], F32)
        hrs = sb("hrs", [P, 2, TT, H], F32)
        cat = sb("cat", [P, TT, H, KW], F16)
        qkT = sb("qkT", [P, 2, H, S], F16)
        vv = sb("vv", [P, TT, H, VW], BF16)
        vd = sb("vd", [P, H, VW], BF16)
        pmx = sb("pmx", [P, TT, S // DCA], F32)
        mneg = sb("mneg", [P, R, TT, 2], F16)
        pf = sb("pf", [P, PR, S], F32)
        phl = sb("phl", [P, R, 2, TT, S], F16)
        osum = sb("osum", [P, 2, TT, HD], F32)
        odiv = sb("odiv", [P, 2, TT, HD], F32)
        orec = sb("orec", [P, 2, TT], F32)
        gl = sb("gl", [P, R, S], F32)
        it = sb("it", [P, R, S], F32)
        ihl = sb("ihl", [P, R, 2, S], F16)
        wgu = sb("wgu", [P, R, GU], F16)
        wdn = sb("wdn", [P, R, 2 * D], F16)

        qT, kT = qkT[:, 0, :, :], qkT[:, 1, :, :]
        xhl = ihl
        cen = phl[:, :, :, :, :].rearrange("p r l k t -> p (r l k t)").bitcast(F32).rearrange(
            "p (a t d) -> p a t d", a=2, t=TT)
        codes = phl[:, 0, :, :, :].rearrange("p l k t -> p (l k t)").bitcast(I32).rearrange(
            "p (s k c) -> p s k c", s=4, k=4)
        codesb = phl[:, 1, 0, 0:2, :].bitcast(BF16)
        codes16 = phl[:, 1, 0, 2:4, :].bitcast(U16)
        nib = it[:, :, :].rearrange("p s n -> p (s n)").bitcast(U16).rearrange("p (s r c) -> p s r c", s=R, r=2)
        nibs = phl[:, 1, 1, :, :].rearrange("p k t -> p (k t)").bitcast(U16).rearrange("p (s r c) -> p s r c", s=R, r=2)
        val16 = pf[:, R:PR, :].rearrange("p s n -> p (s n)").bitcast(F16).rearrange("p (s r c) -> p s r c", s=R, r=2)
        ssb = pf[:, 0:R, :].rearrange("p s n -> p (s n)").bitcast(F16).rearrange("p (s k l c) -> p s k l c", s=R, k=4, l=2)
        free16 = qkT[:, :, :, :].rearrange("p a h t -> p (a h t)")
        spread = free16[:, 0:16 * P].rearrange("p (j c) -> p j c", j=16)
        shl = free16[:, 16 * P:16 * P + 2 * SG * P].rearrange("p (l n) -> p l n", l=2)
        sT = free16[:, 16 * P + 2 * SG * P:16 * P + 4 * SG * P].rearrange("p (g l c) -> p g l c", g=SG, l=2)
        whl = xnT[:, :, :].rearrange("p k t -> p (k t)").bitcast(F16).rearrange("p (s n) -> p s n", s=R)

        ringA = psum("ringA", [P, R, 512], F32)
        ringB = psum("ringB", [P, R, 512], F32)
        ringO = psum("ringO", [P, R, 512], F32)
        ringT = psum("ringT", [P, R, 512], F32)
        ringT16 = ringT[:, :, :].bitcast(F16)

        def alone(b):
            return isinstance(b, int) and b == 0

        def turn32(b, i):
            return ringT[:, 0, :] if alone(b) and i % 2 else ringA[:, 1, :]

        def turn16(b, i):
            return turn32(b, i).bitcast(F16)

        def projected(b, i):
            return ringT[:, 1, :] if alone(b) and i % 2 else ringA[:, 0, :]

        def unit_free(b, i):
            return max(i, 1) if alone(b) else i + 1

        ringOb = ringO[:, :, :].bitcast(BF16)

        s_init = sem("s_init")
        s_par = sem("s_par")
        s_scales = sem("s_scales")
        s_stat = sem("s_stat")
        s_allmax = sem("s_allmax")
        s_tanh = sem("s_tanh")
        s_code = [sem(f"s_code{i}") for i in range(4)]
        s_cb = sem("s_cb")
        s_shl = sem("s_shl")
        s_st = sem("s_st")
        s_stc = sem("s_stc")
        s_ct = sem("s_ct")
        s_c16 = sem("s_c16")
        s_ss = sem("s_ss")
        s_nib = sem("s_nib")
        s_val = sem("s_val")
        s_wf = sem("s_wf")
        s_wst = [sem(f"s_wst{i}") for i in range(R)]
        s_x = sem("s_x")
        s_xl = sem("s_xl")
        s_y = sem("s_y")
        s_var = sem("s_var")
        s_rstd = sem("s_rstd")
        s_wc = sem("s_wc")
        s_xn = sem("s_xn")
        pt_full, pt_free = sem("pt_full"), sem("pt_free")
        pp_full, pp_free = sem("pp_full"), sem("pp_free")
        tp_full, tp_free = sem("tp_full"), sem("tp_free")
        sa_full, sa_free = sem("sa_full"), sem("sa_free")
        sb_full, sb_free = sem("sb_full"), sem("sb_free")
        s_cen = sem("s_cen")
        s_sq = sem("s_sq")
        s_hn = sem("s_hn")
        s_cat = sem("s_cat")
        s_hl = sem("s_hl")
        s_v = sem("s_v")
        s_mneg = sem("s_mneg")
        s_pl = [sem("s_pl_pool"), sem("s_pl_dve")]
        s_pv = sem("s_pv")
        s_of = sem("s_of")
        s_ctx = sem("s_ctx")
        s_l2n = sem("s_l2n")
        s_l2h = sem("s_l2h")
        s_l2 = sem("s_l2")
        s_loadg = [sem(f"s_loadg{i}") for i in range(R)]
        s_loadd = [sem(f"s_loadd{i}") for i in range(R)]
        s_wused = sem("s_wused")
        g_full, g_free = sem("g_full"), sem("g_free")
        u_full = sem("u_full")
        s_it = sem("s_it")
        s_ih = sem("s_ih")
        s_il = sem("s_il")
        s_dn = sem("s_dn")
        s_ost = sem("s_ost")
        s_out = sem("s_out")

        def turn_bank(i):
            return (ringO[:, 0, :], ringO[:, 1, :], ringA[:, 0, :])[i].bitcast(F16)

        def spread_ring(n):
            return (ringB, ringT)[n % R][:, :, :]

        def acc(tt):
            return ringO[:, tt, :] if tt < R else ringT[:, tt - R, :]

        params = [
            (wq[:, :, :], Wq.rearrange("(k p) n -> p k n", p=P)),
            (wkv[:, :, 0:D], Wk.rearrange("(k p) n -> p k n", p=P)),
            (wkv[:, :, D:2 * D], Wv.rearrange("(k p) n -> p k n", p=P)),
            (wdca[:, :, :], Wkv_dca.rearrange("(k p) n -> p k n", p=P)),
            (wo[:, :, :], Wo.rearrange("(k p) n -> p k n", p=P)),
            (bq_b[:, :], bq.partition_broadcast(P)),
            (bo_b[:, :], bo.partition_broadcast(P)),
            (bkv_b[:, 0, 0:D], bk.partition_broadcast(P)),
            (bkv_b[:, 0, D:2 * D], bv.partition_broadcast(P)),
            (bkv_b[0:LASTM, 1, 0:D], bk.partition_broadcast(LASTM)),
            (bkv_b[0:LASTM, 1, D:2 * D], bv.partition_broadcast(LASTM)),
            (bkv_b[LASTM:P, 1, :].rearrange("p (h a d) -> p a h d", h=H, a=2)[:, 0],
             bkv_dca[0:D].rearrange("(h d) -> h d", h=H).partition_broadcast(DCA)),
            (bkv_b[LASTM:P, 1, :].rearrange("p (h a d) -> p a h d", h=H, a=2)[:, 1],
             bkv_dca[D:2 * D].rearrange("(h d) -> h d", h=H).partition_broadcast(DCA)),
            (qwb[:, 0, :], qn_w.partition_broadcast(P)),
            (qwb[:, 1, :], qn_b.partition_broadcast(P)),
            (kwb[:, 0, 0, :], kn_w.partition_broadcast(P)),
            (kwb[:, 0, 1, :], kn_b.partition_broadcast(P)),
            (kwb[0:LASTM, 1, 0, :], kn_w.partition_broadcast(LASTM)),
            (kwb[0:LASTM, 1, 1, :], kn_b.partition_broadcast(LASTM)),
            (kwb[LASTM:P, 1, 0, :], knd_w.partition_broadcast(DCA)),
            (kwb[LASTM:P, 1, 1, :], knd_b.partition_broadcast(DCA)),
            (kall[:, 0, :], kn_w.partition_broadcast(P)),
            (kall[:, 1, :], kn_b.partition_broadcast(P)),
            (kall[:, 2, :], knd_w.partition_broadcast(P)),
            (kall[:, 3, :], knd_b.partition_broadcast(P)),
            (gates[:, 0:1], g_xattn.partition_broadcast(P)),
            (gates[:, 1:2], g_ffn.partition_broadcast(P)),
        ]
        NPAR = 16 * len(params)

        block = stack.enter_context(nc.Block())

        @block.sync
        def _(sp):
            for n in range(R):
                sp.sem_inc(s_wst[n], 16)
            for m, sc in enumerate((gS, uS)):
                sp.dma_start(sgu[:, m, :, :].rearrange("p (j r) k -> p j (r k)", r=2),
                             sc.rearrange("(j p r) k -> p j (r k)", p=P, r=2)).then_inc(s_scales, 16)
            sp.dma_start(sd[:, :, :], dS.rearrange("(t p) k -> p t k", p=P)).then_inc(s_scales, 16)

            gWv = gW.rearrange("(j p r) k -> j r p k", p=P, r=2)
            uWv = uW.rearrange("(j p r) k -> j r p k", p=P, r=2)
            dWv = dW.rearrange("(t p) (j c) -> j p t c", p=P, j=UD)

            def codes_gu(j, r, slot):
                sp.dma_start(codes[:, slot, 0:2, :].rearrange("p k c -> p (k c)"), gWv[j, r]).then_inc(s_code[slot], 16)
                sp.dma_start(codes[:, slot, 2:4, :].rearrange("p k c -> p (k c)"), uWv[j, r]).then_inc(s_code[slot], 16)

            def codes_d(j, slot):
                sp.dma_start(codes[:, slot, 0:2, :], dWv[j][:, 0:2]).then_inc(s_code[slot], 16)
                sp.dma_start(codes[:, slot, 2:4, :], dWv[j][:, 2:4]).then_inc(s_code[slot], 16)

            for n in range(4):
                codes_gu(n // 2, n % 2, n)
            for dst, src in params:
                sp.dma_start(dst, src).then_inc(s_par, 16)
            sp.dma_start(xn[:, :, :], x[0].rearrange("(t p) d -> p t d", p=P)).then_inc(s_xl, 16)
            sp.dma_start(x_sb[:, :, :], x[0].rearrange("(t p) d -> p t d", p=P)).then_inc(s_x, 16)
            sp.dma_start(y_sb[:, :, :], ctx[0].rearrange("(t p) d -> p t d", p=P)).then_inc(s_y, 16)

            def store_gu(c, u, n):
                sp.wait_ge(s_wf, u + (1 + R))
                sp.dma_start(wscratch[c][:, 0:GU], whl[:, n % R, :]).then_inc(s_wst[n % R], 16)

            with sp.Fori(0, UG // 4 - 1) as q:
                for n in range(4):
                    sp.wait_ge(s_cb, 4 * q + (n + 1))
                    codes_gu(2 * q + (2 + n // 2), n % 2, n)
                    store_gu(4 * q + n, 4 * q + n, n)
            for n in range(4):
                sp.wait_ge(s_cb, UG - 4 + n + 1)
                codes_d(n, n)
                store_gu(UG - 4 + n, UG - 4 + n, n)

            def store_d(j, u, n):
                sp.wait_ge(s_wf, u + (1 + R))
                for r in range(2):
                    sp.dma_start(wscratch[2 * j + r][:, GU:WCH], whl[:, n % R, r * 2 * D:(r + 1) * 2 * D]).then_inc(
                        s_wst[n % R], 16)

            with sp.Fori(0, UD // 4 - 1) as q:
                for n in range(4):
                    sp.wait_ge(s_cb, 4 * q + (UG + n + 1))
                    codes_d(4 * q + (4 + n), n)
                    store_d(4 * q + n, 4 * q + (UG + n), n)
            for n in range(4):
                store_d(UD - 4 + n, UG + UD - 4 + n, n)
            for n in range(R):
                sp.wait_ge(s_wst[n], 16 + 16 * UG // R + 32 * UD // R)

            def weights(b, c, q, n):
                sp.wait_ge(u_full, b * NC + R * q + (n + 1))
                sp.dma_start(wgu[:, n, :], wscratch[c][:, 0:GU]).then_inc(s_loadg[n], 16)
                sp.wait_ge(s_wused, b * NC + R * q + (n + 1))
                sp.dma_start(wdn[:, n, :], wscratch[c][:, GU:WCH]).then_inc(s_loadd[n], 16)

            def batch(b, last):
                stored = None if last else sp.snap(b * (16 * TT) + 16 * TT)
                if not last:
                    sp.wait_ge(pt_full, b * PT_N + TT)
                    sp.dma_start(y_sb[:, :, :], ctx[b + 1].rearrange("(t p) d -> p t d", p=P)).then_inc(s_y, 16)
                for n in range(R):
                    weights(b, n, 0, n)
                if not last:
                    sp.wait_ge(s_l2, b * TT + TT)
                    sp.dma_start(xn[:, :, :], x[b + 1].rearrange("(t p) d -> p t d", p=P)).then_inc(s_xl, 16)
                with sp.Fori(1, NC // R) as q:
                    for n in range(R):
                        weights(b, q * R + n, q, n)
                for i, tt in enumerate(OST):
                    sp.wait_ge(s_ost, b * TT + (i + R + 1))
                    sp.dma_start(out[b, tt * P:(tt + 1) * P, :], x_sb[:, tt, :]).then_inc(s_out, 16)
                if not last:
                    sp.wait_ge(s_out, stored)
                    sp.dma_start(x_sb[:, :, :], x[b + 1].rearrange("(t p) d -> p t d", p=P)).then_inc(s_x, 16)

            with sp.Fori(0, B - 1) as b:
                batch(b, False)
            batch(B - 1, True)
            sp.wait_ge(s_out, 16 * B * TT)

        @block.gpsimd
        def _(pool):
            for m in (ident, ident16, identb):
                pool.memset(m[:, :], 0.0)
            pool.memset(mhalf[:, :], -0.5)
            pool.memset(kmask[:, :, :], 0.0)
            pool.memset(yTd[:, :, :], 0.0)
            pool.memset(yT[:, :, SM:S], 0.0)
            pool.drain()
            for m in (ident, ident16, identb):
                pool.affine_select(out=m[:, :], in_=m[:, :], compare_op=ALU.not_equal, fill=1.0,
                                   base=0, pattern=[[-1, P]], channel_multiplier=1)
            pool.memset(kmask[:, 0, 0:1], 1.0)
            pool.affine_select(out=kmask[:, 1, 0:1], in_=kmask[:, 1, 0:1], compare_op=ALU.is_ge, fill=1.0,
                               base=-LASTM, pattern=[[0, 1]], channel_multiplier=1)
            pool.affine_select(out=kmask[:, 1, 1:2], in_=kmask[:, 1, 1:2], compare_op=ALU.is_gt, fill=1.0,
                               base=LASTM, pattern=[[0, 1]], channel_multiplier=-1)
            pool.memset(spread, 1.0)
            pool.drain()
            pool.affine_select(out=spread, in_=spread, compare_op=ALU.is_ge, fill=0.0,
                               base=0, pattern=[[P, 16], [1, P]], channel_multiplier=-16)
            pool.drain()
            pool.affine_select(out=spread, in_=spread, compare_op=ALU.is_ge, fill=0.0,
                               base=15, pattern=[[-P, 16], [-1, P]], channel_multiplier=16)
            pool.drain()
            pool.memset(stat[:, 6:8], 0.0).then_inc(s_init, 1)
            pool.sem_inc(s_il, R)
            pool.wait_ge(s_stat, 1)
            pool.partition_all_reduce(stat[:, 2:4], stat[:, 0:2], P, bass.bass_isa.ReduceOp.max).then_inc(s_allmax, 1)
            def inverse_root(v, n, count):
                pool.wait_ge(s_var, count)
                pool.tensor_tensor(v, v, mhalf[:, 0:n], ALU.pow).then_inc(s_rstd, 1)

            pool.sem_inc(s_pl[0], 1)
            inverse_root(rstd[:, :], TT, 1)

            def batch(b, last):
                with pool.Fori(0, H // 2) as q:
                    for n in range(2):
                        for k in range(2):
                            pool.wait_ge(sb_free, b * SB_N + q * (2 * TT) + (n * TT + k + 1 + R))
                            i = pool.tensor_tensor(phl[:, n, 1, k, :], pf[:, k, :], phl[:, n, 0, k, :], ALU.subtract)
                        i.then_inc(s_pl[0], 1)
                for tt in range(0, TT, 2):
                    inverse_root(rstd[:, tt:tt + 2], 2, b * NV + (2 + tt // 2))

                def low(c, n):
                    pool.wait_ge(s_ih, b * NC + c + 1)
                    pool.tensor_tensor(ihl[:, n, 1, :], it[:, n, :], ihl[:, n, 0, :], ALU.subtract).then_inc(s_il, 1)

                for c in range(2 * R):
                    low(c, c % R)
                    if c == CH_X - 2 and not last:
                        inverse_root(rstd[:, :], TT, (b + 1) * NV + 1)
                with pool.Fori(2, NC // R) as q:
                    for n in range(R):
                        low(R * q + n, n)

            with pool.Fori(0, B - 1) as b:
                batch(b, False)
            batch(B - 1, True)

        @block.scalar
        def _(act):
            act.sem_inc(tp_free, R)
            act.sem_inc(sb_free, R)
            act.sem_inc(pt_free, 1)
            act.sem_inc(g_free, 1)
            act.sem_inc(s_c16, R)
            act.sem_inc(s_ss, R)
            act.sem_inc(s_val, R)

            def cast_codes(q, n):
                act.wait_ge(s_code[n], q * 32 + 32)
                act.wait_ge(s_ct, q * 4 + (n + 1))
                act.activation(codesb[:, n % R, :],
                               codes[:, n, :, :].rearrange("p k c -> p (k c)").bitcast(U8)[:, 0:4 * 512:4],
                               ACT.Copy).then_inc(s_cb, 1)

            def codes_out(u, n):
                act.wait_ge(s_ct, u + (1 + R))
                act.wait_ge(s_nib, u + 1)
                act.activation(codes16[:, n % R, :], ringOb[:, n % R, 0:512], ACT.Copy).then_inc(s_c16, 1)

            def scales_out(u, n):
                act.wait_ge(s_wf, u + 1)
                act.activation(ssb[:, n % R, :, :, :].rearrange("p k l c -> p (k l c)"),
                               spread_ring(n).rearrange("p a b -> p (a b)"), ACT.Copy).then_inc(s_ss, 1)

            def values(u, n, down):
                act.wait_ge(s_nib, u + (1 + R))
                act.wait_ge(s_wf, u + 1)
                if down is None:
                    i = act.activation(val16[:, n % R, :, :], nib[:, n % R, :, :].bitcast(F16), ACT.Copy, scale=CODE)
                else:
                    for r in range(2):
                        i = act.activation(val16[:, n % R, r, :], nib[:, n % R, r, :].bitcast(F16), ACT.Copy,
                                           scale=mprod[:, bass.ds(down + r, 1)])
                i.then_inc(s_val, 1)

            for i in range(3):
                act.wait_ge(s_st, i + 1)
                act.activation(sT[:, 4 * i:4 * i + 4, :, :].rearrange("p g l c -> p (g l c)"), turn_bank(i),
                               ACT.Copy).then_inc(s_stc, 1)
            cast_codes(0, 0)
            cast_codes(0, 1)
            codes_out(0, 0)
            scales_out(0, 0)
            with act.Fori(0, UG // 4) as q:
                for n in range(4):
                    cast_codes(q + (n + 2) // 4, (n + 2) % 4)
                    codes_out(q * 4 + (n + 1), n + 1)
                    values(q * 4 + n, n, None)
                    scales_out(q * 4 + (n + 1), n + 1)
            with act.Fori(0, UD // 4 - 1) as q:
                for n in range(4):
                    cast_codes(q + (UG // 4 + (n + 2) // 4), (n + 2) % 4)
                    codes_out(q * 4 + (UG + n + 1), n + 1)
                    values(q * 4 + (UG + n), n, 8 * q + 2 * n)
                    scales_out(q * 4 + (UG + n + 1), n + 1)
            for n in range(4):
                u = UG + UD - 4 + n
                if n < 2:
                    cast_codes((UG + UD) // 4 - 1, n + 2)
                if n < 3:
                    codes_out(u + 1, n + 1)
                values(u, n, 2 * (UD - 4 + n))
                if n < 3:
                    scales_out(u + 1, n + 1)

            for n in range(R):
                act.wait_ge(s_wst[n], 16 + 16 * UG // R + 32 * UD // R)
            act.wait_ge(s_par, NPAR)
            act.activation(tgates[:, :], gates[:, :], ACT.Tanh).then_inc(s_tanh, 1)

            def prepare(b, c):
                def pt_wait(i):
                    act.wait_ge(pt_full, b * PT_N + (i + 1))

                def squares(i):
                    act.wait_ge(s_cen, b * (2 * TT) + (i + 1))
                    act.activation(sq[:, i % R, :], cen[:, 1 - i // TT, i % TT, :], ACT.Square).then_inc(s_sq, 1)

                def high(a, tt):
                    act.wait_ge(s_hn, b * (2 * TT) + ((1 - a) * TT + tt + 1))
                    v = cen[:, a, tt, :].rearrange("p (h d) -> p h d", h=H)
                    hi = cat[:, tt, :, 0:QW].rearrange("p h (w d) -> p h w d", w=3)[:, :, 0:2 + a:1 + a, :]
                    act.activation(hi, v.unsqueeze(2).broadcast_to([P, H, 2, HD]), ACT.Copy).then_inc(s_cat, 1)

                def turned(a, j, i):
                    rows = (QW, KW)[a]
                    pt_wait(i)
                    act.activation(qkT[0:rows, a, 2 * j:2 * j + 2, :].rearrange("p h t -> p (h t)"),
                                   turn16(b, i)[0:rows, :], ACT.Copy).then_inc(pt_free, 1)

                if CH_Y <= c < CH_Y + TT:
                    tt = c - CH_Y
                    pt_wait(PT_Y + tt)
                    src = turn32(b, PT_Y + tt)[:, 0:YT * P].rearrange("p (k t) -> p k t", k=YT)
                    if tt < TT - 1:
                        i = act.activation(yT[:, :, tt * P:(tt + 1) * P], src, ACT.Copy)
                    else:
                        act.activation(yT[:, :, tt * P:SM], src[:, :, 0:LASTM], ACT.Copy)
                        i = act.activation(yTd[:, :, LASTM:P], src[:, :, LASTM:P], ACT.Copy)
                    i.then_inc(pt_free, 1)
                if CH_X <= c < CH_X + TT:
                    tt = c - CH_X
                    pt_wait(PT_X + tt)
                    act.activation(xnT[:, :, tt * P:(tt + 1) * P], turn32(b, PT_X + tt).rearrange("p (k t) -> p k t", k=KT),
                                   ACT.Copy).then_inc(pt_free, 1)
                if CH_KV <= c < CH_Q and (c - CH_KV) % 2:
                    squares((c - CH_KV) // 2)
                if CH_Q + 1 <= c < CH_Q + 1 + TT:
                    high(1, c - CH_Q - 1)
                if CH_Q <= c < CH_Q + TT:
                    squares(TT + c - CH_Q)
                if CH_TK <= c < CH_TK + H // 2:
                    turned(1, c - CH_TK, PT_K + c - CH_TK)
                if c == CH_TQ - 1:
                    for tt in range(TT):
                        high(0, tt)
                if c >= CH_TQ:
                    turned(0, c - CH_TQ, PT_Q + c - CH_TQ)

            for c in range(NC):
                prepare(0, c)

            def batch(b, last):
                def tp_wait(i):
                    act.wait_ge(tp_full, b * TP_N + (i + 1))

                def maxima(h, n):
                    act.wait_ge(tp_full, b * TP_N + h + (TP_M + 1))
                    act.activation(qT[QW:KW, bass.ds(h, 1), :].rearrange("p a t -> p (a t)"),
                                   ringT16[QW:KW, n, 0:S], ACT.Copy).then_inc(tp_free, 1)

                def exps(h, n):
                    act.wait_ge(s_pv, b * H + h + 1)
                    for k in range(TT):
                        act.wait_ge(sb_full, b * SB_N + h * TT + (k + 1))
                        if k % 2 == 0:
                            act.wait_ge(s_pl[k // 2], b * H + h + 1)
                        act.activation(pf[:, k, :], ringB[:, k % R, :], ACT.Exp, scale=exp_scale[:, 0:1])
                        act.activation(phl[:, n, 0, k, :], ringB[:, k % R, :], ACT.Exp, scale=exp_scale[:, 0:1]).then_inc(sb_free, 1)

                maxima(0, 0)
                exps(0, 0)
                maxima(1, 1)
                with act.Fori(0, (H - 2) // 2) as q:
                    for n in range(2):
                        exps(2 * q + (n + 1), 1 - n)
                        maxima(2 * q + (n + 2), n)
                def turned_ctx(k):
                    tp_wait(TP_C + k)
                    act.activation(xnT[:, k, :], ringT[:, k % R, :], ACT.Copy).then_inc(tp_free, 1)

                turned_ctx(0)
                turned_ctx(1)
                exps(H - 1, 1)
                turned_ctx(2)
                turned_ctx(3)
                def high2(tt):
                    act.wait_ge(s_l2n, b * TT + (tt + 1))
                    if tt >= R:
                        act.wait_ge(tp_full, b * TP_N + (TP_L + 2 * (tt - R) + 2))
                    act.activation(xhl[:, tt % R, 0, :], xn[:, tt, :], ACT.Copy).then_inc(s_l2h, 1)

                def turned2(tt):
                    for l in range(2):
                        tp_wait(TP_L + 2 * tt + l)
                        act.activation(xT[:, l, :, tt * P:(tt + 1) * P],
                                       ringT16[:, l, 0:512].rearrange("p (k t) -> p k t", k=KT), ACT.Copy).then_inc(tp_free, 1)

                high2(0)
                high2(1)
                turned2(0)
                high2(2)
                turned2(1)
                high2(3)
                turned2(2)
                turned2(3)

                def inner(c, n):
                    act.wait_ge(g_full, b * NC + c + 1)
                    act.wait_ge(s_it, b * NC + c + 1)
                    act.activation(gl[:, n, :], ringB[:, 0, :], ACT.Gelu_apprx_tanh,
                                   scale=dg[:, bass.ds(c, 1)]).then_inc(g_free, 1)
                    act.wait_ge(s_it, b * NC + c + (1 + R))
                    act.wait_ge(s_wused, b * NC + c + 1)
                    act.activation(ihl[:, n, 0, :], it[:, n, :], ACT.Copy).then_inc(s_ih, 1)

                if last:
                    with act.Fori(0, NC // R) as q:
                        for n in range(R):
                            inner(R * q + n, n)
                else:
                    for c in range(NC):
                        inner(c, c % R)
                        prepare(b + 1, c)

            with act.Fori(0, B - 1) as b:
                batch(b, False)
            batch(B - 1, True)

        @block.tensor
        def _(pe):
            pe.sem_inc(s_ct, R)
            pe.sem_inc(s_pv, R)
            pe.sem_inc(u_full, R)
            pe.sem_inc(s_wused, R)
            pe.wait_ge(s_init, 1)

            pe.wait_ge(s_shl, 1)
            for i in range(3):
                for g in range(4):
                    for l in range(2):
                        e = pe.transpose(turn_bank(i)[:, (2 * g + l) * P:(2 * g + l + 1) * P],
                                         shl[:, l, (4 * i + g) * P:(4 * i + g + 1) * P], ident16[:, :])
                e.then_inc(s_st, 1)
            pe.wait_ge(s_stc, 3)

            def turn(u, n, block_of):
                pe.wait_ge(s_cb, u + 1)
                pe.wait_ge(s_c16, u + 1)
                for k in range(4):
                    pe.transpose(ringOb[:, n, k * P:(k + 1) * P], codesb[:, n, k * P:(k + 1) * P], identb[:, :])
                pe.wait_ge(s_ss, u + 1)
                for k in range(4):
                    e, g = block_of(k)
                    i = pe.matmul(spread_ring(n)[:, k // 2, (k % 2) * 2 * P:(k % 2 + 1) * 2 * P],
                                  spread[:, bass.ds(e, 1), :].rearrange("p a c -> p (a c)"),
                                  sT[:, g, :, :].rearrange("p a l c -> p (a l c)"), start=True, stop=True)
                i.then_inc(s_ct, 1)

            with pe.Fori(0, GR) as g:
                with pe.Fori(0, NC // GR // 2) as q:
                    for n in range(2):
                        turn((NC // GR) * g + 2 * q + n, n,
                             lambda k: (4 * q + (2 * n + k % 2), bass.ds(g + GR * (k // 2), 1)))
            with pe.Fori(0, UD // 2) as q:
                for n in range(2):
                    turn(2 * q + (UG + n), n, lambda k: (2 * q + n, slice(2 * GR + k, 2 * GR + k + 1)))
            pe.wait_ge(s_c16, UG + UD + R)
            pe.wait_ge(s_ss, UG + UD + R)
            pe.wait_ge(s_par, NPAR)

            def prepare(b, c):
                def turn_wait(i):
                    pe.wait_ge(pt_free, b * PT_N + unit_free(b, i))

                def turn_qk(a, j, i):
                    rows = (QW, KW)[a]
                    pe.wait_ge(s_hl, b * (2 * TT) + (2 - a) * TT)
                    turn_wait(i)
                    for r in range(2):
                        for tt in range(TT):
                            e = pe.transpose(turn16(b, i)[0:rows, (r * TT + tt) * P:(r * TT + tt + 1) * P],
                                             cat[:, tt, 2 * j + r, 0:rows], ident16[:, :])
                    e.then_inc(pt_full, 1)

                if CH_Y <= c < CH_Y + TT:
                    tt = c - CH_Y
                    pe.wait_ge(s_y, b * 16 + 16)
                    turn_wait(PT_Y + tt)
                    for k in range(YT):
                        i = pe.transpose(turn32(b, PT_Y + tt)[:, k * P:(k + 1) * P], y_sb[:, tt, k * P:(k + 1) * P], ident[:, :])
                    i.then_inc(pt_full, 1)
                if CH_X <= c < CH_X + TT:
                    tt = c - CH_X
                    pe.wait_ge(s_xn, b * TT + (tt + 1))
                    turn_wait(PT_X + tt)
                    for k in range(KT):
                        i = pe.transpose(turn32(b, PT_X + tt)[:, k * P:(k + 1) * P], xn[:, tt, k * P:(k + 1) * P], ident[:, :])
                    i.then_inc(pt_full, 1)
                if alone(b) and c == CH_KV:
                    pe.wait_ge(s_wc, 1)
                if CH_KV <= c < CH_Q:
                    tt, e = (c - CH_KV) // 2, (c - CH_KV) % 2
                    pe.wait_ge(pp_free, b * PP_N + unit_free(b, PP_KV + 2 * tt + e))
                    bank = projected(b, PP_KV + 2 * tt + e)
                    pe.wait_ge(pt_free, b * PT_N + (PT_Y + tt + 2))
                    last = tt == TT - 1
                    for k in range(YT):
                        i = pe.matmul(bank, yT[:, k, tt * P:(tt + 1) * P], wkv[:, k, e * D:(e + 1) * D],
                                      start=(k == 0), stop=(k == YT - 1 and not last))
                    if last:
                        for k in range(YT):
                            w = wdca[:, k, :].rearrange("p (a h d) -> p h a d", a=2, h=H)
                            i = pe.matmul(bank, yTd[:, k, :], w[:, e * (H // 2):(e + 1) * (H // 2)],
                                          start=False, stop=(k == YT - 1))
                    i.then_inc(pp_full, 1)
                if CH_Q <= c < CH_Q + TT:
                    tt = c - CH_Q
                    pe.wait_ge(pp_free, b * PP_N + unit_free(b, PP_Q + tt))
                    bank = projected(b, PP_Q + tt)
                    pe.wait_ge(pt_free, b * PT_N + (PT_X + tt + 2))
                    for k in range(KT):
                        i = pe.matmul(bank, xnT[:, k, tt * P:(tt + 1) * P], wq[:, k, :],
                                      start=(k == 0), stop=(k == KT - 1))
                    i.then_inc(pp_full, 1)
                if CH_TK <= c < CH_TK + H // 2:
                    turn_qk(1, c - CH_TK, PT_K + c - CH_TK)
                if c >= CH_TQ:
                    turn_qk(0, c - CH_TQ, PT_Q + c - CH_TQ)

            def max_scores(b, h, tiles):
                for tt in tiles:
                    pe.wait_ge(sa_free, b * SA_N + h * TT + (SA_A + tt + 1))
                    pe.matmul(ringA[:, tt % R, :], qT[0:QW, bass.ds(h, 1), tt * P:(tt + 1) * P].rearrange("p a t -> p (a t)"),
                              kT[0:QW, bass.ds(h, 1), :].rearrange("p a t -> p (a t)"),
                              start=True, stop=True).then_inc(sa_full, 1)

            for c in range(NC):
                prepare(0, c)
            pe.wait_ge(pt_free, PT_N + 1)
            max_scores(0, 0, range(TT))

            def batch(b, last):
                def scores_max(h, tiles=range(TT)):
                    max_scores(b, h, tiles)

                def tp_wait(i):
                    pe.wait_ge(tp_free, b * TP_N + (i + 1))

                def sa_wait(i):
                    pe.wait_ge(sa_free, b * SA_N + (i + 1))

                def turn_max(h, n):
                    pe.wait_ge(s_mneg, b * H + h + 1)
                    pe.wait_ge(tp_free, b * TP_N + h + (TP_M + 1))
                    for tt in range(TT):
                        i = pe.transpose(ringT16[QW:KW, n, tt * P:(tt + 1) * P], mneg[:, n, tt, :], ident16[:, :])
                    i.then_inc(tp_full, 1)

                def scores(h, tiles=range(TT)):
                    pe.wait_ge(tp_free, b * TP_N + h + (TP_M + 1 + R))
                    for k in tiles:
                        pe.wait_ge(sb_free, b * SB_N + h * TT + (k + 1))
                        pe.matmul(ringB[:, k % R, :], kT[0:KW, bass.ds(h, 1), k * P:(k + 1) * P].rearrange("p a t -> p (a t)"),
                                  qT[0:KW, bass.ds(h, 1), :].rearrange("p a t -> p (a t)"),
                                  start=True, stop=True).then_inc(sb_full, 1)

                def weigh(h, n):
                    for e in range(2):
                        pe.wait_ge(s_pl[e], b * H + h + 2)
                    pe.wait_ge(s_of, b * H + h + 1)
                    for tt in range(TT):
                        for k in range(TT):
                            for l in range(2):
                                pe.matmul(ringO[:, 0, tt * VW:(tt + 1) * VW], phl[:, n, l, k, tt * P:(tt + 1) * P],
                                          vv[:, k, bass.ds(h, 1), :].rearrange("p a w -> p (a w)"),
                                          start=(k == 0 and l == 0), stop=(k == TT - 1 and l == 1))
                        for l in range(2):
                            i = pe.matmul(ringO[:, 1, tt * VW:(tt + 1) * VW], phl[:, n, l, TT - 1, tt * P:(tt + 1) * P],
                                          vd[:, bass.ds(h, 1), :].rearrange("p a w -> p (a w)"),
                                          start=(l == 0), stop=(l == 1))
                    i.then_inc(s_pv, 1)

                pe.wait_ge(s_v, b + 1)
                scores_max(1, (0, 1))
                pe.wait_ge(s_ost, b * TT + R)
                turn_max(0, 0)
                scores_max(1, (2, 3))
                scores(0)
                turn_max(1, 1)
                scores_max(2, (0, 1))

                def step(h, n, ahead):
                    scores(h, (0, 1))
                    scores_max(h + 1, (2, 3))
                    scores(h, (2, 3))
                    turn_max(h + 1, n)
                    if ahead:
                        scores_max(h + 2, (0, 1))
                    weigh(h - 1, n)

                with pe.Fori(0, (H - 4) // 2) as q:
                    for n in range(2):
                        step(2 * q + (n + 1), n, True)
                step(H - 3, 0, True)
                step(H - 2, 1, False)

                def turn_ctx(k):
                    pe.wait_ge(s_ctx, b * H + (k + 1) * (H // KT))
                    tp_wait(TP_C + k)
                    for tt in range(TT):
                        i = pe.transpose(ringT[:, k % R, tt * P:(tt + 1) * P], xn[:, tt, k * P:(k + 1) * P], ident[:, :])
                    i.then_inc(tp_full, 1)

                def project(tiles, heads):
                    for tt in tiles:
                        if heads[0] == 0:
                            if tt < R:
                                sa_wait(SA_O + tt)
                            else:
                                pe.wait_ge(sb_free, b * SB_N + (SB_O + tt - R + 1))
                        for k in heads:
                            tp_wait(TP_C + k + R)
                            i = pe.matmul((ringA, ringB)[tt // R][:, tt % R, :], xnT[:, k, tt * P:(tt + 1) * P], wo[:, k, :],
                                          start=(k == 0), stop=(k == KT - 1))
                        if heads[-1] == KT - 1:
                            i.then_inc((sa_full, sb_full)[tt // R], 1)

                turn_ctx(0)
                turn_ctx(1)
                scores(H - 1)
                weigh(H - 2, 0)
                turn_ctx(2)
                project((0, 1), (0, 1))
                weigh(H - 1, 1)
                project((0, 1), (2,))
                project((2,), (0, 1))
                turn_ctx(3)
                project((3,), (0, 1))
                project((0, 1), (3,))
                project((2, 3), (2, 3))
                for tt in range(TT):
                    pe.wait_ge(s_l2, b * TT + (tt + 1))
                    for l in range(2):
                        tp_wait(TP_L + 2 * tt + l)
                        v = xhl[:, tt % R, l, :].rearrange("p (j c r) -> p j r c", j=2, r=2)
                        for k in range(KT):
                            i = pe.transpose(ringT16[:, l, k * P:(k + 1) * P], v[:, k // 2, k % 2, :], ident16[:, :])
                        i.then_inc(tp_full, 1)

                def gate_up(q, c, n):
                    w = wgu[:, n, :].rearrange("p (l m k c) -> p l m k c", l=2, m=2, k=KT)
                    pe.wait_ge(s_loadg[n], b * (16 * NC // R) + q * 16 + 16)
                    for m in range(2):
                        if m == 0:
                            pe.wait_ge(g_free, b * NC + c + 1)
                        else:
                            pe.wait_ge(s_it, b * NC + c + R)
                        for k in range(KT):
                            for e, (wl, xl) in enumerate(((0, 0), (0, 1), (1, 0))):
                                i = pe.matmul(ringB[:, m, :], w[:, wl, m, k, :], xT[:, xl, k, :],
                                              start=(k == 0 and e == 0), stop=(k == KT - 1 and e == 2))
                        i.then_inc(u_full if m else g_full, 1)

                def down(q, c, n, first, stop):
                    w = wdn[:, n, :].rearrange("p (l d) -> p l d", l=2)
                    pe.wait_ge(s_loadd[n], b * (16 * NC // R) + q * 16 + 16)
                    pe.wait_ge(s_il, b * NC + c + (1 + R))
                    for tt in range(TT):
                        for e, (il, wl) in enumerate(((0, 0), (0, 1), (1, 0))):
                            i = pe.matmul(acc(tt), ihl[:, n, il, tt * P:(tt + 1) * P], w[:, wl, :],
                                          start=(first and e == 0), stop=(stop and e == 2))
                    i.then_inc(s_wused, 1)

                pe.wait_ge(tp_free, b * TP_N + (TP_N + R))
                pe.wait_ge(s_of, b * H + (H + 1))
                gate_up(0, 0, 0)
                if last:
                    gate_up(0, 1, 1)
                    down(0, 0, 0, True, False)
                    with pe.Fori(1, NC // R) as q:
                        gate_up(q, R * q, 0)
                        down(q - 1, R * q - 1, 1, False, False)
                        gate_up(q, R * q + 1, 1)
                        down(q, R * q, 0, False, False)
                else:
                    prepare(b + 1, 0)
                    for c in range(1, NC):
                        gate_up(c // R, c, c % R)
                        prepare(b + 1, c)
                        if c == NC - 1:
                            pe.wait_ge(pt_free, (b + 1) * PT_N + (PT_N + 1))
                            max_scores(b + 1, 0, (0, 1))
                        down((c - 1) // R, c - 1, (c - 1) % R, c == 1, False)
                    max_scores(b + 1, 0, (2, 3))
                down((NC - 1) // R, NC - 1, (NC - 1) % R, False, True)
                pe.wait_ge(s_wused, b * NC + (NC + R))
                pe.sem_inc(s_dn, 1)

            with pe.Fori(0, B - 1) as b:
                batch(b, False)
            batch(B - 1, True)

        @block.vector
        def _(dve):
            dve.sem_inc(sa_free, R)
            dve.sem_inc(s_wf, R)
            dve.sem_inc(s_nib, R)
            dve.sem_inc(s_of, 1)
            dve.sem_inc(s_ost, R)
            dve.sem_inc(pp_free, 1)
            dve.sem_inc(s_it, R)
            dve.sem_inc(s_pl[1], 1)

            dve.wait_ge(s_scales, 48)
            dve.wait_ge(s_init, 1)
            dve.tensor_reduce(pgu[:, :, :], sgu[:, :, :, :], AX.X, ALU.max, apply_absolute_value=True)
            dve.tensor_reduce(stat[:, 1:2], sd[:, :, :].rearrange("p t k -> p (t k)"), AX.X, ALU.max,
                              apply_absolute_value=True)
            dve.drain()
            dve.tensor_scalar(pgu[:, :, :], pgu[:, :, :], TINY, None, ALU.max)
            dve.drain()
            dve.tensor_scalar(pgu[:, :, :].bitcast(U32), pgu[:, :, :].bitcast(U32), POW2, None, ALU.bitwise_and)
            dve.drain()
            dve.reciprocal(igu[:, :, :], pgu[:, :, :])
            dve.tensor_tensor(mprod[:, :], pgu[:, 0, :], pgu[:, 1, :], ALU.mult)
            dve.tensor_scalar(dg[:, :], pgu[:, 0, :], 1.0 / (W_UP * X_UP), None, ALU.mult)
            dve.drain()
            dve.tensor_scalar(mu[:, :], igu[:, 0, :], I_UP / (W_UP * X_UP), None, ALU.mult)
            dve.tensor_reduce(stat[:, 0:1], mprod[:, :], AX.X, ALU.max)
            dve.drain()
            dve.tensor_scalar(igu[:, :, :], igu[:, :, :], W_UP, None, ALU.mult)
            dve.drain()
            dve.tensor_tensor(sgu[:, :, :, :].rearrange("p m c k -> p (m c) k"), sgu[:, :, :, :].rearrange("p m c k -> p (m c) k"),
                              igu[:, :, :].rearrange("p m c -> p (m c)").unsqueeze(2).broadcast_to([P, 2 * NC, 16]),
                              ALU.mult).then_inc(s_stat, 1)
            dve.wait_ge(s_allmax, 1)
            dve.tensor_scalar(stat[:, 2:4], stat[:, 2:4], TINY, None, ALU.max)
            dve.drain()
            dve.tensor_scalar(stat[:, 2:4].bitcast(U32), stat[:, 2:4].bitcast(U32), POW2, None, ALU.bitwise_and)
            dve.drain()
            dve.reciprocal(stat[:, 4:6], stat[:, 2:4])
            dve.tensor_tensor(out_scale[:, :], stat[:, 2:3], stat[:, 3:4], ALU.mult)
            dve.drain()
            dve.tensor_scalar(mprod[:, :], mprod[:, :], stat[:, 4:5], CODE, ALU.mult, ALU.mult)
            dve.tensor_scalar(sd[:, :, :], sd[:, :, :], stat[:, 5:6], W_UP, ALU.mult, ALU.mult)
            dve.drain()
            big = gl[:, :, :].rearrange("p a b -> p (a b)")[:, 0:SG * P // 2]
            dif = sq[:, :, :].rearrange("p a b -> p (a b)")[:, 0:SG * P // 2]
            for h in range(2):
                half = slice(h * SG * P // 2, (h + 1) * SG * P // 2)
                dve.tensor_scalar(big, scales[:, half], 2.0 ** 15 + 1.0, None, ALU.mult)
                dve.drain()
                dve.tensor_tensor(dif, big, scales[:, half], ALU.subtract)
                dve.drain()
                dve.tensor_tensor(shl[:, 0, half], big, dif, ALU.subtract)
                dve.drain()
                dve.tensor_tensor(shl[:, 1, half], scales[:, half], shl[:, 0, half], ALU.subtract)
            dve.drain()
            dve.sem_inc(s_shl, 1)

            def nibbles(u, n):
                dve.wait_ge(s_c16, u + (1 + R))
                dve.wait_ge(s_val, u + 1)
                for r in range(2):
                    c = codes16[:, n % R, :]
                    dve.tensor_scalar(nib[:, n % R, r, :], c, 9 - 4 * r, 0x0E00, ALU.logical_shift_left, ALU.bitwise_and)
                    dve.tensor_scalar(nibs[:, n % R, r, :], c, 12 - 4 * r, 0x8000, ALU.logical_shift_left, ALU.bitwise_and)
                dve.drain()
                dve.tensor_tensor(nib[:, n % R, :, :], nib[:, n % R, :, :], nibs[:, n % R, :, :], ALU.bitwise_or).then_inc(s_nib, 1)

            def weights(u, n, stores, down):
                dve.wait_ge(s_val, u + (1 + R))
                dve.wait_ge(s_ss, u + (1 + R))
                dve.wait_ge(s_wst[n % R], stores)
                v = val16[:, n % R, :, :].rearrange("p r (k c) -> p k r c", k=4)
                for l in range(2):
                    if not down:
                        w = whl[:, n % R, l * 1024:(l + 1) * 1024].rearrange("p (k r c) -> p k r c", k=4, r=2)
                    else:
                        w = whl[:, n % R, :].rearrange("p (r l k c) -> p l k r c", r=2, l=2, k=4)[:, l]
                    i = dve.tensor_tensor(w, v, ssb[:, n % R, :, l, :].unsqueeze(2).broadcast_to([P, 4, 2, P]), ALU.mult)
                i.then_inc(s_wf, 1)

            done = 16 + 16 * UG // R
            nibbles(0, 0)
            with dve.Fori(0, UG // 4) as q:
                for n in range(4):
                    nibbles(4 * q + (n + 1), n + 1)
                    weights(4 * q + n, n, q * 32 + (16 + 16 * (n // R)), False)
            with dve.Fori(0, UD // 4 - 1) as q:
                for n in range(4):
                    nibbles(4 * q + (UG + n + 1), n + 1)
                    weights(4 * q + (UG + n), n, q * 64 + (done + 32 * (n // R)), True)
            for n in range(4):
                u = UG + UD - 4 + n
                if n < 3:
                    nibbles(u + 1, n + 1)
                weights(u, n, (UD // 4 - 1) * 64 + done + 32 * (n // R), True)

            dve.wait_ge(s_par, NPAR)

            def center(v, n):
                dve.tensor_reduce(hsum[:, 0:n], v, AX.X, ALU.add)
                dve.drain()
                dve.scalar_tensor_tensor(v, hsum[:, 0:n].unsqueeze(2).broadcast_to([P, n, HD]), -1.0 / HD, v,
                                         ALU.mult, ALU.add)
                dve.drain()

            center(wq[:, :, :].rearrange("p k (h d) -> p (k h) d", h=H), KT * H)
            center(bq_b[:, :].rearrange("p (h d) -> p h d", h=H), H)
            for k in range(YT):
                center(wkv[:, k, :].rearrange("p (h w) -> p h w", h=H)[:, :, 0:HD], H)
                center(wdca[:, k, 0:D].rearrange("p (h d) -> p h d", h=H), H)
            for kind in range(2):
                center(bkv_b[:, kind, :].rearrange("p (h w) -> p h w", h=H)[:, :, 0:HD], H)
            dve.sem_inc(s_wc, 1)

            dve.tensor_reduce(qk_p2[:, 0:1], qwb[:, :, :].rearrange("p a d -> p (a d)"), AX.X, ALU.max,
                              apply_absolute_value=True)
            dve.tensor_reduce(qk_p2[:, 1:2], kall[:, :, :].rearrange("p a d -> p (a d)"), AX.X, ALU.max,
                              apply_absolute_value=True)
            dve.drain()
            dve.tensor_scalar(qk_p2[:, 0:2], qk_p2[:, 0:2], TINY, None, ALU.max)
            dve.drain()
            dve.tensor_scalar(qk_p2[:, 0:2].bitcast(U32), qk_p2[:, 0:2].bitcast(U32), POW2, None, ALU.bitwise_and)
            dve.drain()
            dve.reciprocal(qk_p2[:, 2:4], qk_p2[:, 0:2])
            dve.scalar_tensor_tensor(exp_scale[:, :], qk_p2[:, 0:1], SCALE, qk_p2[:, 1:2], ALU.mult, ALU.mult)
            dve.drain()
            dve.tensor_scalar(qwb[:, :, :], qwb[:, :, :], qk_p2[:, 2:3], None, ALU.mult)
            dve.tensor_scalar(kwb[:, :, :, :].rearrange("p a b d -> p (a b d)"),
                              kwb[:, :, :, :].rearrange("p a b d -> p (a b d)"), qk_p2[:, 3:4], None, ALU.mult)
            dve.drain()
            dve.tensor_scalar(qwb[:, 0, :], qwb[:, 0, :], HD ** 0.5, None, ALU.mult)
            for kind in range(2):
                dve.tensor_scalar(kwb[:, kind, 0, :], kwb[:, kind, 0, :], HD ** 0.5, None, ALU.mult)
            for tt in range(TT):
                kind = tt // (TT - 1)
                dve.tensor_copy(cat[:, tt, :, QW:KW], kmask[:, kind, :].unsqueeze(1).broadcast_to([P, H, 2]))
                dve.tensor_copy(vv[:, tt, :, VW - 1:VW], kmask[:, kind, 0:1].unsqueeze(1).broadcast_to([P, H, 1]))
            dve.tensor_copy(vd[:, :, VW - 1:VW], kmask[:, 1, 1:2].unsqueeze(1).broadcast_to([P, H, 1]))
            dve.wait_ge(s_tanh, 1)
            dve.tensor_scalar(bo_b[:, :], bo_b[:, :], tgates[:, 0:1], None, ALU.mult)
            dve.tensor_scalar(out_scale[:, :], out_scale[:, :], tgates[:, 1:2], None, ALU.mult)
            dve.drain()


            def prepare(b, c):
                def head_roots(v):
                    dve.drain()
                    dve.tensor_scalar(nv[:, 0, :], v, HD * EPS_H, None, ALU.add)
                    dve.drain()
                    dve.tensor_scalar(nv[:, 1, :].bitcast(I32), nv[:, 0, :].bitcast(I32), 1, None, ALU.logical_shift_right)
                    dve.tensor_scalar(nv[:, 0, :], nv[:, 0, :], -0.5, None, ALU.mult)
                    dve.drain()
                    dve.tensor_scalar(v.bitcast(I32), nv[:, 1, :].bitcast(I32), -1.0, ROOT, ALU.mult, ALU.add)
                    dve.drain()
                    for _ in range(3):
                        dve.tensor_tensor(nv[:, 1, :], v, v, ALU.mult)
                        dve.drain()
                        dve.tensor_tensor(nv[:, 1, :], nv[:, 1, :], nv[:, 0, :], ALU.mult)
                        dve.drain()
                        dve.scalar_tensor_tensor(v, nv[:, 1, :], 1.5, v, ALU.add, ALU.mult)
                        dve.drain()

                def head_sums(i):
                    a, tt = 1 - i // TT, i % TT
                    dve.wait_ge(s_sq, b * (2 * TT) + (i + 1))
                    dve.tensor_reduce(hrs[:, a, tt, :], sq[:, i % R, :].rearrange("p (h d) -> p h d", h=H), AX.X, ALU.add)

                def split_values(dst, src):
                    dve.tensor_copy(dst[:, :, 0:HD], src)
                    dve.drain()
                    dve.tensor_tensor(src, src, dst[:, :, 0:HD], ALU.subtract)
                    dve.drain()
                    dve.tensor_copy(dst[:, :, HD:2 * HD], src)
                    dve.drain()
                    return dve.tensor_tensor(dst[:, :, 2 * HD:3 * HD], src, dst[:, :, HD:2 * HD], ALU.subtract)

                def keys_values(tt, e):
                    kind = tt // (TT - 1)
                    dve.wait_ge(pp_full, b * PP_N + (PP_KV + 2 * tt + e + 1))
                    src = projected(b, PP_KV + 2 * tt + e).rearrange("p (h w) -> p h w", h=H // 2)
                    bias = bkv_b[:, kind, e * D:(e + 1) * D].rearrange("p (h w) -> p h w", h=H // 2)
                    half = slice(e * D // 2, (e + 1) * D // 2)
                    dve.tensor_tensor(val[:, half].rearrange("p (h d) -> p h d", d=HD), src[:, :, HD:2 * HD],
                                      bias[:, :, HD:2 * HD], ALU.add)
                    dve.tensor_tensor(cen[:, 1, tt, half].rearrange("p (h d) -> p h d", d=HD), src[:, :, 0:HD],
                                      bias[:, :, 0:HD], ALU.add).then_inc(pp_free, 1)
                    dve.drain()
                    if e == 0:
                        return
                    dve.sem_inc(s_cen, 1)
                    v = val[:, :].rearrange("p (h d) -> p h d", h=H)
                    if kind:
                        v2 = vald[:, :].rearrange("p (h d) -> p h d", h=H)
                        dve.tensor_scalar(v2, v, kmask[:, 1, 1:2], None, ALU.mult)
                        dve.drain()
                        dve.tensor_scalar(v, v, kmask[:, 1, 0:1], None, ALU.mult)
                        dve.drain()
                        split_values(vd, v2)
                    i = split_values(vv[:, tt, :, :], v)
                    if kind:
                        i.then_inc(s_v, 1)
                    dve.drain()

                def low(a, tt):
                    v = cen[:, a, tt, :].rearrange("p (h d) -> p h d", h=H)
                    lo = 2 - a
                    dve.wait_ge(s_cat, b * (2 * TT) + ((1 - a) * TT + tt + 1))
                    dve.tensor_tensor(cat[:, tt, :, lo * HD:(lo + 1) * HD], v, cat[:, tt, :, 0:HD],
                                      ALU.subtract).then_inc(s_hl, 1)

                def norm(a, tt):
                    w = qwb if a == 0 else kwb[:, tt // (TT - 1), :, :]
                    v = cen[:, a, tt, :].rearrange("p (h d) -> p h d", h=H)
                    dve.tensor_tensor(v, v, hrs[:, a, tt, :].unsqueeze(2).broadcast_to([P, H, HD]), ALU.mult)
                    dve.drain()
                    dve.tensor_tensor(v, v, w[:, 0, :].unsqueeze(1).broadcast_to([P, H, HD]), ALU.mult)
                    dve.drain()
                    dve.tensor_tensor(v, v, w[:, 1, :].unsqueeze(1).broadcast_to([P, H, HD]), ALU.add).then_inc(s_hn, 1)

                if c == CH_X - 2:
                    dve.wait_ge(s_xl, b * 16 + 16)
                    for tt in range(TT):
                        dve.bn_stats(bst[:, tt, :], xn[:, tt, :])
                    dve.drain()
                    for tt in range(TT):
                        dve.bn_aggr(mv[:, tt, :], bst[:, tt, :])
                    dve.drain()
                    dve.tensor_scalar(rstd[:, :], mv[:, :, 1], EPS_X, None, ALU.add).then_inc(s_var, 1)
                if c == CH_X - 1:
                    dve.wait_ge(s_rstd, b * NV + 1)
                    for tt in range(TT):
                        dve.tensor_scalar(xn[:, tt, :], xn[:, tt, :], mv[:, tt, 0:1], rstd[:, tt:tt + 1],
                                          ALU.subtract, ALU.mult).then_inc(s_xn, 1)
                if CH_KV <= c < CH_Q:
                    keys_values((c - CH_KV) // 2, (c - CH_KV) % 2)
                if CH_KV + 2 <= c <= CH_Q and (c - CH_KV) % 2 == 0:
                    head_sums((c - CH_KV) // 2 - 1)
                if c == CH_Q:
                    head_roots(hrs[:, 1, :, :].rearrange("p t h -> p (t h)"))
                if CH_Q + 1 <= c < CH_Q + 1 + TT:
                    norm(1, c - CH_Q - 1)
                    if c > CH_Q + 1:
                        low(1, c - CH_Q - 2)
                if CH_Q <= c < CH_Q + TT:
                    tt = c - CH_Q
                    dve.wait_ge(pp_full, b * PP_N + (PP_Q + tt + 1))
                    dve.tensor_tensor(cen[:, 0, tt, :], projected(b, PP_Q + tt), bq_b[:, :], ALU.add).then_inc(pp_free, 1)
                    dve.drain()
                    dve.sem_inc(s_cen, 1)
                if CH_Q + 1 <= c < CH_Q + 1 + TT:
                    head_sums(TT + c - CH_Q - 1)
                if c == CH_Q + TT:
                    low(1, TT - 1)
                    head_roots(hrs[:, 0, :, :].rearrange("p t h -> p (t h)"))
                if CH_Q + TT + 1 <= c < CH_Q + 2 * TT + 1:
                    norm(0, c - CH_Q - TT - 1)
                if c == CH_TQ - 1:
                    for tt in range(TT):
                        low(0, tt)

            def tile_maxima(b, h):
                for tt in range(TT):
                    dve.wait_ge(sa_full, b * SA_N + h * TT + (SA_A + tt + 1))
                    dve.tensor_reduce(pmx[:, tt, :], ringA[:, tt % R, :].rearrange("p (g k) -> p g k", k=DCA),
                                      AX.X, ALU.max).then_inc(sa_free, 1)

            def negated_maxima(b, h, n, first):
                if not first:
                    dve.wait_ge(tp_full, b * TP_N + h + (TP_M - 1))
                dve.tensor_reduce(mneg[:, n, :, 0], pmx[:, :, 0:SM // DCA], AX.X, ALU.max, negate=True)
                dve.tensor_scalar(mneg[:, n, :, 1], pmx[:, :, SM // DCA], -1.0, None, ALU.mult).then_inc(s_mneg, 1)

            def first_maxima(b):
                dve.drain()
                tile_maxima(b, 0)
                dve.drain()
                negated_maxima(b, 0, 0, True)
                dve.drain()

            for c in range(NC):
                prepare(0, c)
            first_maxima(0)

            def batch(b, last):
                def lows(h, n):
                    dve.wait_ge(sb_free, b * SB_N + h * TT + (TT + R))
                    dve.tensor_tensor(phl[:, n, 1, 2:TT, :], pf[:, 2:TT, :], phl[:, n, 0, 2:TT, :],
                                      ALU.subtract).then_inc(s_pl[1], 1)

                def sum_parts(h):
                    dve.wait_ge(s_pv, b * H + h + (1 + R))
                    o = ringO[:, :, 0:TT * VW].rearrange("p a (t w) -> p a t w", t=TT)
                    for a in range(2):
                        dve.tensor_reduce(osum[:, a, :, :], o[:, a, :, 0:3 * HD].rearrange("p t (w d) -> p t d w", w=3),
                                          AX.X, ALU.add)
                    dve.reciprocal(orec[:, :, :], o[:, :, :, VW - 1]).then_inc(s_of, 1)

                def divide():
                    dve.tensor_tensor(odiv[:, :, :, :].rearrange("p a t d -> p (a t) d"),
                                      osum[:, :, :, :].rearrange("p a t d -> p (a t) d"),
                                      orec[:, :, :].rearrange("p a t -> p (a t)").unsqueeze(2).broadcast_to([P, 2 * TT, HD]),
                                      ALU.mult)

                def both(h):
                    dve.tensor_tensor(xn[:, :, bass.ds(h * HD, HD)], odiv[:, 0, :, :], odiv[:, 1, :, :],
                                      ALU.add).then_inc(s_ctx, 1)

                def step(h, n):
                    tile_maxima(b, h + 1)
                    dve.drain()
                    negated_maxima(b, h + 1, n, False)
                    sum_parts(h - 2)
                    dve.drain()
                    divide()
                    dve.drain()
                    both(h - 2)
                    lows(h, 1 - n)

                def head_out(h):
                    dve.drain()
                    sum_parts(h)
                    dve.drain()
                    divide()
                    dve.drain()
                    both(h)

                for h in range(1, 3):
                    tile_maxima(b, h)
                    dve.drain()
                    negated_maxima(b, h, h % 2, h == 1)
                    lows(h - 1, (h - 1) % 2)
                    dve.drain()
                step(2, 1)
                with dve.Fori(0, (H - 4) // 2) as q:
                    for n in range(2):
                        step(2 * q + (n + 3), n)
                head_out(H - 3)
                lows(H - 1, 1)
                head_out(H - 2)
                head_out(H - 1)

                dve.wait_ge(s_x, b * 16 + 16)
                for tt in range(TT):
                    dve.tensor_tensor(x_sb[:, tt, :], x_sb[:, tt, :], bo_b[:, :], ALU.add)

                def statistics(pair):
                    dve.drain()
                    for tt in pair:
                        if tt < R:
                            dve.wait_ge(sa_full, b * SA_N + (SA_O + tt + 1))
                        else:
                            dve.wait_ge(sb_full, b * SB_N + (SB_O + tt - R + 1))
                        dve.scalar_tensor_tensor(x_sb[:, tt, :], (ringA, ringB)[tt // R][:, tt % R, :], tgates[:, 0:1],
                                                 x_sb[:, tt, :], ALU.mult, ALU.add).then_inc((sa_free, sb_free)[tt // R], 1)
                    dve.drain()
                    for tt in pair:
                        dve.bn_stats(bst[:, tt, :], x_sb[:, tt, :])
                    dve.drain()
                    for tt in pair:
                        dve.bn_aggr(mv[:, tt, :], bst[:, tt, :])
                    dve.drain()
                    dve.tensor_scalar(rstd[:, pair[0]:pair[0] + 2], mv[:, pair[0]:pair[0] + 2, 1], X_UP ** -2,
                                      EPS_X * X_UP ** -2, ALU.mult, ALU.add).then_inc(s_var, 1)

                def normalize(pair):
                    dve.wait_ge(s_rstd, b * NV + (2 + pair[0] // 2))
                    for tt in pair:
                        dve.tensor_scalar(xn[:, tt, :], x_sb[:, tt, :], mv[:, tt, 0:1], rstd[:, tt:tt + 1],
                                          ALU.subtract, ALU.mult).then_inc(s_l2n, 1)

                def low2(pair):
                    for tt in pair:
                        dve.wait_ge(s_l2h, b * TT + (tt + 1))
                        dve.tensor_tensor(xhl[:, tt % R, 1, :], xn[:, tt, :], xhl[:, tt % R, 0, :],
                                          ALU.subtract).then_inc(s_l2, 1)

                statistics((0, 1))
                normalize((0, 1))
                statistics((2, 3))
                low2((0, 1))
                normalize((2, 3))
                low2((2, 3))
                def inner(c, n):
                    dve.wait_ge(u_full, b * NC + c + (1 + R))
                    dve.wait_ge(g_free, b * NC + c + 2)
                    dve.wait_ge(s_il, b * NC + c + 1)
                    dve.scalar_tensor_tensor(it[:, n, :], ringB[:, 1, :], mu[:, bass.ds(c, 1)], gl[:, n, :],
                                             ALU.mult, ALU.mult).then_inc(s_it, 1)

                if last:
                    with dve.Fori(0, NC // R) as q:
                        for n in range(R):
                            inner(R * q + n, n)
                else:
                    for c in range(NC):
                        inner(c, c % R)
                        prepare(b + 1, c)
                    first_maxima(b + 1)
                dve.wait_ge(s_dn, b + 1)
                for tt in OST:
                    dve.scalar_tensor_tensor(x_sb[:, tt, :], acc(tt), out_scale[:, 0:1], x_sb[:, tt, :],
                                             ALU.mult, ALU.add).then_inc(s_ost, 1)

            with dve.Fori(0, B - 1) as b:
                batch(b, False)
            batch(B - 1, True)


_INS = ['x', 'ctx_1024', 'g_xattn', 'g_ffn'] + ['L0_xattn_' + n for n in (
    'Wq', 'bq', 'Wk', 'bk', 'Wv', 'bv', 'Wkv_dca', 'bkv_dca', 'qn_w', 'qn_b', 'kn_w', 'kn_b', 'kn_dca_w', 'kn_dca_b',
    'Wo', 'bo')] + ['L0_ffn_' + n for n in (
        'gate_W_packed', 'gate_scales', 'up_W_packed', 'up_scales', 'down_W_packed', 'down_scales')]
_OUTS = [((B, S, D), 'float32')]


def kernel(**inputs):
    import numpy as _np
    import concourse.bacc as _bacc
    from concourse import mybir as _mybir
    from concourse.bass_utils import run_bass_kernel_spmd as _run

    nc = _bacc.Bacc("TRN2", target_bir_lowering=False, num_devices=1)
    arrays, args = {}, []
    for name in _INS:
        a = _np.ascontiguousarray(inputs[name])
        arrays[f"in_{name}_dram"] = a
        args.append(nc.dram_tensor(f"in_{name}_dram", a.shape, _mybir.dt.from_np(a.dtype), kind="ExternalInput").ap())
    for i, (shape, dtype) in enumerate(_OUTS):
        dt = _mybir.dt.from_np(_np.dtype(dtype))
        args.append(nc.dram_tensor(f"out_{i}_dram", shape, dt, kind="ExternalOutput").ap())
    block_kernel(nc, *args)
    r = _run(nc, [arrays], core_ids=[0])
    return r.results[0]["out_0_dram"]
```
